# Optimizing a Trainium2 kernel written in Bass

```python
import numpy as np
import jax
import jax.numpy as jnp

def _softmax(x, axis=-1):
    return jax.nn.softmax(x, axis=axis)

def _gelu(x):
    return jax.nn.gelu(x, approximate=True)

def _silu(x):
    return jax.nn.silu(x)

def _sigmoid(x):
    return jax.nn.sigmoid(x)

def _layernorm(x, axis=-1, eps=1e-05):
    m = jnp.mean(x, axis=axis, keepdims=True)
    v = jnp.var(x, axis=axis, keepdims=True)
    return (x - m) / jnp.sqrt(v + eps)

def _scatter_add(tgt, idx, src, axis=0):
    return tgt.at[idx].add(src)

def _segment_sum(src, seg, n):
    return jax.ops.segment_sum(src, seg, n)
kernel_name = 'mk_vit_tower_d1_tok_img256_r4_f797e7'

def setup_inputs(seed: int=0):
    np.random.seed(seed)
    _w = jnp.asarray

    def _rec_inputs():
        import jax
        import jax.numpy as jnp
        _rk = jax.random.key(seed)
        x = -0.000395706 + 0.999959 * jax.random.normal(jax.random.fold_in(_rk, 1), (64, 1, 96, 96), jnp.float32)
        return x
    x = _rec_inputs()

    def _L0_tok_setup():
        import jax, jax.numpy as jnp
        import numpy as np
        from jax import lax
        EMBED_DIM = 64
        key = jax.random.key(seed)
        ks = jax.random.split(key, 11)
        B, H, W = (64, 224, 224)
        D = EMBED_DIM
        x = jax.random.normal(ks[0], (B, 1, H, W), dtype=jnp.float32)
        conv_w = jax.random.normal(ks[1], (4, 1, 2, 2), dtype=jnp.float32) * 0.5
        conv_b = jax.random.normal(ks[2], (4,), dtype=jnp.float32) * 0.1
        s = 1.0 / np.sqrt(D)
        wq = jax.random.normal(ks[3], (D, D), dtype=jnp.float32) * s
        bq = jax.random.normal(ks[4], (D,), dtype=jnp.float32) * 0.02
        wk = jax.random.normal(ks[5], (D, D), dtype=jnp.float32) * s
        bk = jax.random.normal(ks[6], (D,), dtype=jnp.float32) * 0.02
        wv = jax.random.normal(ks[7], (D, D), dtype=jnp.float32) * s
        bv = jax.random.normal(ks[8], (D,), dtype=jnp.float32) * 0.02
        wo = jax.random.normal(ks[9], (D, D), dtype=jnp.float32) * s
        bo = jax.random.normal(ks[10], (D,), dtype=jnp.float32) * 0.02
        return {'x': x, 'conv_w': conv_w, 'conv_b': conv_b, 'wq': wq, 'bq': bq, 'wk': wk, 'bk': bk, 'wv': wv, 'bv': bv, 'wo': wo, 'bo': bo}
    _L0_tok_all = _L0_tok_setup()
    _L0_tok_in = {k: v for k, v in _L0_tok_all.items() if k in ('conv_w', 'conv_b', 'wq', 'bq', 'wk', 'bk', 'wv', 'bv', 'wo', 'bo')}
    del _L0_tok_all

    def _L0_attn_setup():
        import jax, jax.numpy as jnp
        import numpy as np
        import math
        STATE_DIM = 64
        R_MIN, R_MAX = (0.4, 0.9)
        PHASE_MAX = 2.0 * math.pi
        BATCH, SEQ = (8, 1024)

        def _binop(e_i, e_j):
            a_i, b_i = e_i
            a_j, b_j = e_j
            return (a_j * a_i, a_j * b_i + b_j)
        key = jax.random.key(seed)
        k_x, k_u1, k_u2, k_br, k_bi, k_cr, k_ci = jax.random.split(key, 7)
        D = STATE_DIM
        x = jax.random.normal(k_x, (BATCH, SEQ, D), dtype=jnp.float32)
        u1 = jax.random.uniform(k_u1, (D,), dtype=jnp.float32)
        nu_log = jnp.log(-0.5 * jnp.log(u1 * (R_MAX + R_MIN) * (R_MAX - R_MIN) + R_MIN ** 2))
        u2 = jax.random.uniform(k_u2, (D,), dtype=jnp.float32)
        theta_log = jnp.log(PHASE_MAX * u2)
        lam_mod = jnp.exp(-jnp.exp(nu_log))
        gamma_log = jnp.log(jnp.sqrt(1.0 - jnp.square(lam_mod)))
        s_b = 1.0 / math.sqrt(2 * D)
        s_c = 1.0 / math.sqrt(D)
        B_re = jax.random.normal(k_br, (D, D), dtype=jnp.float32) * s_b
        B_im = jax.random.normal(k_bi, (D, D), dtype=jnp.float32) * s_b
        C_re = jax.random.normal(k_cr, (D, D), dtype=jnp.float32) * s_c
        C_im = jax.random.normal(k_ci, (D, D), dtype=jnp.float32) * s_c
        return {'x': x, 'nu_log': nu_log, 'theta_log': theta_log, 'gamma_log': gamma_log, 'B_re': B_re, 'B_im': B_im, 'C_re': C_re, 'C_im': C_im}
    _L0_attn_all = _L0_attn_setup()
    _L0_attn_in = {k: v for k, v in _L0_attn_all.items() if k in ('nu_log', 'theta_log', 'gamma_log', 'B_re', 'B_im', 'C_re', 'C_im')}
    del _L0_attn_all

    def _L0_ffn_setup():
        import jax, jax.numpy as jnp
        import numpy as np
        B, T, C = (64, 96, 64)
        NH, NKV = (4, 2)
        HD = C // NH
        NREP = NH // NKV
        NE, TOPK = (8, 2)
        HID = int(8 / 3 * C)
        EPS_RMS = 1e-06

        def _rope_tables(t_len):
            inv_freq = 1.0 / 10000.0 ** (np.arange(0, HD, 2, dtype=np.float32) / HD)
            t = np.arange(t_len, dtype=np.float32)
            freqs = np.outer(t, inv_freq)
            emb = np.concatenate([freqs, freqs], axis=-1)
            return (jnp.asarray(np.cos(emb)), jnp.asarray(np.sin(emb)))

        def _rotate_half(x):
            h = x.shape[-1] // 2
            return jnp.concatenate([-x[..., h:], x[..., :h]], axis=-1)

        def _rmsnorm(v, w):
            return v * jax.lax.rsqrt(jnp.mean(v * v, axis=-1, keepdims=True) + EPS_RMS) * w
        key = jax.random.key(seed)
        ks = jax.random.split(key, 10)
        s = lambda k, shape: jax.random.normal(k, shape, jnp.float32) * 0.02
        return {'x': jax.random.normal(ks[0], (B, T, C), jnp.float32), 'ln1_w': jnp.ones((C,), jnp.float32), 'ln2_w': jnp.ones((C,), jnp.float32), 'wq': s(ks[1], (NH * HD, C)), 'wk': s(ks[2], (NKV * HD, C)), 'wv': s(ks[3], (NKV * HD, C)), 'wo': s(ks[4], (C, C)), 'router_w': s(ks[5], (NE, C)), 'w1': s(ks[6], (NE, HID, C)), 'w2': s(ks[7], (NE, C, HID)), 'w3': s(ks[8], (NE, HID, C))}
    _L0_ffn_all = _L0_ffn_setup()
    _L0_ffn_in = {k: v for k, v in _L0_ffn_all.items() if k in ('ln1_w', 'ln2_w', 'wq', 'wk', 'wv', 'wo', 'router_w', 'w1', 'w2', 'w3')}
    del _L0_ffn_all
    return {'x': x, 'L0_tok_conv_w': _L0_tok_in['conv_w'], 'L0_tok_conv_b': _L0_tok_in['conv_b'], 'L0_tok_wq': _L0_tok_in['wq'], 'L0_tok_bq': _L0_tok_in['bq'], 'L0_tok_wk': _L0_tok_in['wk'], 'L0_tok_bk': _L0_tok_in['bk'], 'L0_tok_wv': _L0_tok_in['wv'], 'L0_tok_bv': _L0_tok_in['bv'], 'L0_tok_wo': _L0_tok_in['wo'], 'L0_tok_bo': _L0_tok_in['bo'], 'L0_attn_nu_log': _L0_attn_in['nu_log'], 'L0_attn_theta_log': _L0_attn_in['theta_log'], 'L0_attn_gamma_log': _L0_attn_in['gamma_log'], 'L0_attn_B_re': _L0_attn_in['B_re'], 'L0_attn_B_im': _L0_attn_in['B_im'], 'L0_attn_C_re': _L0_attn_in['C_re'], 'L0_attn_C_im': _L0_attn_in['C_im'], 'L0_ffn_ln1_w': _L0_ffn_in['ln1_w'], 'L0_ffn_ln2_w': _L0_ffn_in['ln2_w'], 'L0_ffn_wq': _L0_ffn_in['wq'], 'L0_ffn_wk': _L0_ffn_in['wk'], 'L0_ffn_wv': _L0_ffn_in['wv'], 'L0_ffn_wo': _L0_ffn_in['wo'], 'L0_ffn_router_w': _L0_ffn_in['router_w'], 'L0_ffn_w1': _L0_ffn_in['w1'], 'L0_ffn_w2': _L0_ffn_in['w2'], 'L0_ffn_w3': _L0_ffn_in['w3']}

def reference(x, L0_tok_conv_w, L0_tok_conv_b, L0_tok_wq, L0_tok_bq, L0_tok_wk, L0_tok_bk, L0_tok_wv, L0_tok_bv, L0_tok_wo, L0_tok_bo, L0_attn_nu_log, L0_attn_theta_log, L0_attn_gamma_log, L0_attn_B_re, L0_attn_B_im, L0_attn_C_re, L0_attn_C_im, L0_ffn_ln1_w, L0_ffn_ln2_w, L0_ffn_wq, L0_ffn_wk, L0_ffn_wv, L0_ffn_wo, L0_ffn_router_w, L0_ffn_w1, L0_ffn_w2, L0_ffn_w3):
    import jax
    import jax.numpy as jnp

    def _L0_tok_ref(x, conv_w, conv_b, wq, bq, wk, bk, wv, bv, wo, bo):
        import jax, jax.numpy as jnp
        import numpy as np
        from jax import lax
        EMBED_DIM = 64
        B = x.shape[0]
        D = EMBED_DIM
        feat = lax.conv_general_dilated(x, conv_w, window_strides=(2, 2), padding='VALID', dimension_numbers=('NCHW', 'OIHW', 'NCHW'))
        feat = feat + conv_b[None, :, None, None]
        qfeat = feat.reshape(B, -1)
        seq_len = qfeat.shape[1] // D
        qfeat = qfeat.reshape(B, seq_len, D)
        Q = jnp.einsum('bsd,ed->bse', qfeat, wq) + bq
        K = jnp.einsum('bsd,ed->bse', qfeat, wk) + bk
        V = jnp.einsum('bsd,ed->bse', qfeat, wv) + bv
        scores = jax.nn.softmax(jnp.einsum('bse,bte->bst', Q, K) / jnp.sqrt(jnp.float32(D)), axis=-1)
        attn_out = jnp.einsum('bst,bte->bse', scores, V)
        out = jnp.einsum('bse,fe->bsf', attn_out, wo) + bo
        return out

    def _L0_attn_ref(x, nu_log, theta_log, gamma_log, B_re, B_im, C_re, C_im):
        import jax, jax.numpy as jnp
        import numpy as np
        import math
        STATE_DIM = 64
        R_MIN, R_MAX = (0.4, 0.9)
        PHASE_MAX = 2.0 * math.pi
        BATCH, SEQ = (8, 1024)

        def _binop(e_i, e_j):
            a_i, b_i = e_i
            a_j, b_j = e_j
            return (a_j * a_i, a_j * b_i + b_j)
        L_mod = jnp.exp(-jnp.exp(nu_log))
        theta = jnp.exp(theta_log)
        L_diag = (L_mod * jnp.cos(theta) + 1j * L_mod * jnp.sin(theta)).astype(jnp.complex64)
        B = (B_re + 1j * B_im).astype(jnpp.complex64) if False else (B_re + 1j * B_im).astype(jnp.complex64)
        C = (C_re + 1j * C_im).astype(jnp.complex64)
        B_norm = B * jnp.exp(gamma_log)[:, None]
        B_elems = x.astype(jnp.complex64) @ B_norm.T
        L_elems = jnp.broadcast_to(L_diag, B_elems.shape)
        _, inner_states = jax.lax.associative_scan(_binop, (L_elems, B_elems), axis=1)
        return (inner_states @ C.T).real

    def _L0_ffn_ref(x, ln1_w, ln2_w, wq, wk, wv, wo, router_w, w1, w2, w3):
        import jax, jax.numpy as jnp
        import numpy as np
        B, T, C = (64, 96, 64)
        NH, NKV = (4, 2)
        HD = C // NH
        NREP = NH // NKV
        NE, TOPK = (8, 2)
        HID = int(8 / 3 * C)
        EPS_RMS = 1e-06

        def _rope_tables(t_len):
            inv_freq = 1.0 / 10000.0 ** (np.arange(0, HD, 2, dtype=np.float32) / HD)
            t = np.arange(t_len, dtype=np.float32)
            freqs = np.outer(t, inv_freq)
            emb = np.concatenate([freqs, freqs], axis=-1)
            return (jnp.asarray(np.cos(emb)), jnp.asarray(np.sin(emb)))

        def _rotate_half(x):
            h = x.shape[-1] // 2
            return jnp.concatenate([-x[..., h:], x[..., :h]], axis=-1)

        def _rmsnorm(v, w):
            return v * jax.lax.rsqrt(jnp.mean(v * v, axis=-1, keepdims=True) + EPS_RMS) * w
        Bx, Tx, Cx = x.shape
        h = _rmsnorm(x, ln1_w)
        q = (h @ wq.T).reshape(Bx, Tx, NH, HD).transpose(0, 2, 1, 3)
        k = (h @ wk.T).reshape(Bx, Tx, NKV, HD).transpose(0, 2, 1, 3)
        v = (h @ wv.T).reshape(Bx, Tx, NKV, HD).transpose(0, 2, 1, 3)
        cos, sin = _rope_tables(Tx)
        cos, sin = (cos[None, None], sin[None, None])
        q = q * cos + _rotate_half(q) * sin
        k = k * cos + _rotate_half(k) * sin
        k = jnp.repeat(k, NREP, axis=1)
        v = jnp.repeat(v, NREP, axis=1)
        scores = jnp.einsum('bhtd,bhsd->bhts', q, k) / jnp.sqrt(jnp.float32(HD))
        causal = jnp.tril(jnp.ones((Tx, Tx), dtype=bool))
        scores = jnp.where(causal[None, None], scores, jnp.float32(-1e+30))
        att = jax.nn.softmax(scores, axis=-1)
        y = jnp.einsum('bhts,bhsd->bhtd', att, v).transpose(0, 2, 1, 3).reshape(Bx, Tx, Cx)
        x = x + y @ wo.T
        flat = _rmsnorm(x, ln2_w).reshape(-1, Cx)
        probs = jax.nn.softmax(flat @ router_w.T, axis=-1)
        tp, ti = jax.lax.top_k(probs, TOPK)
        tp = tp / (jnp.sum(tp, axis=-1, keepdims=True) + 1e-09)
        weights = jnp.sum(tp[..., None] * jax.nn.one_hot(ti, NE, dtype=flat.dtype), axis=1)
        out = jnp.zeros_like(flat)
        for e in range(NE):
            hh = jax.nn.silu(flat @ w1[e].T) * (flat @ w3[e].T)
            out = out + weights[:, e:e + 1] * (hh @ w2[e].T)
        return x + out.reshape(Bx, Tx, Cx)
    h = _L0_tok_ref(x, L0_tok_conv_w, L0_tok_conv_b, L0_tok_wq, L0_tok_bq, L0_tok_wk, L0_tok_bk, L0_tok_wv, L0_tok_bv, L0_tok_wo, L0_tok_bo)
    h = h + _L0_attn_ref(_layernorm(h, axis=-1), L0_attn_nu_log, L0_attn_theta_log, L0_attn_gamma_log, L0_attn_B_re, L0_attn_B_im, L0_attn_C_re, L0_attn_C_im)
    h = h + _L0_ffn_ref(_layernorm(h, axis=-1), L0_ffn_ln1_w, L0_ffn_ln2_w, L0_ffn_wq, L0_ffn_wk, L0_ffn_wv, L0_ffn_wo, L0_ffn_router_w, L0_ffn_w1, L0_ffn_w2, L0_ffn_w3)
    return h

_drawn_inputs = setup_inputs


def setup_inputs(seed=0):
    import zlib

    import numpy as np

    out = dict(_drawn_inputs(seed))
    spreads = {'L0_ffn_ln1_w': (1.0, 0.6), 'L0_ffn_ln2_w': (1.0, 0.6)}
    factors = {'L0_tok_bq': 3.291,
     'L0_tok_bk': 8.0,
     'L0_ffn_wq': 8.0,
     'L0_ffn_wk': 8.0,
     'L0_ffn_wv': 8.0,
     'L0_ffn_wo': 8.0,
     'L0_ffn_router_w': 8.0,
     'L0_ffn_w1': 8.0,
     'L0_ffn_w2': 8.0,
     'L0_ffn_w3': 8.0}
    for name, (base, spread) in spreads.items():
        noise = np.random.default_rng([zlib.crc32(name.encode()), seed]).standard_normal(out[name].shape)
        drawn = base * np.exp(spread * noise) if base else spread * noise
        out[name] = jnp.asarray(drawn.astype(out[name].dtype))
    for name, factor in factors.items():
        out[name] = (out[name] * factor).astype(out[name].dtype)
    return out
```

```python
import numpy as np
from contextlib import ExitStack
import concourse.bass as bass
from concourse import mybir

D = 64
S = 144
IMAGES = 64
SIDE = 96
PAIRS = 4
GROUPS = IMAGES // (2 * PAIRS)
W = PAIRS * S
HW = W // 2
HS = S // 2
BANDS = SIDE // 8
CH = 4
NH, NKV, HD = 4, 2, 16
HP = 32
NE, HID = 8, 170
EH = NE * HID
TILES = -(-EH // 128)
CHUNKS = 3
CW = 2 * W // CHUNKS
QW = CW // 2
TC = 96
NTC = W // TC

C_ID, C_AVG, C_HM, C_ROPE, C_PRI, C_NEG = 0, 128, 256, 264, 552, 560
C_DUP = C_NEG + HS
C_END = C_DUP + 256


def constants():
    f = np.float32
    c = np.zeros((128, C_END), f)
    c[:, C_ID:C_ID + 128] = np.eye(128, dtype=f)
    for p in range(2):
        c[64 * p:64 * p + 64, C_AVG + 64 * p:C_AVG + 64 * p + 64] = 1.0 / D
    for h in range(8):
        c[16 * h:16 * h + 16, C_HM + h] = HD ** -0.5
    inv = 1.0 / 10000.0 ** (np.arange(0, HD, 2, dtype=f) / HD)
    fr = np.outer(np.arange(S, dtype=f), inv)
    emb = np.concatenate([fr, fr], -1)
    c[:, C_ROPE:C_ROPE + S] = np.tile(np.cos(emb).T, (8, 1))
    c[:, C_ROPE + S:C_ROPE + 2 * S] = np.tile(np.sin(emb).T, (8, 1))
    c[:, C_PRI:C_PRI + NE] = np.arange(NE, 0, -1)
    t = np.arange(HS)
    c[:HS, C_NEG:C_NEG + HS] = np.where(t[None, :] > t[:, None], -1e30, 0.0)
    for p in range(2):
        for r in range(2):
            c[64 * p:64 * p + 64, C_DUP + 128 * p + 64 * r:C_DUP + 128 * p + 64 * r + 64] = np.eye(D, dtype=f)
    s = np.zeros((40, EH), f)
    for e in range(NE):
        s[e, e * HID:(e + 1) * HID] = 1.0
        s[32 + e, e * HID:(e + 1) * HID] = 1.0
    return c, s


def vit_tower(nc, x, conv_w, conv_b, wq, bq, wk, bk, wv, bv, wo, bo, nu_log, theta_log, gamma_log,
              B_re, B_im, C_re, C_im, ln1_w, ln2_w, wq2, wk2, wv2, wo2, router_w, w1, w2, w3,
              consts, experts, out):
    fp32, bf16, f32r = mybir.dt.float32, mybir.dt.bfloat16, mybir.dt.float32r
    ALU, ACT, AX = mybir.AluOpType, mybir.ActivationFunctionType, mybir.AxisListType
    PI = float(np.pi)

    ctx = ExitStack()
    with ctx:
        def sb(name, shape, dt=fp32):
            return ctx.enter_context(nc.sbuf_tensor(name, shape, dt))

        class Count:
            def __init__(self, name, per):
                self.sem, self.per = ctx.enter_context(nc.semaphore(name)), per

            def at(self, g, n):
                return g * self.per + n

        def one(name):
            return ctx.enter_context(nc.semaphore(name))

        cst = sb("cst", [128, C_END])
        ident = cst[:, C_ID:C_ID + 128]
        avg = cst[:, C_AVG:C_AVG + 128]
        rope_cos = cst[:, C_ROPE:C_ROPE + S]
        rope_sin = cst[:, C_ROPE + S:C_ROPE + 2 * S]
        ident_b = sb("ident_b", [128, 128], bf16)
        neg_b = sb("neg_b", [HS, HS], bf16)
        ones = sb("ones", [HS, D])
        NR = 13
        (R_WQ, R_WK, R_WO, R_BRE, R_BIM, R_CRE, R_CIM, R_WQ2, R_WK2, R_WV2, R_WO2, R_RT, R_WV) = range(NR)
        raw = sb("raw", [128, NR, 128])
        wt = sb("wt", [128, NR - 1, 128])
        wvo = sb("wvo", [128, 128])
        q_rot = sb("q_rot", [128, 128])
        k_rot = sb("k_rot", [128, 128])
        w1h, w1l = sb("w1h", [128, EH], f32r), sb("w1l", [128, EH], f32r)
        w3h, w3l = sb("w3h", [128, EH], f32r), sb("w3l", [128, EH], f32r)
        sel = sb("sel", [128, EH], f32r)
        w2t = sb("w2t", [128, TILES, D])
        V_BQ, V_BK, V_BV, V_BO, V_NU, V_TH, V_GA, V_L1, V_L2 = range(9)
        col = sb("col", [128, 9])
        bq8 = sb("bq8", [128, 1])
        bvo = sb("bvo", [128, 1])
        cw = sb("cw", [TC, CH * 4])
        cb = sb("cb", [TC, CH])
        eps = sb("eps", [128, 2])
        tmp = sb("tmp", [128, 8])
        ang = sb("ang", [128, 8])
        lam = sb("lam", [128, 1])
        gam = sb("gam", [128, 1])
        rot_cos, rot_sin = sb("rot_cos", [128, S]), sb("rot_sin", [128, S])
        rot_t = sb("rot_t", [128, S])
        decay = sb("decay", [128, W])

        img = sb("img", [TC, 768])
        y = sb("y", [TC, CH, 192])
        xf = sb("xf", [128, W])
        qf = sb("qf", [128, W])
        kbd = sb("kbd", [128, PAIRS, 2, S])
        v1 = sb("v1", [HS, 2 * PAIRS, 128])
        nm1 = sb("nm1", [HS, 2, 2])
        pb1 = sb("pb1", [HS, 2, 2 * S])
        pt1 = sb("pt1", [HS, 2, 2 * S])
        rc1 = sb("rc1", [128, 2, HS])
        h1 = sb("h1", [128, W])
        cen = sb("cen", [128, W])
        sq = sb("sq", [128, W])
        rstd = sb("rstd", [128, W])
        xn = sb("xn", [128, W])
        t4 = sb("t4", [128, 4, W])
        zin = sb("zin", [128, 2, W])
        z = sb("z", [128, 2, W])
        ab = sb("ab", [128, 2, W])
        h2 = sb("h2", [128, W])
        xl = sb("xl", [128, W])
        xr = sb("xr", [128, W])
        q2 = sb("q2", [128, W])
        k2 = sb("k2", [128, W])
        km = sb("km", [128, 8, W])
        kmf, t4f = km[:, :, :].rearrange("q h w -> q (h w)"), t4[:, :, :].rearrange("q k w -> q (k w)")
        RW = TILES * 2 * D
        raw1 = kmf[:, 0:RW].rearrange("q (k r c) -> q k r c", k=TILES, r=2)
        raw3 = kmf[:, RW:2 * RW].rearrange("q (k r c) -> q k r c", k=TILES, r=2)
        raw2 = kmf[0:D, 2 * RW:2 * RW + EH]
        sel_raw = t4f[0:40, 0:EH]
        w_full = z[:, :, 0:512]
        v2 = sb("v2", [HS, 2 * PAIRS, 128])
        nm2 = sb("nm2", [HS, 2, 4])
        pb2 = sb("pb2", [HS, 2, 3 * S])
        pt2 = sb("pt2", [HS, 2, 3 * S])
        rc2 = sb("rc2", [128, 2, S])
        on2 = sb("on2", [128, 2, S])
        h3 = sb("h3", [128, W])
        h23 = sb("h23", [128, W])
        flat = sb("flat", [128, W])
        NT = 2 * NTC
        rl = sb("rl", [TC, NT, NE])
        re = sb("re", [TC, NT, NE])
        rk = sb("rk", [TC, NT, NE])
        rs1 = sb("rs1", [TC, NT, NE])
        rs2 = sb("rs2", [TC, NT, NE])
        rt = sb("rt", [TC, NT, NE])
        rm = sb("rm", [TC, 6, NT])
        wtok = sb("wtok", [TC, NT, 40])
        wrow = sb("wrow", [128, 2 * W], f32r)
        xs = sb("xs", [128, 2 * W], f32r)
        sg = sb("sg", [128, 2, CW])
        tg = sb("tg", [128, 2, CW])
        hh = sb("hh", [128, 3, CW])
        h4 = sb("h4", [128, W])
        ot = sb("ot", [TC, NTC, 128])

        P = [ctx.enter_context(nc.psum_tensor(f"P{i}", [128, 512], fp32)) for i in range(8)]

        s_zero, s_cst, s_col, s_raw = one("s_zero"), one("s_cst"), one("s_col"), one("s_raw")
        s_rex = one("s_rex")
        s_tr, s_ev = one("s_tr"), one("s_ev")
        s_dch, s_ach, s_pch = one("s_dch"), one("s_ach"), one("s_pch")
        s_gam, s_lin, s_ang, s_sin = one("s_gam"), one("s_lin"), one("s_ang"), one("s_sin")
        s_dset, s_aset, s_pset = one("s_dset"), one("s_aset"), one("s_pset")
        s_img = Count("s_img", 32)
        s_cv0, s_cv, s_ft, s_xe = Count("s_cv0", 4), Count("s_cv", 12), Count("s_ft", 2), Count("s_xe", 4)
        s_qkv, s_qe, s_ke, s_ve = Count("s_qkv", 6), Count("s_qe", 2), Count("s_ke", 4), Count("s_ve", 2)
        U1 = 2 * PAIRS
        (s_s1, s_m1, s_d1, s_e1, s_t1, s_pt1, s_o1, s_r1, s_h1) = (
            Count(n, U1) for n in ("s_s1", "s_m1", "s_d1", "s_e1", "s_t1", "s_pt1", "s_o1", "s_r1", "s_h1"))
        s_h1b = Count("s_h1b", 2)
        norms = [{k: Count(f"s_{k}{n}", 2) for k in ("mean", "cen", "sq", "var", "ln", "rs", "nx")} for n in range(2)]
        norms += [{k: Count(f"s_{k}{n}", 2) for k in ("sq", "var", "ln", "rs", "nx")} for n in range(2, 4)]
        s_b, s_rm, s_ra, s_sc = Count("s_b", 4), Count("s_rm", 8), Count("s_ra", 4), Count("s_sc", 2)
        s_rb, s_rc, s_y, s_h2 = Count("s_rb", 4), Count("s_rc", 2), Count("s_y", 2), Count("s_h2", 2)
        s_qk2, s_rp, s_rq, s_km = Count("s_qk2", 8), Count("s_rp", 8), Count("s_rq", 4), Count("s_km", 8)
        s_v2, s_v2e = Count("s_v2", 2), Count("s_v2e", 2)
        U2 = PAIRS * 4
        (s_s2, s_e2, s_t2, s_pt2, s_o2) = (Count(n, U2) for n in ("s_s2", "s_e2", "s_t2", "s_pt2", "s_o2"))
        s_m2, s_d2 = Count("s_m2", 2 * U2), Count("s_d2", 2 * U2)
        s_r2, s_on, s_at = (Count(n, 2 * PAIRS) for n in ("s_r2", "s_on", "s_at"))
        s_h3, s_h23 = Count("s_h3", PAIRS), Count("s_h23", 1)
        TOPK = 18
        s_rt, s_tk, s_re = Count("s_rt", 1), Count("s_tk", TOPK), Count("s_re", 1)
        s_wk = Count("s_wk", 2)
        s_wt, s_wh, s_wl = Count("s_wt", 3), Count("s_wh", 3), Count("s_wl", 3)
        s_dup, s_xh, s_xl = Count("s_dup", 3), Count("s_xh", 3), Count("s_xl", 3)
        N = CHUNKS * TILES
        s_g, s_u, s_wb, s_sg, s_tg, s_hh = (Count(n, N) for n in ("s_g", "s_u", "s_wb", "s_sg", "s_tg", "s_hh"))
        s_yo, s_h4 = Count("s_yo", N), Count("s_h4", 3)
        s_ot, s_oe, s_out = Count("s_ot", 2), Count("s_oe", 2), Count("s_out", 32)

        def half(t, a):
            return t[:, a * HW:(a + 1) * HW]

        def two(t, a):
            return half(t, a).rearrange("q (i s) -> q i s", s=S)

        def per_token(t):
            return t.unsqueeze(1).broadcast_to([128, 2, S])

        def rows(k):
            return min(128, EH - 128 * k)

        RAWV = [(V_BQ, bq), (V_BK, bk), (V_BV, bv), (V_BO, bo), (V_NU, nu_log), (V_TH, theta_log),
                (V_GA, gamma_log), (V_L1, ln1_w), (V_L2, ln2_w)]

        block = ctx.enter_context(nc.Block())

        @block.sync
        def _(sp):
            sp.dma_start(cst[:, :], consts).then_inc(s_cst, 16)
            sp.dma_start(sel_raw, experts).then_inc(s_cst, 16)
            for k, v in RAWV:
                for p in range(2):
                    sp.dma_start(col[64 * p:64 * p + 64, k:k + 1], v.rearrange("(d a) -> d a", a=1)).then_inc(s_col, 16)
            sp.dma_start(cw[:, :], conv_w.rearrange("c a i j -> (c a i j)").partition_broadcast(TC)).then_inc(s_col, 16)
            sp.dma_start(cb[:, :], conv_b.partition_broadcast(TC)).then_inc(s_col, 16)
            sp.wait_ge(s_zero, 2)
            for p in range(2):
                for k, m in ((R_WQ, wq), (R_WK, wk), (R_WO, wo), (R_WV, wv), (R_BRE, B_re), (R_BIM, B_im),
                             (R_CRE, C_re), (R_CIM, C_im), (R_WQ2, wq2)):
                    sp.dma_start(raw[64 * p:64 * p + 64, k, 64 * p:64 * p + 64], m).then_inc(s_raw, 16)
                for h in range(NH):
                    kv = h // (NH // NKV)
                    r = 64 * p + HD * h
                    sp.dma_start(raw[r:r + HD, R_WK2, 64 * p:64 * p + 64], wk2[HD * kv:HD * kv + HD, :]).then_inc(s_raw, 16)
                for kv in range(NKV):
                    r = 64 * p + HP * kv
                    sp.dma_start(raw[r:r + HD, R_WV2, 64 * p:64 * p + 64], wv2[HD * kv:HD * kv + HD, :]).then_inc(s_raw, 16)
                sp.dma_start(raw[NE * p:NE * p + NE, R_RT, 64 * p:64 * p + 64], router_w).then_inc(s_raw, 16)
            sp.dma_start(raw[0:64, R_WO2, :].rearrange("f (h d) -> f h d", h=NH)[:, :, 0:HD],
                         wo2.rearrange("f (h d) -> f h d", h=NH)).then_inc(s_raw, 16)
            full = (TILES - 1) * 128
            for t, m in ((raw1, w1), (raw3, w3)):
                f = m.rearrange("e h c -> (e h) c")
                for r in range(2):
                    sp.dma_start(t[:, 0:TILES - 1, r, :], f[0:full, :].rearrange("(k q) c -> q k c", q=128)).then_inc(s_rex, 16)
                    sp.dma_start(t[0:EH - full, TILES - 1, r, :], f[full:EH, :]).then_inc(s_rex, 16)
            sp.dma_start(raw2.rearrange("f (e h) -> f e h", e=NE), w2.rearrange("e f h -> f e h")).then_inc(s_rex, 16)

            xv = x.rearrange("b a h w -> (b a h w)").rearrange("(n r) -> n r", r=768)
            half_rows = IMAGES // 2 * BANDS
            ov = out.rearrange("b s d -> (b s) d")
            half_tok = IMAGES // 2 * S

            def load(g):
                for p in range(2):
                    sp.dma_start(img[48 * p:48 * p + 48, :],
                                 xv[bass.ds(g * (PAIRS * BANDS) + p * half_rows, PAIRS * BANDS), :]).then_inc(s_img.sem, 16)

            def store(g):
                for p in range(2):
                    sp.dma_start(ov[bass.ds(g * W + p * half_tok, W), :].rearrange("(c r) d -> r c d", r=TC),
                                 ot[:, :, 64 * p:64 * p + 64]).then_inc(s_out.sem, 16)

            load(0)
            with sp.Fori(1, GROUPS) as g:
                sp.wait_ge(s_cv.sem, s_cv.at(g, 0))
                load(g)
                sp.wait_ge(s_oe.sem, s_oe.at(g, 0))
                store(g - 1)
            sp.wait_ge(s_oe.sem, s_oe.at(GROUPS, 0))
            store(GROUPS - 1)
            sp.wait_ge(s_out.sem, s_out.per * GROUPS + 1)

        @block.gpsimd
        def _(pool):
            nc.gpsimd.memset(raw[:, :, :], 0.0).then_inc(s_zero, 1)
            nc.gpsimd.memset(kbd[:, :, :, :], 0.0).then_inc(s_zero, 1)
            nc.gpsimd.memset(wtok[:, :, :], 0.0).then_inc(s_pset, 1)
            nc.gpsimd.memset(wrow[:, :].bitcast(fp32), 0.0).then_inc(s_pset, 1)
            nc.gpsimd.memset(sel[:, :].bitcast(fp32), 0.0).then_inc(s_pset, 1)
            nc.gpsimd.memset(ones[:, :], 1.0).then_inc(s_pset, 1)
            nc.gpsimd.memset(ot[:, :, :], 0.0).then_inc(s_out.sem, 1)
            nc.gpsimd.memset(eps[:, 0:1], 1e-5).then_inc(s_pset, 1)
            nc.gpsimd.memset(eps[:, 1:2], 1e-6).then_inc(s_pset, 1)
            with pool.Fori(0, GROUPS) as g:
                for a in range(2):
                    pool.wait_ge(s_rm.sem, s_rm.at(g, 4 * a + 4))
                    nc.gpsimd.tensor_tensor(half(zin[:, 0], a), half(t4[:, 0], a), half(t4[:, 1], a), ALU.add).then_inc(s_ra.sem, 1)
                    nc.gpsimd.tensor_tensor(half(zin[:, 1], a), half(t4[:, 2], a), half(t4[:, 3], a), ALU.subtract).then_inc(s_ra.sem, 1)
                pool.wait_ge(s_rb.sem, s_rb.at(g, 4))
                nc.gpsimd.tensor_tensor(ab[:, 0], t4[:, 0], t4[:, 1], ALU.subtract).then_inc(s_rc.sem, 1)
                nc.gpsimd.tensor_tensor(ab[:, 1], t4[:, 2], t4[:, 3], ALU.add).then_inc(s_rc.sem, 1)
                for n, (dst, a) in enumerate(((q2, 0), (q2, 1), (k2, 0), (k2, 1))):
                    pool.wait_ge(s_rp.sem, s_rp.at(g, 2 * n + 2))
                    k = 2 * (n // 2)
                    nc.gpsimd.tensor_tensor(half(dst[:, :], a), half(t4[:, k], a), half(t4[:, k + 1], a), ALU.add).then_inc(s_rq.sem, 1)
                pool.wait_ge(s_h3.sem, s_h3.at(g, PAIRS))
                nc.gpsimd.tensor_tensor(h23[:, :], h2[:, :], h3[:, :], ALU.add).then_inc(s_h23.sem, 1)

        @block.scalar
        def _(act):
            chain = [0]

            def link(ins):
                chain[0] += 1
                ins.then_inc(s_ach, 1)
                act.wait_ge(s_ach, chain[0])

            act.wait_ge(s_cst, 32)
            act.wait_ge(s_pset, 6)
            nc.scalar.activation(ident_b[:, :], ident, ACT.Copy).then_inc(s_aset, 1)
            nc.scalar.activation(neg_b[:, :], cst[0:HS, C_NEG:C_NEG + HS], ACT.Copy).then_inc(s_aset, 1)
            nc.scalar.activation(sel[0:40, :], sel_raw, ACT.Copy).then_inc(s_aset, 1)
            act.wait_ge(s_col, 20 * 16)
            link(nc.scalar.activation(tmp[:, 0:1], col[:, V_NU:V_NU + 1], ACT.Exp))
            nc.scalar.activation(lam[:, :], tmp[:, 0:1], ACT.Exp, scale=-1.0).then_inc(s_lin, 1)
            nc.scalar.activation(tmp[:, 1:2], col[:, V_TH:V_TH + 1], ACT.Exp).then_inc(s_lin, 1)
            nc.scalar.activation(gam[:, :], col[:, V_GA:V_GA + 1], ACT.Exp).then_inc(s_gam, 1)
            act.wait_ge(s_ang, 1)
            nc.scalar.activation(ang[:, 6:7], ang[:, 4:5], ACT.Sin).then_inc(s_sin, 1)
            nc.scalar.activation(ang[:, 7:8], ang[:, 5:6], ACT.Sin).then_inc(s_sin, 1)

            with act.Fori(0, GROUPS) as g:
                act.wait_ge(s_img.sem, s_img.at(g, 32))
                iv = img[:, :].rearrange("q (i a j b) -> q i a j b", i=4, a=2, b=2)
                for c in range(CH):
                    nc.scalar.activation(y[:, c, :].rearrange("q (i j) -> q i j", i=4), iv[:, :, 0, :, 0], ACT.Identity,
                                         bias=cb[:, c:c + 1], scale=cw[:, 4 * c:4 * c + 1]).then_inc(s_cv0.sem, 1)
                for c in range(CH):
                    act.wait_ge(s_ft.sem, s_ft.at(g, 1 + c // 2))
                    src = P[c // 2][:, (c % 2) * 144:(c % 2) * 144 + 144].rearrange("q (k i b) -> q k i b", k=3, i=PAIRS)
                    dst = xf[:, :].rearrange("q (i c b k) -> q c k i b", i=PAIRS, c=CH, k=3)[:, c]
                    nc.scalar.activation(dst, src, ACT.Copy).then_inc(s_xe.sem, 1)
                for a in range(2):
                    act.wait_ge(s_qkv.sem, s_qkv.at(g, 1 + a))
                    nc.scalar.activation(half(qf[:, :], a), P[2 + a][:, 0:HW], ACT.Identity,
                                         bias=bq8[:, 0:1], scale=D ** -0.5).then_inc(s_qe.sem, 1)
                for a in range(2):
                    act.wait_ge(s_qkv.sem, s_qkv.at(g, 5 + a))
                    nc.scalar.activation(v1[:, 4 * a:4 * a + 4, :].rearrange("q i e -> q (i e)"), P[6 + a][0:HS, :],
                                         ACT.Copy).then_inc(s_ve.sem, 1)

                def attn1_out(u):
                    act.wait_ge(s_t1.sem, s_t1.at(g, u + 1))
                    nc.scalar.activation(pt1[:, u % 2], P[2 + u % 2][0:HS, 0:2 * S], ACT.Copy).then_inc(s_pt1.sem, 1)

                for u in range(U1):
                    act.wait_ge(s_d1.sem, s_d1.at(g, u + 1))
                    nc.scalar.activation(pb1[:, u % 2], pb1[:, u % 2], ACT.Exp).then_inc(s_e1.sem, 1)
                    if u >= 1:
                        if u >= 3:
                            act.wait_ge(s_o1.sem, s_o1.at(g, u - 2))
                        attn1_out(u - 1)
                act.wait_ge(s_o1.sem, s_o1.at(g, U1 - 2))
                attn1_out(U1 - 1)
                for a in range(2):
                    act.wait_ge(s_h1.sem, s_h1.at(g, 4 * a + 4))
                    nc.scalar.activation(half(h1[:, :], a), half(h1[:, :], a), ACT.Identity, bias=bvo[:, 0:1]).then_inc(s_h1b.sem, 1)

                def norm(n, src, ready, e):
                    s = norms[n]
                    for a in range(2):
                        act.wait_ge(ready.sem, ready.at(g, (ready.per // 2) * (a + 1)))
                        nc.scalar.activation(half(sq[:, :], a), half(src[:, :], a), ACT.Square).then_inc(s["sq"].sem, 1)
                    for a in range(2):
                        act.wait_ge(s["var"].sem, s["var"].at(g, a + 1))
                        nc.scalar.activation(half(rstd[:, :], a), P[2 + a][:, 0:HW], ACT.Ln, bias=eps[:, e:e + 1]).then_inc(s["ln"].sem, 1)
                    for a in range(2):
                        act.wait_ge(s["ln"].sem, s["ln"].at(g, a + 1))
                        nc.scalar.activation(half(rstd[:, :], a), half(rstd[:, :], a), ACT.Exp, scale=-0.5).then_inc(s["rs"].sem, 1)

                norm(0, cen, norms[0]["cen"], 0)
                norm(1, cen, norms[1]["cen"], 0)
                norm(2, xl, norms[1]["nx"], 1)
                act.wait_ge(s_rq.sem, s_rq.at(g, 4))
                for h in range(8):
                    nc.scalar.activation(km[:, h, :], k2[:, :], ACT.Copy, scale=cst[:, C_HM + h:C_HM + h + 1]).then_inc(s_km.sem, 1)
                for a in range(2):
                    act.wait_ge(s_v2.sem, s_v2.at(g, a + 1))
                    nc.scalar.activation(v2[:, 4 * a:4 * a + 4, :].rearrange("q i e -> q (i e)"), P[a][0:HS, :],
                                         ACT.Copy).then_inc(s_v2e.sem, 1)

                def attn2_out(v):
                    act.wait_ge(s_t2.sem, s_t2.at(g, v + 1))
                    nc.scalar.activation(pt2[:, v % 2], P[2 + v % 2][0:HS, 0:3 * S], ACT.Copy).then_inc(s_pt2.sem, 1)

                for v in range(U2):
                    act.wait_ge(s_d2.sem, s_d2.at(g, 2 * v + 2))
                    nc.scalar.activation(pb2[:, v % 2], pb2[:, v % 2], ACT.Exp).then_inc(s_e2.sem, 1)
                    if v >= 1:
                        if v >= 3:
                            act.wait_ge(s_o2.sem, s_o2.at(g, v - 2))
                        attn2_out(v - 1)
                act.wait_ge(s_o2.sem, s_o2.at(g, U2 - 2))
                attn2_out(U2 - 1)
                norm(3, h3, s_h3, 1)
                act.wait_ge(s_tk.sem, s_tk.at(g, 2))
                nc.scalar.activation(re[:, :, :], rl[:, :, :], ACT.Exp).then_inc(s_re.sem, 1)
                for q in range(CHUNKS):
                    act.wait_ge(s_dup.sem, s_dup.at(g, q + 1))
                    nc.scalar.activation(xs[:, q * CW:(q + 1) * CW], P[q][:, 0:CW], ACT.Copy).then_inc(s_xh.sem, 1)
                for q in range(CHUNKS):
                    act.wait_ge(s_wt.sem, s_wt.at(g, q + 1))
                    nc.scalar.activation(wrow[0:40, q * CW:(q + 1) * CW], P[5 + q][0:40, 0:CW], ACT.Copy).then_inc(s_wh.sem, 1)
                for n in range(N):
                    m = rows(n % TILES)
                    act.wait_ge(s_g.sem, s_g.at(g, n + 1))
                    if n >= 2:
                        act.wait_ge(s_tg.sem, s_tg.at(g, n - 1))
                    nc.scalar.activation(sg[0:m, n % 2], P[n % 2][0:m, 0:CW], ACT.Silu).then_inc(s_sg.sem, 1)
                for a in range(2):
                    act.wait_ge(s_ot.sem, s_ot.at(g, a + 1))
                    if a == 0:
                        act.wait_ge(s_out.sem, s_out.at(g, 1))
                    nc.scalar.activation(ot[:, 3 * a:3 * a + 3, :].rearrange("q c e -> q (c e)"), P[a][0:TC, 0:CW],
                                         ACT.Copy).then_inc(s_oe.sem, 1)

        @block.vector
        def _(dve):
            V = nc.vector
            chain = [0]

            def link(ins):
                chain[0] += 1
                ins.then_inc(s_dch, 1)
                dve.wait_ge(s_dch, chain[0])

            dve.wait_ge(s_col, 20 * 16)
            dve.wait_ge(s_raw, 33 * 16)
            dve.wait_ge(s_gam, 1)
            for k in (R_BRE, R_BIM):
                V.tensor_scalar(raw[:, k, :], raw[:, k, :], gam[:, 0:1], None, ALU.mult).then_inc(s_gam, 1)
            dve.wait_ge(s_lin, 2)
            link(V.tensor_copy(ang[:, 0:1], tmp[:, 1:2]))
            link(V.tensor_scalar_add(ang[:, 1:2], ang[:, 0:1], PI / 2))
            link(V.tensor_scalar(ang[:, 2:4], ang[:, 0:2], 1 / (2 * PI), 12582912.0, ALU.mult, ALU.add))
            link(V.tensor_scalar_add(ang[:, 2:4], ang[:, 2:4], -12582912.0))
            hi = 6.28125
            link(V.scalar_tensor_tensor(out=ang[:, 4:6], in0=ang[:, 2:4], scalar=-hi, in1=ang[:, 0:2], op0=ALU.mult, op1=ALU.add))
            link(V.scalar_tensor_tensor(out=ang[:, 4:6], in0=ang[:, 2:4], scalar=-(2 * PI - hi), in1=ang[:, 4:6], op0=ALU.mult, op1=ALU.add))
            pi32 = 3.1415925
            V.tensor_scalar(ang[:, 4:6], ang[:, 4:6], pi32, -pi32, ALU.min, ALU.max).then_inc(s_ang, 1)
            link(V.memset(rot_cos[:, 0:1], 1.0))
            link(V.memset(rot_sin[:, 0:1], 0.0))
            dve.wait_ge(s_sin, 2)
            link(V.tensor_copy(rot_sin[:, 1:2], ang[:, 6:7]))
            link(V.tensor_copy(rot_cos[:, 1:2], ang[:, 7:8]))
            m = 1
            while m < S - 1:
                n = min(m, S - 1 - m)
                c, s = rot_cos[:, m:m + 1], rot_sin[:, m:m + 1]
                a, b = slice(1, 1 + n), slice(m + 1, m + 1 + n)
                link(V.tensor_scalar(rot_t[:, a], rot_sin[:, a], s, None, ALU.mult))
                link(V.scalar_tensor_tensor(out=rot_cos[:, b], in0=rot_cos[:, a], scalar=c, in1=rot_t[:, a], op0=ALU.mult, op1=ALU.subtract))
                link(V.tensor_scalar(rot_t[:, a], rot_cos[:, a], s, None, ALU.mult))
                link(V.scalar_tensor_tensor(out=rot_sin[:, b], in0=rot_sin[:, a], scalar=c, in1=rot_t[:, a], op0=ALU.mult, op1=ALU.add))
                m *= 2
            link(V.memset(decay[:, :], 1.0))
            link(V.tensor_scalar(decay[:, :], decay[:, :], lam[:, 0:1], None, ALU.mult))
            link(V.memset(decay[:, :].rearrange("q (i s) -> q i s", s=S)[:, :, 0:1], 0.0))
            V.tensor_scalar(bq8[:, :], col[:, V_BQ:V_BQ + 1], D ** -0.5, None, ALU.mult).then_inc(s_dset, 1)
            for k in range(3):
                dve.wait_ge(s_tr, k + 1)
                V.tensor_copy(wt[:, 4 * k:4 * k + 4, :].rearrange("q a b -> q (a b)"), P[k][:, :]).then_inc(s_ev, 1)
            dve.wait_ge(s_ev, 3)
            for k in (R_WQ2, R_WK2, R_WV2):
                link(V.tensor_scalar(wt[:, k, :], wt[:, k, :], col[:, V_L1:V_L1 + 1], None, ALU.mult))
            link(V.tensor_scalar(wt[:, R_RT, :], wt[:, R_RT, :], col[:, V_L2:V_L2 + 1], None, ALU.mult))
            link(V.tensor_scalar(wt[:, R_CIM, :], wt[:, R_CIM, :], -1.0, None, ALU.mult))
            for k, dst in ((R_WQ2, q_rot), (R_WK2, k_rot)):
                a = wt[:, k, :].rearrange("q (h r j) -> q h r j", r=2, j=HD // 2)
                b = dst[:, :].rearrange("q (h r j) -> q h r j", r=2, j=HD // 2)
                V.tensor_scalar(b[:, :, 0], a[:, :, 1], -1.0, None, ALU.mult).then_inc(s_dset, 1)
                V.tensor_copy(b[:, :, 1], a[:, :, 0]).then_inc(s_dset, 1)
            n_ev = 3
            for j, (wh, wl) in enumerate(((w1h, w1l), (w3h, w3l))):
                for k in range(3):
                    lo, hi_ = 512 * k, min(512 * (k + 1), EH)
                    n = 3 * j + k
                    w = w_full[:, n % 2, 0:hi_ - lo]
                    dve.wait_ge(s_tr, 4 + n)
                    link(V.tensor_scalar(w, P[(3 + n) % 8][:, 0:hi_ - lo], col[:, V_L2:V_L2 + 1], None, ALU.mult))
                    link(V.tensor_copy(wh[:, lo:hi_], w))
                    V.tensor_tensor(wl[:, lo:hi_], w, wh[:, lo:hi_].bitcast(fp32), ALU.subtract).then_inc(s_ev, 1)
            for k, (b, t0, t1) in enumerate(((1, 0, 8), (2, 8, TILES))):
                dve.wait_ge(s_tr, 10 + k)
                full = t1 if t1 < TILES else TILES - 1
                V.tensor_copy(w2t[:, t0:full, :].rearrange("q a b -> q (a b)"), P[b][:, 0:D * (full - t0)]).then_inc(s_dset, 1)
                if full < t1:
                    r = rows(full)
                    V.tensor_copy(w2t[0:r, full, :], P[b][0:r, D * (full - t0):D * (full - t0 + 1)]).then_inc(s_dset, 1)
            dve.wait_ge(s_tr, 12)
            V.tensor_copy(wvo[:, :], P[3][:, 0:128]).then_inc(s_dset, 1)
            V.tensor_scalar(bvo[:, :], P[3][:, 128:129], col[:, V_BO:V_BO + 1], None, ALU.add).then_inc(s_dset, 1)

            with dve.Fori(0, GROUPS) as g:
                iv = img[:, :].rearrange("q (i a j b) -> q i a j b", i=4, a=2, b=2)
                for t in range(1, 4):
                    for c in range(CH):
                        if t == 1:
                            dve.wait_ge(s_cv0.sem, s_cv0.at(g, c + 1))
                        else:
                            dve.wait_ge(s_cv.sem, s_cv.at(g, 4 * (t - 2) + c + 1))
                        yc = y[:, c, :].rearrange("q (i j) -> q i j", i=4)
                        V.scalar_tensor_tensor(out=yc, in0=iv[:, :, t // 2, :, t % 2], scalar=cw[:, 4 * c + t:4 * c + t + 1],
                                               in1=yc, op0=ALU.mult, op1=ALU.add).then_inc(s_cv.sem, 1)
                for a in range(2):
                    dve.wait_ge(s_qkv.sem, s_qkv.at(g, 3 + a))
                    for p in range(2):
                        q = slice(64 * p, 64 * p + 64)
                        V.tensor_scalar(kbd[q, 2 * a:2 * a + 2, p, :], P[4 + a][q, 0:HW].rearrange("q (i s) -> q i s", s=S),
                                        col[q, V_BK:V_BK + 1], None, ALU.add).then_inc(s_ke.sem, 1)

                def attn1_close(u):
                    b = P[4 + u % 2]
                    i, sh = u // 2, u % 2
                    dve.wait_ge(s_o1.sem, s_o1.at(g, u + 1))
                    V.reciprocal(rc1[:, u % 2], b[:, HS:2 * HS]).then_inc(s_r1.sem, 1)
                    dve.wait_ge(s_r1.sem, s_r1.at(g, u + 1))
                    V.tensor_tensor(h1[:, i * S + sh * HS:i * S + (sh + 1) * HS], b[:, 0:HS], rc1[:, u % 2],
                                    ALU.mult).then_inc(s_h1.sem, 1)

                for u in range(U1):
                    sc = P[u % 2][0:HS, 0:2 * S].rearrange("q (p t) -> q p t", p=2)
                    dve.wait_ge(s_s1.sem, s_s1.at(g, u + 1))
                    V.tensor_reduce(nm1[:, u % 2, :], sc, AX.X, ALU.max).then_inc(s_m1.sem, 1)
                    dve.wait_ge(s_m1.sem, s_m1.at(g, u + 1))
                    if u >= 2:
                        dve.wait_ge(s_t1.sem, s_t1.at(g, u - 1))
                    V.tensor_tensor(pb1[:, u % 2].rearrange("q (p t) -> q p t", p=2), sc,
                                    nm1[:, u % 2, :].unsqueeze(2).broadcast_to([HS, 2, S]), ALU.subtract).then_inc(s_d1.sem, 1)
                    if u >= 2:
                        attn1_close(u - 2)
                attn1_close(U1 - 2)
                attn1_close(U1 - 1)

                def centre(n, src):
                    s = norms[n]
                    for a in range(2):
                        dve.wait_ge(s["mean"].sem, s["mean"].at(g, a + 1))
                        V.tensor_tensor(half(cen[:, :], a), half(src[:, :], a), P[a][:, 0:HW], ALU.subtract).then_inc(s["cen"].sem, 1)

                def scale(n, src, dst):
                    s = norms[n]
                    for a in range(2):
                        dve.wait_ge(s["rs"].sem, s["rs"].at(g, a + 1))
                        V.tensor_tensor(half(dst[:, :], a), half(src[:, :], a), half(rstd[:, :], a), ALU.mult).then_inc(s["nx"].sem, 1)

                centre(0, h1)
                scale(0, cen, xn)
                for a in range(2):
                    dve.wait_ge(s_b.sem, s_b.at(g, 2 * a + 2))
                    re_in = P[4 + 2 * a][:, 0:HW].rearrange("q (i s) -> q i s", s=S)
                    im_in = P[5 + 2 * a][:, 0:HW].rearrange("q (i s) -> q i s", s=S)
                    for k, (v, c) in enumerate(((re_in, rot_cos), (im_in, rot_sin), (im_in, rot_cos), (re_in, rot_sin))):
                        V.tensor_tensor(two(t4[:, k], a), v, per_token(c[:, :]), ALU.mult).then_inc(s_rm.sem, 1)
                for r in range(2):
                    dve.wait_ge(s_ra.sem, s_ra.at(g, 4))
                    V.tensor_tensor_scan(z[:, r], decay[:, :], zin[:, r], 0.0, ALU.mult, ALU.add).then_inc(s_sc.sem, 1)
                for k, (r, c) in enumerate(((0, rot_cos), (1, rot_sin), (0, rot_sin), (1, rot_cos))):
                    dve.wait_ge(s_sc.sem, s_sc.at(g, 2))
                    V.tensor_tensor(t4[:, k].rearrange("q (i s) -> q i s", s=S), z[:, r].rearrange("q (i s) -> q i s", s=S),
                                    c[:, :].unsqueeze(1).broadcast_to([128, PAIRS, S]), ALU.mult).then_inc(s_rb.sem, 1)
                for a in range(2):
                    dve.wait_ge(s_y.sem, s_y.at(g, a + 1))
                    V.tensor_tensor(half(h2[:, :], a), half(h1[:, :], a), P[a][:, 0:HW], ALU.add).then_inc(s_h2.sem, 1)
                centre(1, h2)
                scale(1, cen, xl)
                scale(2, xl, xr)
                for n in range(4):
                    a, k = n % 2, 2 * (n // 2)
                    for j, c in enumerate((rope_cos, rope_sin)):
                        dve.wait_ge(s_qk2.sem, s_qk2.at(g, 2 * n + j + 1))
                        V.tensor_tensor(two(t4[:, k + j], a), P[2 * n + j][:, 0:HW].rearrange("q (i s) -> q i s", s=S),
                                        per_token(c), ALU.mult).then_inc(s_rp.sem, 1)

                def attn2_close(b):
                    o = P[4 + b % 2]
                    dve.wait_ge(s_o2.sem, s_o2.at(g, 2 * b + 2))
                    V.reciprocal(rc2[:, b % 2], o[:, S:2 * S]).then_inc(s_r2.sem, 1)
                    dve.wait_ge(s_r2.sem, s_r2.at(g, b + 1))
                    if b >= 2:
                        dve.wait_ge(s_at.sem, s_at.at(g, b - 1))
                    V.tensor_tensor(on2[:, b % 2], o[:, 0:S], rc2[:, b % 2], ALU.mult).then_inc(s_on.sem, 1)

                def residual(i):
                    dve.wait_ge(s_at.sem, s_at.at(g, 2 * i + 2))
                    t = slice(i * S, (i + 1) * S)
                    V.tensor_tensor(h3[:, t], xl[:, t], P[6 + i % 2][:, 0:S], ALU.add).then_inc(s_h3.sem, 1)

                for v in range(U2):
                    b = P[v % 2]
                    s0 = b[0:HS, 0:S].rearrange("q (h t) -> q h t", h=2)
                    s1 = b[0:HS, S:3 * S].rearrange("q (h t) -> q h t", h=2)
                    dve.wait_ge(s_s2.sem, s_s2.at(g, v + 1))
                    V.tensor_reduce(nm2[:, v % 2, 0:2], s0, AX.X, ALU.max).then_inc(s_m2.sem, 1)
                    V.tensor_reduce(nm2[:, v % 2, 2:4], s1, AX.X, ALU.max).then_inc(s_m2.sem, 1)
                    if v >= 2:
                        dve.wait_ge(s_t2.sem, s_t2.at(g, v - 1))
                    dve.wait_ge(s_m2.sem, s_m2.at(g, 2 * v + 1))
                    V.tensor_tensor(pb2[:, v % 2, 0:S].rearrange("q (h t) -> q h t", h=2), s0,
                                    nm2[:, v % 2, 0:2].unsqueeze(2).broadcast_to([HS, 2, HS]), ALU.subtract).then_inc(s_d2.sem, 1)
                    dve.wait_ge(s_m2.sem, s_m2.at(g, 2 * v + 2))
                    V.tensor_tensor(pb2[:, v % 2, S:3 * S].rearrange("q (h t) -> q h t", h=2), s1,
                                    nm2[:, v % 2, 2:4].unsqueeze(2).broadcast_to([HS, 2, S]), ALU.subtract).then_inc(s_d2.sem, 1)
                    if v >= 3 and v % 2:
                        attn2_close((v - 3) // 2)
                    if v >= 7 and v % 4 == 3:
                        residual((v - 7) // 4)
                attn2_close(2 * PAIRS - 1)
                residual(PAIRS - 1)
                scale(3, h3, flat)

                full = [TC, NT, NE]

                def wide(k):
                    return rm[:, k, :].unsqueeze(2).broadcast_to(full)

                pri = cst[0:TC, C_PRI:C_PRI + NE].unsqueeze(1).broadcast_to(full)
                step = [0]

                def then(ins, wait=True):
                    step[0] += 1
                    ins.then_inc(s_tk.sem, 1)
                    if wait:
                        dve.wait_ge(s_tk.sem, s_tk.at(g, step[0]))

                dve.wait_ge(s_rt.sem, s_rt.at(g, 1))
                logits = P[4][0:TC, 0:NT * NE].rearrange("q (n e) -> q n e", e=NE)
                then(V.tensor_reduce(rm[:, 0, :], logits, AX.X, ALU.max))
                then(V.tensor_tensor(rl[:, :, :], logits, wide(0), ALU.subtract))
                then(V.tensor_scalar(rk[:, :, :], rl[:, :, :], 0.0, None, ALU.is_ge))
                then(V.tensor_tensor(rk[:, :, :], rk[:, :, :], pri, ALU.mult))
                then(V.tensor_reduce(rm[:, 1, :], rk[:, :, :], AX.X, ALU.max))
                then(V.tensor_tensor(rs1[:, :, :], rk[:, :, :], wide(1), ALU.is_equal))
                then(V.scalar_tensor_tensor(out=rt[:, :, :], in0=rs1[:, :, :], scalar=-1e30, in1=rl[:, :, :], op0=ALU.mult, op1=ALU.add))
                then(V.tensor_reduce(rm[:, 2, :], rt[:, :, :], AX.X, ALU.max))
                then(V.tensor_tensor(rk[:, :, :], rt[:, :, :], wide(2), ALU.is_equal))
                then(V.tensor_tensor(rk[:, :, :], rk[:, :, :], pri, ALU.mult))
                then(V.tensor_reduce(rm[:, 3, :], rk[:, :, :], AX.X, ALU.max))
                then(V.tensor_tensor(rs2[:, :, :], rk[:, :, :], wide(3), ALU.is_equal))
                then(V.tensor_tensor(rs1[:, :, :], rs1[:, :, :], rs2[:, :, :], ALU.add))
                dve.wait_ge(s_re.sem, s_re.at(g, 1))
                then(V.tensor_tensor(rt[:, :, :], re[:, :, :], rs1[:, :, :], ALU.mult), wait=False)
                then(V.tensor_reduce(rm[:, 4, :], re[:, :, :], AX.X, ALU.add))
                then(V.tensor_reduce(rm[:, 5, :], rt[:, :, :], AX.X, ALU.add))
                then(V.scalar_tensor_tensor(out=rm[:, 5, :], in0=rm[:, 4, :], scalar=1e-9, in1=rm[:, 5, :], op0=ALU.mult, op1=ALU.add))
                then(V.reciprocal(rm[:, 5, :], rm[:, 5, :]))
                assert step[0] == TOPK
                for r in range(2):
                    V.tensor_tensor(wtok[:, :, 32 * r:32 * r + NE], rt[:, :, :], wide(5), ALU.mult).then_inc(s_wk.sem, 1)
                for q in range(CHUNKS):
                    c = slice(q * CW, (q + 1) * CW)
                    dve.wait_ge(s_xh.sem, s_xh.at(g, q + 1))
                    V.tensor_tensor(xs[64:128, c], P[q][64:128, 0:CW], xs[64:128, c].bitcast(fp32), ALU.subtract).then_inc(s_xl.sem, 1)
                for q in range(CHUNKS):
                    c = slice(q * CW, (q + 1) * CW)
                    dve.wait_ge(s_wh.sem, s_wh.at(g, q + 1))
                    V.tensor_tensor(wrow[32:40, c], P[5 + q][32:40, 0:CW], wrow[32:40, c].bitcast(fp32), ALU.subtract).then_inc(s_wl.sem, 1)

                def finish(q):
                    c = slice(q * QW, (q + 1) * QW)
                    dve.wait_ge(s_yo.sem, s_yo.at(g, TILES * (q + 1)))
                    if q == 0:
                        dve.wait_ge(s_h23.sem, s_h23.at(g, 1))
                    V.tensor_tensor(h4[:, c], h23[:, c], P[6 + q % 2][:, 0:QW], ALU.add).then_inc(s_h4.sem, 1)

                for n in range(N):
                    m = rows(n % TILES)
                    dve.wait_ge(s_sg.sem, s_sg.at(g, n + 1))
                    dve.wait_ge(s_u.sem, s_u.at(g, n + 1))
                    if n >= 2:
                        dve.wait_ge(s_hh.sem, s_hh.at(g, n - 1))
                    V.tensor_tensor(tg[0:m, n % 2], sg[0:m, n % 2], P[2 + n % 2][0:m, 0:CW], ALU.mult).then_inc(s_tg.sem, 1)
                    dve.wait_ge(s_tg.sem, s_tg.at(g, n + 1))
                    dve.wait_ge(s_wb.sem, s_wb.at(g, n + 1))
                    if n >= 3:
                        dve.wait_ge(s_yo.sem, s_yo.at(g, n - 2))
                    V.tensor_tensor(hh[0:m, n % 3], tg[0:m, n % 2], P[4 + n % 2][0:m, 0:CW], ALU.mult).then_inc(s_hh.sem, 1)
                    if n % TILES == 3 and n > TILES:
                        finish(n // TILES - 1)
                finish(CHUNKS - 1)

        @block.tensor
        def _(pe):
            mm = nc.tensor.matmul
            pe.wait_ge(s_cst, 32)
            pe.wait_ge(s_raw, 33 * 16)
            pe.wait_ge(s_gam, 3)
            for k in range(12):
                last = nc.tensor.transpose(P[k // 4][:, (k % 4) * 128:(k % 4 + 1) * 128], raw[:, k, :], ident)
                if k % 4 == 3:
                    last.then_inc(s_tr, 1)
            pe.wait_ge(s_rex, 9 * 16)
            for j, src in enumerate((raw1, raw3)):
                for k in range(TILES):
                    n = 3 * j + k // 4
                    if k % 4 == 0 and 3 + n >= 8:
                        pe.wait_ge(s_ev, 1)
                    m = rows(k)
                    last = nc.tensor.transpose(P[(3 + n) % 8][:, (k % 4) * 128:(k % 4) * 128 + m],
                                               src[0:m, k].rearrange("q r c -> q (r c)"), ident[0:m, 0:m])
                    if k % 4 == 3 or k == TILES - 1:
                        last.then_inc(s_tr, 1)
            pe.wait_ge(s_ev, 3)
            for k in range(TILES):
                m = rows(k)
                last = nc.tensor.transpose(P[1 + k // 8][0:m, (k % 8) * D:(k % 8 + 1) * D], raw2[:, 128 * k:128 * k + m],
                                           ident[0:D, 0:D])
                if k in (7, TILES - 1):
                    last.then_inc(s_tr, 1)
            pe.wait_ge(s_ev, 4)
            mm(P[3][:, 0:128], raw[:, R_WV, :], wt[:, R_WO, :], start=True, stop=True)
            mm(P[3][:, 128:129], wt[:, R_WO, :], col[:, V_BV:V_BV + 1], start=True, stop=True).then_inc(s_tr, 1)
            pe.wait_ge(s_dset, 10)
            pe.wait_ge(s_aset, 3)
            pe.wait_ge(s_pset, 6)
            pe.wait_ge(s_ev, 9)

            with pe.Fori(0, GROUPS) as g:
                pe.wait_ge(s_cv.sem, s_cv.at(g, 12))
                for c in range(CH):
                    for k in range(3):
                        for p in range(2):
                            o = (c % 2) * 144 + k * 48
                            last = mm(P[c // 2][64 * p:64 * p + 64, o:o + 48], y[:, c, 64 * k:64 * k + 64],
                                      ident[0:TC, 48 * p:48 * p + 48], start=True, stop=True)
                    if c % 2:
                        last.then_inc(s_ft.sem, 1)
                pe.wait_ge(s_xe.sem, s_xe.at(g, 4))
                for a in range(2):
                    mm(P[2 + a][:, 0:HW], wt[:, R_WQ, :], half(xf[:, :], a), start=True, stop=True).then_inc(s_qkv.sem, 1)
                for a in range(2):
                    mm(P[4 + a][:, 0:HW], wt[:, R_WK, :], half(xf[:, :], a), start=True, stop=True).then_inc(s_qkv.sem, 1)
                for n in range(2 * PAIRS):
                    last = mm(P[6 + n // 4][0:HS, (n % 4) * 128:(n % 4 + 1) * 128], xf[:, n * HS:(n + 1) * HS], wvo[:, :],
                              start=True, stop=True)
                    if n % 4 == 3:
                        last.then_inc(s_qkv.sem, 1)

                def score1(u):
                    if u == 0:
                        pe.wait_ge(s_qe.sem, s_qe.at(g, 2))
                        pe.wait_ge(s_ke.sem, s_ke.at(g, 4))
                    if u >= 2:
                        pe.wait_ge(s_d1.sem, s_d1.at(g, u - 1))
                    mm(P[u % 2][0:HS, 0:2 * S], qf[:, u * HS:(u + 1) * HS], kbd[:, u // 2].rearrange("q p t -> q (p t)"),
                       start=True, stop=True).then_inc(s_s1.sem, 1)

                def turn1(u):
                    pe.wait_ge(s_e1.sem, s_e1.at(g, u + 1))
                    if u >= 2:
                        pe.wait_ge(s_pt1.sem, s_pt1.at(g, u - 1))
                    for k in range(4):
                        last = nc.tensor.transpose(P[2 + u % 2][0:HS, k * HS:(k + 1) * HS], pb1[:, u % 2, k * HS:(k + 1) * HS],
                                                   ident[0:HS, 0:HS])
                    last.then_inc(s_t1.sem, 1)

                def value1(u):
                    i, b = u // 2, P[4 + u % 2]
                    if u == 0:
                        pe.wait_ge(s_ve.sem, s_ve.at(g, 2))
                    pe.wait_ge(s_pt1.sem, s_pt1.at(g, u + 1))
                    if u >= 2:
                        pe.wait_ge(s_h1.sem, s_h1.at(g, u - 1))
                    for w in range(2):
                        for th in range(2):
                            for p in range(2):
                                lhs = ones[:, :] if w else v1[:, 2 * i + th, 64 * p:64 * p + 64]
                                k = 2 * p + th
                                last = mm(b[64 * p:64 * p + 64, w * HS:(w + 1) * HS], lhs, pt1[:, u % 2, k * HS:(k + 1) * HS],
                                          start=(th == 0), stop=(th == 1))
                    last.then_inc(s_o1.sem, 1)

                score1(0)
                score1(1)
                for u in range(U1):
                    turn1(u)
                    if u + 2 < U1:
                        score1(u + 2)
                    if u >= 1:
                        value1(u - 1)
                value1(U1 - 1)

                def mean(n, src, ready):
                    s = norms[n]
                    for a in range(2):
                        pe.wait_ge(ready.sem, ready.at(g, a + 1))
                        mm(P[a][:, 0:HW], avg, half(src[:, :], a), start=True, stop=True).then_inc(s["mean"].sem, 1)

                def var(n):
                    s = norms[n]
                    for a in range(2):
                        pe.wait_ge(s["sq"].sem, s["sq"].at(g, a + 1))
                        mm(P[2 + a][:, 0:HW], avg, half(sq[:, :], a), start=True, stop=True).then_inc(s["var"].sem, 1)

                mean(0, h1, s_h1b)
                var(0)
                for a in range(2):
                    pe.wait_ge(norms[0]["nx"].sem, norms[0]["nx"].at(g, a + 1))
                    mm(P[4 + 2 * a][:, 0:HW], wt[:, R_BRE, :], half(xn[:, :], a), start=True, stop=True).then_inc(s_b.sem, 1)
                    mm(P[5 + 2 * a][:, 0:HW], wt[:, R_BIM, :], half(xn[:, :], a), start=True, stop=True).then_inc(s_b.sem, 1)
                pe.wait_ge(s_rc.sem, s_rc.at(g, 2))
                for a in range(2):
                    mm(P[a][:, 0:HW], wt[:, R_CRE, :], half(ab[:, 0], a), start=True, stop=False)
                    mm(P[a][:, 0:HW], wt[:, R_CIM, :], half(ab[:, 1], a), start=False, stop=True).then_inc(s_y.sem, 1)
                mean(1, h2, s_h2)
                var(1)
                var(2)
                pe.wait_ge(norms[2]["nx"].sem, norms[2]["nx"].at(g, 2))
                for n in range(4):
                    a = n % 2
                    for j, w in enumerate((wt[:, R_WQ2, :], q_rot[:, :]) if n < 2 else (wt[:, R_WK2, :], k_rot[:, :])):
                        mm(P[2 * n + j][:, 0:HW], w, half(xr[:, :], a), start=True, stop=True).then_inc(s_qk2.sem, 1)
                pe.wait_ge(s_rp.sem, s_rp.at(g, 2))
                for n in range(2 * PAIRS):
                    last = mm(P[n // 4][0:HS, (n % 4) * 128:(n % 4 + 1) * 128], xr[:, n * HS:(n + 1) * HS], wt[:, R_WV2, :],
                              start=True, stop=True)
                    if n % 4 == 3:
                        last.then_inc(s_v2.sem, 1)

                def score2(v):
                    i, h0 = v // 4, 2 * (v % 4)
                    b = P[v % 2]
                    if v == 0:
                        pe.wait_ge(s_km.sem, s_km.at(g, 8))
                        pe.wait_ge(s_v2e.sem, s_v2e.at(g, 2))
                    if v >= 2:
                        pe.wait_ge(s_d2.sem, s_d2.at(g, 2 * v - 2))
                    mm(b[0:HS, 0:S], q2[:, i * S:i * S + HS], km[:, h0:h0 + 2, i * S:i * S + HS], start=True, stop=False)
                    mm(b[0:HS, 0:S], ident_b[0:HS, 0:HS], neg_b[:, :].unsqueeze(1).broadcast_to([HS, 2, HS]),
                       start=False, stop=True)
                    late = b[0:HS, S:3 * S].rearrange("q (h t) -> q h t", h=2)
                    mm(late, q2[:, i * S + HS:(i + 1) * S], km[:, h0:h0 + 2, i * S:(i + 1) * S], start=True, stop=False)
                    mm(late[:, :, HS:S], ident_b[0:HS, 0:HS], neg_b[:, :].unsqueeze(1).broadcast_to([HS, 2, HS]),
                       start=False, stop=True).then_inc(s_s2.sem, 1)

                def turn2(v):
                    pe.wait_ge(s_e2.sem, s_e2.at(g, v + 1))
                    if v >= 2:
                        pe.wait_ge(s_pt2.sem, s_pt2.at(g, v - 1))
                    b, src = P[2 + v % 2], pb2[:, v % 2]
                    for h in range(2):
                        for dst, s in ((h * S, h * HS), (h * S + HS, S + h * S), (2 * S + h * HS, S + h * S + HS)):
                            last = nc.tensor.transpose(b[0:HS, dst:dst + HS], src[:, s:s + HS], ident[0:HS, 0:HS])
                    last.then_inc(s_t2.sem, 1)

                def value2(v):
                    i, p, kv = v // 4, v // 2 % 2, v % 2
                    b = P[4 + v // 2 % 2]
                    pe.wait_ge(s_pt2.sem, s_pt2.at(g, v + 1))
                    if kv == 0 and v >= 4:
                        pe.wait_ge(s_on.sem, s_on.at(g, v // 2 - 1))
                    e = slice(64 * p + HP * kv, 64 * p + HP * kv + HP)
                    for w in range(2):
                        for h in range(2):
                            o = b[64 * kv + HP * h:64 * kv + HP * h + HP, w * S:(w + 1) * S]
                            pt = pt2[:, v % 2]
                            mm(o, ones[:, 0:HP] if w else v2[:, 2 * i, e], pt[:, h * S:(h + 1) * S], start=True, stop=False)
                            last = mm(o[:, HS:S], ones[:, 0:HP] if w else v2[:, 2 * i + 1, e],
                                      pt[:, 2 * S + h * HS:2 * S + (h + 1) * HS], start=False, stop=True)
                    last.then_inc(s_o2.sem, 1)

                def project2(b):
                    i, p = b // 2, b % 2
                    pe.wait_ge(s_on.sem, s_on.at(g, b + 1))
                    if p == 0 and i >= 2:
                        pe.wait_ge(s_h3.sem, s_h3.at(g, i - 1))
                    mm(P[6 + i % 2][64 * p:64 * p + 64, 0:S], wt[:, R_WO2, 0:D], on2[:, b % 2], start=True,
                       stop=True).then_inc(s_at.sem, 1)

                score2(0)
                score2(1)
                for v in range(U2):
                    turn2(v)
                    if v + 2 < U2:
                        score2(v + 2)
                    if v >= 1:
                        value2(v - 1)
                    if v >= 4 and v % 2 == 0:
                        project2(v // 2 - 2)
                value2(U2 - 1)
                project2(2 * PAIRS - 2)
                project2(2 * PAIRS - 1)
                var(3)
                pe.wait_ge(norms[3]["nx"].sem, norms[3]["nx"].at(g, 2))
                for c in range(NTC):
                    last = mm(P[4][0:TC, c * 2 * NE:(c + 1) * 2 * NE], flat[:, c * TC:(c + 1) * TC], wt[:, R_RT, 0:2 * NE],
                              start=True, stop=True)
                last.then_inc(s_rt.sem, 1)
                for q in range(CHUNKS):
                    for p in range(2):
                        last = mm(P[q][:, p * QW:(p + 1) * QW],
                                  cst[:, C_DUP + 128 * p:C_DUP + 128 * p + 128],
                                  flat[:, q * QW:(q + 1) * QW], start=True, stop=True)
                    last.then_inc(s_dup.sem, 1)
                pe.wait_ge(s_wk.sem, s_wk.at(g, 2))
                for q in range(CHUNKS):
                    for p in range(2):
                        for c in range(2):
                            o = p * QW + c * TC
                            last = mm(P[5 + q][0:40, o:o + TC], wtok[:, (2 * q + c) * 2 + p, :], ident[0:TC, 0:TC],
                                      start=True, stop=True)
                    last.then_inc(s_wt.sem, 1)
                pe.wait_ge(s_xl.sem, s_xl.at(g, 3))
                pe.wait_ge(s_wl.sem, s_wl.at(g, 3))

                def second(n):
                    q, k = n // TILES, n % TILES
                    m = rows(k)
                    pe.wait_ge(s_hh.sem, s_hh.at(g, n + 1))
                    if k == 0 and q >= 2:
                        pe.wait_ge(s_h4.sem, s_h4.at(g, q - 1))
                    for p in range(2):
                        last = mm(P[6 + q % 2][64 * p:64 * p + 64, 0:QW], w2t[0:m, k, :], hh[0:m, n % 3, p * QW:(p + 1) * QW],
                                  start=(k == 0), stop=(k == TILES - 1))
                    last.then_inc(s_yo.sem, 1)

                for n in range(N):
                    q, k = n // TILES, n % TILES
                    m = rows(k)
                    e = slice(128 * k, 128 * k + m)
                    xq = xs[:, q * CW:(q + 1) * CW]
                    if n >= 2:
                        pe.wait_ge(s_sg.sem, s_sg.at(g, n - 1))
                    mm(P[n % 2][0:m, 0:CW], w1h[:, e], xq, start=True, stop=False)
                    mm(P[n % 2][0:m, 0:CW], w1l[:, e], xq, start=False, stop=True).then_inc(s_g.sem, 1)
                    if n >= 2:
                        pe.wait_ge(s_tg.sem, s_tg.at(g, n - 1))
                    mm(P[2 + n % 2][0:m, 0:CW], w3h[:, e], xq, start=True, stop=False)
                    mm(P[2 + n % 2][0:m, 0:CW], w3l[:, e], xq, start=False, stop=True).then_inc(s_u.sem, 1)
                    if n >= 2:
                        pe.wait_ge(s_hh.sem, s_hh.at(g, n - 1))
                    mm(P[4 + n % 2][0:m, 0:CW], sel[:, e], wrow[:, q * CW:(q + 1) * CW], start=True, stop=True).then_inc(s_wb.sem, 1)
                    if n >= 2:
                        second(n - 2)
                second(N - 2)
                second(N - 1)
                for c in range(NTC):
                    pe.wait_ge(s_h4.sem, s_h4.at(g, c // 2 + 1))
                    last = nc.tensor.transpose(P[c // 3][0:TC, (c % 3) * 128:(c % 3 + 1) * 128], h4[:, c * TC:(c + 1) * TC], ident)
                    if c % 3 == 2:
                        last.then_inc(s_ot.sem, 1)


_INS = ["x", "L0_tok_conv_w", "L0_tok_conv_b", "L0_tok_wq", "L0_tok_bq", "L0_tok_wk", "L0_tok_bk", "L0_tok_wv", "L0_tok_bv",
        "L0_tok_wo", "L0_tok_bo", "L0_attn_nu_log", "L0_attn_theta_log", "L0_attn_gamma_log", "L0_attn_B_re", "L0_attn_B_im",
        "L0_attn_C_re", "L0_attn_C_im", "L0_ffn_ln1_w", "L0_ffn_ln2_w", "L0_ffn_wq", "L0_ffn_wk", "L0_ffn_wv", "L0_ffn_wo",
        "L0_ffn_router_w", "L0_ffn_w1", "L0_ffn_w2", "L0_ffn_w3"]


def kernel(**inputs):
    import numpy as _np
    import concourse.bacc as _bacc
    from concourse import mybir as _mybir
    from concourse.bass_utils import run_bass_kernel_spmd as _run

    nc = _bacc.Bacc("TRN2", target_bir_lowering=False, num_devices=1)
    arrays, args = {}, []
    c, s = constants()
    for name, a in [(n, inputs[n]) for n in _INS] + [("consts", c), ("experts", s)]:
        a = _np.ascontiguousarray(a)
        arrays[f"in_{name}_dram"] = a
        args.append(nc.dram_tensor(f"in_{name}_dram", a.shape, _mybir.dt.from_np(a.dtype), kind="ExternalInput").ap())
    args.append(nc.dram_tensor("out_0_dram", (IMAGES, S, D), _mybir.dt.float32, kind="ExternalOutput").ap())
    vit_tower(nc, *args)
    r = _run(nc, [arrays], core_ids=[0])
    return r.results[0]["out_0_dram"]
```

```python
import numpy as np
from contextlib import ExitStack
import concourse.bass as bass
from concourse import mybir

D = 64
S = 144
IMAGES = 64
SIDE = 96
PAIRS = 4
GROUPS = IMAGES // (2 * PAIRS)
ROUNDS = GROUPS // 2
W = PAIRS * S
HW = W // 2
HS = S // 2
QA = 128
QB = S - QA
BANDS = SIDE // 8
CH = 4
NH, NKV, HD = 4, 2, 16
HP = 32
NE, HID = 8, 170
EH = NE * HID
TILES = -(-EH // 128)
CHUNKS = 3
CW = 2 * W // CHUNKS
QW = CW // 2
TC = 96
NTC = W // TC

C_ID, C_AVG, C_CEN, C_HM, C_ROPE, C_PRI, C_NEG = 0, 128, 256, 384, 392, 680, 688
C_DUP = C_NEG + S
C_END = C_DUP + 256


def constants():
    f = np.float32
    c = np.zeros((128, C_END), f)
    c[:, C_ID:C_ID + 128] = np.eye(128, dtype=f)
    for p in range(2):
        c[64 * p:64 * p + 64, C_AVG + 64 * p:C_AVG + 64 * p + 64] = 1.0 / D
    c[:, C_CEN:C_CEN + 128] = c[:, C_ID:C_ID + 128] - c[:, C_AVG:C_AVG + 128]
    for h in range(8):
        c[16 * h:16 * h + 16, C_HM + h] = HD ** -0.5
    inv = 1.0 / 10000.0 ** (np.arange(0, HD, 2, dtype=f) / HD)
    fr = np.outer(np.arange(S, dtype=f), inv)
    emb = np.concatenate([fr, fr], -1)
    c[:, C_ROPE:C_ROPE + S] = np.tile(np.cos(emb).T, (8, 1))
    c[:, C_ROPE + S:C_ROPE + 2 * S] = np.tile(np.sin(emb).T, (8, 1))
    c[:, C_PRI:C_PRI + NE] = np.arange(NE, 0, -1)
    t = np.arange(QA)
    c[:, C_NEG:C_NEG + QA] = np.where(t[None, :] > t[:, None], -1e30, 0.0)
    c[:, C_NEG + QA:C_NEG + S] = np.where(t[None, :QB] > t[:, None] % QB, -1e30, 0.0)
    for p in range(2):
        for r in range(2):
            c[64 * p:64 * p + 64, C_DUP + 128 * p + 64 * r:C_DUP + 128 * p + 64 * r + 64] = np.eye(D, dtype=f)
    s = np.zeros((40, EH), f)
    for e in range(NE):
        s[e, e * HID:(e + 1) * HID] = 1.0
        s[32 + e, e * HID:(e + 1) * HID] = 1.0
    return c, s


def vit_tower(nc, x, conv_w, conv_b, wq, bq, wk, bk, wv, bv, wo, bo, nu_log, theta_log, gamma_log,
              B_re, B_im, C_re, C_im, ln1_w, ln2_w, wq2, wk2, wv2, wo2, router_w, w1, w2, w3,
              consts, experts, out):
    fp32, bf16, f32r = mybir.dt.float32, mybir.dt.bfloat16, mybir.dt.float32r
    ALU, ACT, AX = mybir.AluOpType, mybir.ActivationFunctionType, mybir.AxisListType
    PI = float(np.pi)

    ctx = ExitStack()
    with ctx:
        def sb(name, shape, dt=fp32):
            return ctx.enter_context(nc.sbuf_tensor(name, shape, dt))

        class Count:
            def __init__(self, name, per):
                self.sem, self.per = ctx.enter_context(nc.semaphore(name)), per

            def at(self, r, n, st=0):
                return r * (2 * self.per) + st * self.per + n

        def one(name):
            return ctx.enter_context(nc.semaphore(name))

        cst = sb("cst", [128, C_END])
        ident = cst[:, C_ID:C_ID + 128]
        avg = cst[:, C_AVG:C_AVG + 128]
        centre = cst[:, C_CEN:C_CEN + 128]
        rope_cos = cst[:, C_ROPE:C_ROPE + S]
        rope_sin = cst[:, C_ROPE + S:C_ROPE + 2 * S]
        ident_b = sb("ident_b", [128, 128], bf16)
        neg_b = sb("neg_b", [128, S], bf16)
        NR = 14
        (R_WQ, R_WK, R_WO, R_BRE, R_BIM, R_CRE, R_CIM, R_WQ2, R_WK2, R_WV2, R_WO2, R_RT, R_WO3, R_WV) = range(NR)
        wt = sb("wt", [128, NR - 1, 128])
        wvo = sb("wvo", [128, 128])
        q_rot = sb("q_rot", [128, 128])
        k_rot = sb("k_rot", [128, 128])
        w1h, w1l = sb("w1h", [128, EH], f32r), sb("w1l", [128, EH], f32r)
        w3h, w3l = sb("w3h", [128, EH], f32r), sb("w3l", [128, EH], f32r)
        sel = sb("sel", [128, EH], f32r)
        w2t = sb("w2t", [128, TILES, D])
        V_BQ, V_BK, V_BV, V_BO, V_NU, V_TH, V_GA, V_L1, V_L2 = range(9)
        col = sb("col", [128, 9])
        bq8 = sb("bq8", [128, 1])
        bvo = sb("bvo", [128, 1])
        cw = sb("cw", [TC, CH * 4])
        cb = sb("cb", [TC, CH])
        eps = sb("eps", [128, 2])
        tmp = sb("tmp", [128, 8])
        ang = sb("ang", [128, 8])
        lam = sb("lam", [128, 1])
        gam = sb("gam", [128, 1])
        rot_cos, rot_sin = sb("rot_cos", [128, S]), sb("rot_sin", [128, S])
        decay = sb("decay", [128, W])

        def both(name, shape, dt=fp32):
            return [sb(f"{name}{st}", shape, dt) for st in range(2)]

        NT = 2 * NTC
        img = both("img", [TC, 768])
        y = both("y", [TC, CH, 192])
        t4 = both("t4", [128, 4, W])
        km = both("km", [128, 8, W])
        kbd = both("kbd", [128, PAIRS, 2, S])
        h1 = both("h1", [128, W])
        h2 = both("h2", [128, W])
        xl = both("xl", [128, W])
        h3 = both("h3", [128, W])
        q2 = both("q2", [128, W])
        k2 = both("k2", [128, W])
        vt = both("vt", [128, 2 * PAIRS, 128])
        pt = both("pt", [128, 4 * QA])
        ex = both("ex", [128, 2, 3, 4])
        rl, re, rk, rs1, rs2, rt = (both(n, [TC, NT, NE]) for n in ("rl", "re", "rk", "rs1", "rs2", "rt"))
        rm = both("rm", [TC, 6, NT])
        wtok = both("wtok", [TC, NT, 40])
        ot = both("ot", [TC, NTC, 128])
        wrow = both("wrow", [128, 2 * W], f32r)
        xs = both("xs", [128, 2 * W], f32r)
        sg = sb("sg", [128, 2, CW])
        tg = sb("tg", [128, 2, CW])
        hh = sb("hh", [128, 3, CW])
        zin = [t[:, 0:2] for t in km]
        z = [t[:, 2:4] for t in km]
        ab = [t[:, 4:6] for t in km]
        xn = [t[:, 6] for t in km]
        xf = [t[:, 7] for t in km]
        qf = [t[:, 2] for t in km]
        xr = [t[:, :] for t in h1]
        sq = [t[:, 0] for t in t4]
        rstd = [t[:, 1] for t in t4]
        flat = [t[:, 2] for t in t4]
        pw = [(t[:, 0, 0:4 * QA], t[:, 3, 0:4 * QA]) for t in t4]
        qt = [t[:, 1, 0:4 * QA] for t in t4]
        on = [t[:, 2, 0:2 * S] for t in t4]
        kmf = [t[:, :, :].rearrange("q h w -> q (h w)") for t in km]
        RW = TILES * 2 * D
        raw1 = kmf[0][:, 0:RW].rearrange("q (k r c) -> q k r c", k=TILES, r=2)
        raw3 = kmf[0][:, RW:2 * RW].rearrange("q (k r c) -> q k r c", k=TILES, r=2)
        raw2 = kmf[0][0:D, 2 * RW:2 * RW + EH]
        raw = kmf[1][:, 0:NR * 128].rearrange("q (a b) -> q a b", a=NR)
        w_full = kmf[1][:, NR * 128:NR * 128 + 1024].rearrange("q (a b) -> q a b", a=2)
        rot_t = kmf[1][:, NR * 128 + 1024:NR * 128 + 1024 + S]
        sel_raw = t4[0][:, :, :].rearrange("q k w -> q (k w)")[0:40, 0:EH]

        PS = ctx.enter_context(nc.psum_tensor("PS", [128, 8, 512], fp32))

        s_zero, s_cst, s_col, s_raw = one("s_zero"), one("s_cst"), one("s_col"), one("s_raw")
        s_rex = one("s_rex")
        s_tr, s_ev = one("s_tr"), one("s_ev")
        s_dch, s_ach = one("s_dch"), one("s_ach")
        s_gam, s_lin, s_ang, s_sin = one("s_gam"), one("s_lin"), one("s_ang"), one("s_sin")
        s_dset, s_aset, s_pset = one("s_dset"), one("s_aset"), one("s_pset")
        s_img = [one(f"s_img{st}") for st in range(2)]
        s_out = [one(f"s_out{st}") for st in range(2)]
        s_cv0, s_cv, s_ft, s_xe = Count("s_cv0", 4), Count("s_cv", 12), Count("s_ft", 2), Count("s_xe", 4)
        s_q, s_k, s_v, s_qe, s_ke, s_ve = (Count(n, c) for n, c in (
            ("s_q", 1), ("s_k", 1), ("s_v", 1), ("s_qe", 1), ("s_ke", 2), ("s_ve", 1)))
        U1 = 2 * PAIRS
        (s_s1, s_m1, s_e1, s_i1, s_n1, s_t1, s_pt1, s_o1) = (
            Count(n, U1) for n in ("s_s1", "s_m1", "s_e1", "s_i1", "s_n1", "s_t1", "s_pt1", "s_o1"))
        s_h1 = Count("s_h1", PAIRS)
        norms = [{k: Count(f"s_{k}{n}", 1) for k in ("cen", "sq", "var", "ln", "rs", "nx")} for n in range(4)]
        s_b, s_rm, s_ra, s_sc = Count("s_b", 2), Count("s_rm", 4), Count("s_ra", 2), Count("s_sc", 2)
        s_rb, s_rc, s_y, s_h2 = Count("s_rb", 4), Count("s_rc", 2), Count("s_y", 1), Count("s_h2", 1)
        s_q2, s_k2, s_rp, s_rq, s_km = Count("s_q2", 1), Count("s_k2", 1), Count("s_rp", 4), Count("s_rq", 2), Count("s_km", 4)
        s_kd = Count("s_kd", 4)
        s_v2, s_v2e = Count("s_v2", 1), Count("s_v2e", 1)
        KINDS = 3
        U2 = PAIRS * KINDS
        s_qt = Count("s_qt", 1)
        (s_s2, s_m2, s_e2, s_i2, s_n2, s_t2, s_pt2, s_o2) = (
            Count(n, U2) for n in ("s_s2", "s_m2", "s_e2", "s_i2", "s_n2", "s_t2", "s_pt2", "s_o2"))
        s_on, s_at = Count("s_on", PAIRS), Count("s_at", PAIRS)
        s_h3, s_h23 = Count("s_h3", PAIRS), Count("s_h23", 1)
        TOPK = 18
        s_rt, s_tk, s_re, s_wk = Count("s_rt", 1), Count("s_tk", TOPK), Count("s_re", 1), Count("s_wk", 2)
        s_dup, s_xh, s_xl = Count("s_dup", 1), Count("s_xh", 1), Count("s_xl", 1)
        s_wt, s_wh, s_wl = Count("s_wt", 1), Count("s_wh", 1), Count("s_wl", 1)
        N = 2 * CHUNKS * TILES
        s_g, s_u, s_wb, s_sg, s_tg, s_hh, s_yo = (
            Count(n, N // 2) for n in ("s_g", "s_u", "s_wb", "s_sg", "s_tg", "s_hh", "s_yo"))
        s_h4, s_ot, s_oe = Count("s_h4", CHUNKS), Count("s_ot", 1), Count("s_oe", 1)

        def halves(st, k):
            return PS[:, 4 * st + k:4 * st + k + 2, 0:HW]

        def quads(ap):
            return ap.rearrange("q (a i s) -> q a i s", a=2, s=S)

        def psum_quads(st, k):
            return halves(st, k).rearrange("q a (i s) -> q a i s", s=S)

        def first(ap):
            return ap.rearrange("q (i s) -> q i s", s=S)[:, :, 0:QA]

        def pair_up(ap):
            return ap.rearrange("q (a w) -> q a w", a=2)

        def per_token(t):
            return t.unsqueeze(1).unsqueeze(1).broadcast_to([128, 2, 2, S])

        def part(t, a):
            return t[:, a * HW:(a + 1) * HW]

        def last_kind(w):
            return 0 <= w < 2 * U2 and w // 2 % KINDS == KINDS - 1

        def rows(k):
            return min(128, EH - 128 * k)

        RAWV = [(V_BQ, bq), (V_BK, bk), (V_BV, bv), (V_BO, bo), (V_NU, nu_log), (V_TH, theta_log),
                (V_GA, gamma_log), (V_L1, ln1_w), (V_L2, ln2_w)]

        block = ctx.enter_context(nc.Block())

        @block.sync
        def _(sp):
            sp.dma_start(cst[:, :], consts).then_inc(s_cst, 16)
            sp.dma_start(sel_raw, experts).then_inc(s_cst, 16)
            for k, v in RAWV:
                for p in range(2):
                    sp.dma_start(col[64 * p:64 * p + 64, k:k + 1], v.rearrange("(d a) -> d a", a=1)).then_inc(s_col, 16)
            sp.dma_start(cw[:, :], conv_w.rearrange("c a i j -> (c a i j)").partition_broadcast(TC)).then_inc(s_col, 16)
            sp.dma_start(cb[:, :], conv_b.partition_broadcast(TC)).then_inc(s_col, 16)
            sp.wait_ge(s_zero, 1)
            for p in range(2):
                for k, m in ((R_WQ, wq), (R_WK, wk), (R_WO, wo), (R_WV, wv), (R_BRE, B_re), (R_BIM, B_im),
                             (R_CRE, C_re), (R_CIM, C_im), (R_WQ2, wq2)):
                    sp.dma_start(raw[64 * p:64 * p + 64, k, 64 * p:64 * p + 64], m).then_inc(s_raw, 16)
                for h in range(NH):
                    kv = h // (NH // NKV)
                    r = 64 * p + HD * h
                    sp.dma_start(raw[r:r + HD, R_WK2, 64 * p:64 * p + 64], wk2[HD * kv:HD * kv + HD, :]).then_inc(s_raw, 16)
                for kv in range(NKV):
                    r = 64 * p + HP * kv
                    sp.dma_start(raw[r:r + HD, R_WV2, 64 * p:64 * p + 64], wv2[HD * kv:HD * kv + HD, :]).then_inc(s_raw, 16)
                sp.dma_start(raw[NE * p:NE * p + NE, R_RT, 64 * p:64 * p + 64], router_w).then_inc(s_raw, 16)
                for j, k in enumerate((R_WO2, R_WO3)):
                    sp.dma_start(raw[64 * p:64 * p + 64, k, 64 * p:64 * p + 64].rearrange("f (g d) -> f g d", g=NKV)[:, :, 0:HD],
                                 wo2.rearrange("f (g r d) -> f r g d", g=NKV, r=2)[:, j]).then_inc(s_raw, 16)
            full = (TILES - 1) * 128
            for t, m in ((raw1, w1), (raw3, w3)):
                f = m.rearrange("e h c -> (e h) c")
                for r in range(2):
                    sp.dma_start(t[:, 0:TILES - 1, r, :], f[0:full, :].rearrange("(k q) c -> q k c", q=128)).then_inc(s_rex, 16)
                    sp.dma_start(t[0:EH - full, TILES - 1, r, :], f[full:EH, :]).then_inc(s_rex, 16)
            sp.dma_start(raw2.rearrange("f (e h) -> f e h", e=NE), w2.rearrange("e f h -> f e h")).then_inc(s_rex, 16)

            xv = x.rearrange("b a h w -> (b a h w)").rearrange("(n r) -> n r", r=768)
            half_rows = IMAGES // 2 * BANDS
            ov = out.rearrange("b s d -> (b s) d")
            half_tok = IMAGES // 2 * S

            def load(r, st):
                for p in range(2):
                    sp.dma_start(img[st][48 * p:48 * p + 48, :],
                                 xv[bass.ds(r * (2 * PAIRS * BANDS) + st * PAIRS * BANDS + p * half_rows, PAIRS * BANDS), :]
                                 ).then_inc(s_img[st], 16)

            def store(r, st):
                for p in range(2):
                    sp.dma_start(ov[bass.ds(r * (2 * W) + st * W + p * half_tok, W), :].rearrange("(c r) d -> r c d", r=TC),
                                 ot[st][:, :, 64 * p:64 * p + 64]).then_inc(s_out[st], 16)

            for st in range(2):
                load(0, st)
            with sp.Fori(1, ROUNDS) as r:
                for st in range(2):
                    sp.wait_ge(s_cv.sem, s_cv.at(r - 1, 12, st))
                    load(r, st)
                for st in range(2):
                    sp.wait_ge(s_oe.sem, s_oe.at(r - 1, 1, st))
                    store(r - 1, st)
            for st in range(2):
                sp.wait_ge(s_cv.sem, s_cv.at(ROUNDS - 1, 12, st))
                load(ROUNDS - 1, st)
            for st in range(2):
                sp.wait_ge(s_oe.sem, s_oe.at(ROUNDS - 1, 1, st))
                store(ROUNDS - 1, st)
            for st in range(2):
                sp.wait_ge(s_out[st], 32 * ROUNDS + 1)

        @block.gpsimd
        def _(pool):
            nc.gpsimd.memset(raw, 0.0).then_inc(s_zero, 1)
            for st in range(2):
                nc.gpsimd.memset(kbd[st][:, :, :, :], 0.0).then_inc(s_pset, 1)
                nc.gpsimd.memset(wtok[st][:, :, :], 0.0).then_inc(s_pset, 1)
                nc.gpsimd.memset(wrow[st][:, :].bitcast(fp32), 0.0).then_inc(s_pset, 1)
                nc.gpsimd.memset(ot[st][:, :, :], 0.0).then_inc(s_out[st], 1)
            nc.gpsimd.memset(sel[:, :].bitcast(fp32), 0.0).then_inc(s_pset, 1)
            nc.gpsimd.memset(eps[:, 0:1], 1e-5).then_inc(s_pset, 1)
            nc.gpsimd.memset(eps[:, 1:2], 1e-6).then_inc(s_pset, 1)
            with pool.Fori(0, ROUNDS) as r:
                for st in range(2):
                    t = t4[st]
                    pool.wait_ge(s_rm.sem, s_rm.at(r, 2, st))
                    nc.gpsimd.tensor_tensor(zin[st][:, 0], t[:, 0], t[:, 1], ALU.add).then_inc(s_ra.sem, 1)
                    pool.wait_ge(s_rm.sem, s_rm.at(r, 4, st))
                    nc.gpsimd.tensor_tensor(zin[st][:, 1], t[:, 2], t[:, 3], ALU.subtract).then_inc(s_ra.sem, 1)
                for st in range(2):
                    t = t4[st]
                    pool.wait_ge(s_rb.sem, s_rb.at(r, 2, st))
                    nc.gpsimd.tensor_tensor(ab[st][:, 0], t[:, 0], t[:, 1], ALU.subtract).then_inc(s_rc.sem, 1)
                    pool.wait_ge(s_rb.sem, s_rb.at(r, 4, st))
                    nc.gpsimd.tensor_tensor(ab[st][:, 1], t[:, 2], t[:, 3], ALU.add).then_inc(s_rc.sem, 1)
                for n, dst in enumerate((q2, k2)):
                    for st in range(2):
                        t = t4[st]
                        pool.wait_ge(s_rp.sem, r * 8 + 4 * n + 2 * st + 2)
                        nc.gpsimd.tensor_tensor(dst[st][:, :], t[:, 2 * n], t[:, 2 * n + 1], ALU.add).then_inc(s_rq.sem, 1)
                hm = cst[:, C_HM:C_HM + 8].unsqueeze(1).unsqueeze(3).broadcast_to([128, PAIRS, 8, QB])
                for st in range(2):
                    pool.wait_ge(s_rq.sem, r * 4 + 2 + st + 1)
                    q = q2[st][:, :].rearrange("q (i s) -> q i s", s=S)[:, :, QA:].unsqueeze(2).broadcast_to([128, PAIRS, 8, QB])
                    nc.gpsimd.tensor_tensor(qt[st].rearrange("q (i h s) -> q i h s", i=PAIRS, h=8), q, hm, ALU.mult).then_inc(s_qt.sem, 1)
                for st in range(2):
                    pool.wait_ge(s_h3.sem, s_h3.at(r, 2 * PAIRS))
                    nc.gpsimd.tensor_tensor(h2[st][:, :], h2[st][:, :], h3[st][:, :], ALU.add).then_inc(s_h23.sem, 1)

        @block.scalar
        def _(act):
            A = nc.scalar.activation
            chain = [0]

            def link(ins):
                chain[0] += 1
                ins.then_inc(s_ach, 1)
                act.wait_ge(s_ach, chain[0])

            act.wait_ge(s_cst, 32)
            act.wait_ge(s_pset, 9)
            A(ident_b[:, :], ident, ACT.Copy).then_inc(s_aset, 1)
            A(neg_b[:, :], cst[:, C_NEG:C_NEG + S], ACT.Copy).then_inc(s_aset, 1)
            A(sel[0:40, :], sel_raw, ACT.Copy).then_inc(s_aset, 1)
            act.wait_ge(s_col, 20 * 16)
            link(A(tmp[:, 0:1], col[:, V_NU:V_NU + 1], ACT.Exp))
            A(lam[:, :], tmp[:, 0:1], ACT.Exp, scale=-1.0).then_inc(s_lin, 1)
            A(tmp[:, 1:2], col[:, V_TH:V_TH + 1], ACT.Exp).then_inc(s_lin, 1)
            A(gam[:, :], col[:, V_GA:V_GA + 1], ACT.Exp).then_inc(s_gam, 1)
            act.wait_ge(s_ang, 1)
            A(ang[:, 6:7], ang[:, 4:5], ACT.Sin).then_inc(s_sin, 1)
            A(ang[:, 7:8], ang[:, 5:6], ACT.Sin).then_inc(s_sin, 1)

            def tap0(r, k):
                st, c = k // CH, k % CH
                if c == 0:
                    act.wait_ge(s_img[st], r * 32 + 32)
                A(y[st][:, c, :].rearrange("q (i j) -> q i j", i=4),
                  img[st][:, :].rearrange("q (i a j b) -> q i a j b", i=4, a=2, b=2)[:, :, 0, :, 0], ACT.Identity,
                  bias=cb[:, c:c + 1], scale=cw[:, 4 * c:4 * c + 1]).then_inc(s_cv0.sem, 1)

            for k in range(2 * CH):
                tap0(0, k)

            with act.Fori(0, ROUNDS) as r:
                nc.scalar.preload_act_table_set("natural_log_exp_and_others")
                for st in range(2):
                    for c in range(CH):
                        act.wait_ge(s_ft.sem, s_ft.at(r, 1 + c // 2, st))
                        src = PS[:, 4 * st + c // 2, (c % 2) * 144:(c % 2) * 144 + 144].rearrange("q (k i b) -> q k i b", k=3, i=PAIRS)
                        dst = xf[st].rearrange("q (i c b k) -> q c k i b", i=PAIRS, c=CH, k=3)[:, c]
                        A(dst, src, ACT.Copy).then_inc(s_xe.sem, 1)
                for st in range(2):
                    act.wait_ge(s_q.sem, s_q.at(r, 1, st))
                    A(pair_up(qf[st]), halves(st, 2), ACT.Identity, bias=bq8[:, 0:1], scale=D ** -0.5).then_inc(s_qe.sem, 1)
                for st in range(2):
                    act.wait_ge(s_v.sem, s_v.at(r, 1, st))
                    A(vt[st][0:HS, :, :].rearrange("q (a i) e -> q a (i e)", a=2), PS[0:HS, 4 * st + 2:4 * st + 4, :],
                      ACT.Copy).then_inc(s_ve.sem, 1)

                def attn1_exp(w):
                    st, u = w % 2, w // 2
                    b, p, e = PS[0:HS, 4 * st + u % 2], pw[st][u % 2], ex[st][0:HS, u % 2]
                    act.wait_ge(s_m1.sem, s_m1.at(r, w + 1))
                    if w >= 4:
                        act.wait_ge(s_t1.sem, s_t1.at(r, w - 3))
                        act.wait_ge(s_i1.sem, s_i1.at(r, w - 3))
                    for p_ in range(2):
                        t = slice(p_ * S, (p_ + 1) * S)
                        last = A(p[0:HS, t], b[:, t], ACT.Exp, bias=e[:, 0, p_:p_ + 1], accum_out=e[:, 1, p_:p_ + 1])
                    last.then_inc(s_e1.sem, 1)

                def attn1_out(w):
                    st = w % 2
                    act.wait_ge(s_t1.sem, s_t1.at(r, w + 1))
                    if w >= 2:
                        act.wait_ge(s_o1.sem, s_o1.at(r, w - 1))
                    A(pt[st][0:HS, 0:2 * S], PS[0:HS, 4 * st + 2, 0:2 * S], ACT.Copy).then_inc(s_pt1.sem, 1)

                for w in range(2 * U1):
                    attn1_exp(w)
                    if w >= 2:
                        attn1_out(w - 2)
                attn1_out(2 * U1 - 2)
                attn1_out(2 * U1 - 1)

                def norm(n, e):
                    s = norms[n]
                    before = {0: s["cen"], 1: s["cen"], 2: norms[1]["nx"], 3: s_h3}[n]
                    for st in range(2):
                        if n == 3:
                            act.wait_ge(s_h3.sem, s_h3.at(r, 2 * PAIRS - 1 + st))
                        else:
                            act.wait_ge(before.sem, before.at(r, 1, st))
                        if n < 2:
                            A(pair_up(sq[st]), halves(st, 0), ACT.Square).then_inc(s["sq"].sem, 1)
                        else:
                            A(sq[st], (xl if n == 2 else h3)[st][:, :], ACT.Square).then_inc(s["sq"].sem, 1)
                    for st in range(2):
                        act.wait_ge(s["var"].sem, s["var"].at(r, 1, st))
                        A(pair_up(rstd[st]), halves(st, 2), ACT.Ln, bias=eps[:, e:e + 1]).then_inc(s["ln"].sem, 1)
                        act.wait_ge(s["ln"].sem, s["ln"].at(r, 1, st))
                        A(rstd[st], rstd[st], ACT.Exp, scale=-0.5).then_inc(s["rs"].sem, 1)

                norm(0, 0)
                norm(1, 0)
                norm(2, 1)
                for st in range(2):
                    act.wait_ge(s_v2.sem, s_v2.at(r, 1, st))
                    A(vt[st][:, 0:PAIRS, :].rearrange("q i e -> q (i e)"), PS[:, 4 * st, :], ACT.Copy)
                    A(vt[st][0:QB, PAIRS:, :].rearrange("q i e -> q (i e)"), PS[0:QB, 4 * st + 1, :],
                      ACT.Copy).then_inc(s_v2e.sem, 1)
                for hf in range(2):
                    for st in range(2):
                        act.wait_ge(s_rq.sem, r * 4 + 2 + st + 1)
                        for h in (NH * hf, NH * hf + 1):
                            A(first(km[st][:, h]), first(k2[st][:, :]), ACT.Copy, scale=cst[:, C_HM + h:C_HM + h + 1]).then_inc(s_km.sem, 1)

                def attn2_exp(w):
                    st, u = w % 2, w // 2
                    b, p, e = PS[:, 4 * st + u % 2], pw[st][u % 2], ex[st][:, u % 2]
                    act.wait_ge(s_m2.sem, s_m2.at(r, w + 1))
                    if w >= 4:
                        act.wait_ge(s_t2.sem, s_t2.at(r, w - 3))
                        act.wait_ge(s_i2.sem, s_i2.at(r, w - 3))
                    if u % KINDS < 2:
                        for h in range(NH):
                            t = slice(h * QA, (h + 1) * QA)
                            last = A(p[:, t], b[:, t], ACT.Exp, bias=e[:, 0, h:h + 1], accum_out=e[:, 1, h:h + 1])
                    else:
                        last = A(p[:, 0:S], b[:, 0:S], ACT.Exp, bias=e[:, 0, 0:1], accum_out=e[:, 1, 0:1])
                    last.then_inc(s_e2.sem, 1)

                def attn2_out(w):
                    st, u = w % 2, w // 2
                    act.wait_ge(s_t2.sem, s_t2.at(r, w + 1))
                    if w >= 2:
                        act.wait_ge(s_o2.sem, s_o2.at(r, w - 1))
                    b = PS[:, 4 * st + 2]
                    if u % KINDS < 2:
                        A(pt[st][:, :], b, ACT.Copy).then_inc(s_pt2.sem, 1)
                    else:
                        A(pt[st][:, 0:QA], b[:, 0:QA], ACT.Copy)
                        A(pt[st][0:QB, QA:2 * QA], b[0:QB, QA:2 * QA], ACT.Copy).then_inc(s_pt2.sem, 1)

                for w in range(2 * U2):
                    attn2_exp(w)
                    if w >= 2:
                        attn2_out(w - 2)
                attn2_out(2 * U2 - 2)
                attn2_out(2 * U2 - 1)
                norm(3, 1)
                for st in range(2):
                    act.wait_ge(s_tk.sem, s_tk.at(r, 2, st))
                    A(re[st][:, :, :], rl[st][:, :, :], ACT.Exp).then_inc(s_re.sem, 1)
                    act.wait_ge(s_dup.sem, s_dup.at(r, 1, st))
                    A(xs[st][:, :].rearrange("q (c w) -> q c w", c=CHUNKS), PS[:, 4 * st + 1:4 * st + 4, 0:CW],
                      ACT.Copy).then_inc(s_xh.sem, 1)
                for st in range(2):
                    act.wait_ge(s_wt.sem, s_wt.at(r, 1, st))
                    A(wrow[st][0:40, :].rearrange("q (c w) -> q c w", c=CHUNKS), PS[0:40, 4 * st + 1:4 * st + 4, 0:CW],
                      ACT.Copy).then_inc(s_wh.sem, 1)
                for n in range(N):
                    m = rows(n % TILES)
                    act.wait_ge(s_g.sem, s_g.at(r, n + 1))
                    if n >= 2:
                        act.wait_ge(s_tg.sem, s_tg.at(r, n - 1))
                    A(sg[0:m, n % 2], PS[0:m, n % 2, 0:CW], ACT.Silu).then_inc(s_sg.sem, 1)
                    if 2 <= n < 2 + 2 * CH:
                        tap0(r + 1, n - 2)
                for st in range(2):
                    act.wait_ge(s_ot.sem, s_ot.at(r, 1, st))
                    act.wait_ge(s_out[st], r * 32 + 1)
                    A(ot[st][:, :, :].rearrange("q (a c) e -> q a (c e)", a=2), PS[0:TC, 2 * st:2 * st + 2, 0:CW],
                      ACT.Copy).then_inc(s_oe.sem, 1)

        @block.vector
        def _(dve):
            V = nc.vector
            chain = [0]

            def link(ins):
                chain[0] += 1
                ins.then_inc(s_dch, 1)
                dve.wait_ge(s_dch, chain[0])

            dve.wait_ge(s_col, 20 * 16)
            dve.wait_ge(s_raw, 36 * 16)
            dve.wait_ge(s_gam, 1)
            for k in (R_BRE, R_BIM):
                V.tensor_scalar(raw[:, k, :], raw[:, k, :], gam[:, 0:1], None, ALU.mult).then_inc(s_gam, 1)
            dve.wait_ge(s_lin, 2)
            link(V.tensor_copy(ang[:, 0:1], tmp[:, 1:2]))
            link(V.tensor_scalar_add(ang[:, 1:2], ang[:, 0:1], PI / 2))
            link(V.tensor_scalar(ang[:, 2:4], ang[:, 0:2], 1 / (2 * PI), 12582912.0, ALU.mult, ALU.add))
            link(V.tensor_scalar_add(ang[:, 2:4], ang[:, 2:4], -12582912.0))
            hi = 6.28125
            link(V.scalar_tensor_tensor(out=ang[:, 4:6], in0=ang[:, 2:4], scalar=-hi, in1=ang[:, 0:2], op0=ALU.mult, op1=ALU.add))
            link(V.scalar_tensor_tensor(out=ang[:, 4:6], in0=ang[:, 2:4], scalar=-(2 * PI - hi), in1=ang[:, 4:6], op0=ALU.mult, op1=ALU.add))
            pi32 = 3.1415925
            V.tensor_scalar(ang[:, 4:6], ang[:, 4:6], pi32, -pi32, ALU.min, ALU.max).then_inc(s_ang, 1)
            link(V.memset(rot_cos[:, 0:1], 1.0))
            link(V.memset(rot_sin[:, 0:1], 0.0))
            dve.wait_ge(s_sin, 2)
            link(V.tensor_copy(rot_sin[:, 1:2], ang[:, 6:7]))
            link(V.tensor_copy(rot_cos[:, 1:2], ang[:, 7:8]))
            m = 1
            while m < S - 1:
                n = min(m, S - 1 - m)
                c, s = rot_cos[:, m:m + 1], rot_sin[:, m:m + 1]
                a, b = slice(1, 1 + n), slice(m + 1, m + 1 + n)
                link(V.tensor_scalar(rot_t[:, a], rot_sin[:, a], s, None, ALU.mult))
                link(V.scalar_tensor_tensor(out=rot_cos[:, b], in0=rot_cos[:, a], scalar=c, in1=rot_t[:, a], op0=ALU.mult, op1=ALU.subtract))
                link(V.tensor_scalar(rot_t[:, a], rot_cos[:, a], s, None, ALU.mult))
                link(V.scalar_tensor_tensor(out=rot_sin[:, b], in0=rot_sin[:, a], scalar=c, in1=rot_t[:, a], op0=ALU.mult, op1=ALU.add))
                m *= 2
            link(V.memset(decay[:, :], 1.0))
            link(V.tensor_scalar(decay[:, :], decay[:, :], lam[:, 0:1], None, ALU.mult))
            link(V.memset(decay[:, :].rearrange("q (i s) -> q i s", s=S)[:, :, 0:1], 0.0))
            V.tensor_scalar(bq8[:, :], col[:, V_BQ:V_BQ + 1], D ** -0.5, None, ALU.mult).then_inc(s_dset, 1)
            for k in range(3):
                dve.wait_ge(s_tr, k + 1)
                V.tensor_copy(wt[:, 4 * k:4 * k + 4, :].rearrange("q a b -> q (a b)"), PS[:, k, :]).then_inc(s_ev, 1)
            dve.wait_ge(s_ev, 3)
            for k in (R_WQ2, R_WK2, R_WV2):
                link(V.tensor_scalar(wt[:, k, :], wt[:, k, :], col[:, V_L1:V_L1 + 1], None, ALU.mult))
            link(V.tensor_scalar(wt[:, R_RT, :], wt[:, R_RT, :], col[:, V_L2:V_L2 + 1], None, ALU.mult))
            link(V.tensor_scalar(wt[:, R_CIM, :], wt[:, R_CIM, :], -1.0, None, ALU.mult))
            for k, dst in ((R_WQ2, q_rot), (R_WK2, k_rot)):
                a = wt[:, k, :].rearrange("q (h r j) -> q h r j", r=2, j=HD // 2)
                b = dst[:, :].rearrange("q (h r j) -> q h r j", r=2, j=HD // 2)
                V.tensor_scalar(b[:, :, 0], a[:, :, 1], -1.0, None, ALU.mult).then_inc(s_dset, 1)
                V.tensor_copy(b[:, :, 1], a[:, :, 0]).then_inc(s_dset, 1)
            for j, (wh, wl) in enumerate(((w1h, w1l), (w3h, w3l))):
                for k in range(3):
                    lo, hi_ = 512 * k, min(512 * (k + 1), EH)
                    n = 3 * j + k
                    w = w_full[:, n % 2, 0:hi_ - lo]
                    dve.wait_ge(s_tr, 4 + n)
                    link(V.tensor_scalar(w, PS[:, (3 + n) % 8, 0:hi_ - lo], col[:, V_L2:V_L2 + 1], None, ALU.mult))
                    link(V.tensor_copy(wh[:, lo:hi_], w))
                    V.tensor_tensor(wl[:, lo:hi_], w, wh[:, lo:hi_].bitcast(fp32), ALU.subtract).then_inc(s_ev, 1)
            for k, (b, t0, t1) in enumerate(((1, 0, 8), (2, 8, TILES))):
                dve.wait_ge(s_tr, 10 + k)
                full = t1 if t1 < TILES else TILES - 1
                V.tensor_copy(w2t[:, t0:full, :].rearrange("q a b -> q (a b)"), PS[:, b, 0:D * (full - t0)]).then_inc(s_dset, 1)
                if full < t1:
                    m = rows(full)
                    V.tensor_copy(w2t[0:m, full, :], PS[0:m, b, D * (full - t0):D * (full - t0 + 1)]).then_inc(s_dset, 1)
            dve.wait_ge(s_tr, 12)
            V.tensor_copy(wvo[:, :], PS[:, 3, 0:128]).then_inc(s_dset, 1)
            V.tensor_copy(wt[:, R_WO3, :], PS[:, 3, 256:384]).then_inc(s_dset, 1)
            V.tensor_scalar(bvo[:, :], PS[:, 3, 128:129], col[:, V_BO:V_BO + 1], None, ALU.add).then_inc(s_dset, 1)

            def tap(r, k):
                st, t, c = k // (3 * CH), 1 + k % (3 * CH) // CH, k % CH
                if t == 1:
                    dve.wait_ge(s_cv0.sem, s_cv0.at(r, c + 1, st))
                else:
                    dve.wait_ge(s_cv.sem, s_cv.at(r, CH * (t - 2) + c + 1, st))
                iv = img[st][:, :].rearrange("q (i a j b) -> q i a j b", i=4, a=2, b=2)
                yc = y[st][:, c, :].rearrange("q (i j) -> q i j", i=4)
                V.scalar_tensor_tensor(out=yc, in0=iv[:, :, t // 2, :, t % 2], scalar=cw[:, 4 * c + t:4 * c + t + 1],
                                       in1=yc, op0=ALU.mult, op1=ALU.add).then_inc(s_cv.sem, 1)

            for k in range(6 * CH):
                tap(0, k)

            with dve.Fori(0, ROUNDS) as r:
                for st in range(2):
                    dve.wait_ge(s_k.sem, s_k.at(r, 1, st))
                    for p in range(2):
                        q = slice(64 * p, 64 * p + 64)
                        V.tensor_scalar(kbd[st][q, :, p, :].rearrange("q (a i) s -> q a i s", a=2), psum_quads(st, 0)[q],
                                        col[q, V_BK:V_BK + 1], None, ALU.add).then_inc(s_ke.sem, 1)

                def attn1_max(w):
                    st, u = w % 2, w // 2
                    dve.wait_ge(s_s1.sem, s_s1.at(r, w + 1))
                    if w >= 4:
                        dve.wait_ge(s_e1.sem, s_e1.at(r, w - 3))
                    V.tensor_reduce(ex[st][0:HS, u % 2, 0, 0:2], PS[0:HS, 4 * st + u % 2, 0:2 * S].rearrange("q (p t) -> q p t", p=2),
                                    AX.X, ALU.max, negate=True).then_inc(s_m1.sem, 1)

                def attn1_weights(w):
                    st, u = w % 2, w // 2
                    e = ex[st][0:HS, u % 2]
                    v = pw[st][u % 2][0:HS, 0:2 * S].rearrange("q (p t) -> q p t", p=2)
                    dve.wait_ge(s_e1.sem, s_e1.at(r, w + 1))
                    V.reciprocal(e[:, 2, 0:2], e[:, 1, 0:2]).then_inc(s_i1.sem, 1)
                    dve.wait_ge(s_i1.sem, s_i1.at(r, w + 1))
                    V.tensor_tensor(v, v, e[:, 2, 0:2].unsqueeze(2).broadcast_to([HS, 2, S]), ALU.mult).then_inc(s_n1.sem, 1)

                def attn1_close(w):
                    st, i = w % 2, w // 4
                    dve.wait_ge(s_o1.sem, s_o1.at(r, w + 1))
                    V.tensor_scalar(h1[st][:, i * S:(i + 1) * S], PS[:, 4 * st + 3, 0:S], bvo[:, 0:1], None, ALU.add).then_inc(s_h1.sem, 1)

                attn1_max(0)
                attn1_max(1)
                for w in range(2 * U1 + 2):
                    if w < 2 * U1:
                        attn1_weights(w)
                    if w >= 2 and (w - 2) // 2 % 2:
                        attn1_close(w - 2)
                    if w + 2 < 2 * U1:
                        attn1_max(w + 2)

                def scale(n, dst):
                    s = norms[n]
                    for st in range(2):
                        dve.wait_ge(s["rs"].sem, s["rs"].at(r, 1, st))
                        src = halves(st, 0) if n < 2 else pair_up((xl if n == 2 else h3)[st][:, :])
                        V.tensor_tensor(pair_up(dst[st]), src, pair_up(rstd[st]), ALU.mult).then_inc(s["nx"].sem, 1)

                scale(0, xn)
                for st in range(2):
                    dve.wait_ge(s_b.sem, s_b.at(r, 2, st))
                    re_in, im_in = psum_quads(st, 0), psum_quads(st, 2)
                    for k, (v, c) in enumerate(((re_in, rot_cos), (im_in, rot_sin), (im_in, rot_cos), (re_in, rot_sin))):
                        V.tensor_tensor(quads(t4[st][:, k]), v, per_token(c[:, :]), ALU.mult).then_inc(s_rm.sem, 1)
                for st in range(2):
                    for k in range(2):
                        dve.wait_ge(s_ra.sem, s_ra.at(r, k + 1, st))
                        V.tensor_tensor_scan(z[st][:, k], decay[:, :], zin[st][:, k], 0.0, ALU.mult, ALU.add).then_inc(s_sc.sem, 1)
                    for k, (j, c) in enumerate(((0, rot_cos), (1, rot_sin), (0, rot_sin), (1, rot_cos))):
                        dve.wait_ge(s_sc.sem, s_sc.at(r, 2, st))
                        V.tensor_tensor(quads(t4[st][:, k]), quads(z[st][:, j]), per_token(c[:, :]), ALU.mult).then_inc(s_rb.sem, 1)
                for st in range(2):
                    dve.wait_ge(s_y.sem, s_y.at(r, 1, st))
                    V.tensor_tensor(pair_up(h2[st][:, :]), pair_up(h1[st][:, :]), halves(st, 0), ALU.add).then_inc(s_h2.sem, 1)
                scale(1, [t[:, :] for t in xl])
                scale(2, xr)
                for n, s in enumerate((s_q2, s_k2)):
                    for st in range(2):
                        dve.wait_ge(s.sem, s.at(r, 1, st))
                        for j, c in enumerate((rope_cos, rope_sin)):
                            V.tensor_tensor(quads(t4[st][:, 2 * n + j]), psum_quads(st, 2 * j), per_token(c), ALU.mult).then_inc(s_rp.sem, 1)

                for hf in range(2):
                    for st in range(2):
                        dve.wait_ge(s_rq.sem, r * 4 + 2 + st + 1)
                        for h in (NH * hf + 2, NH * hf + 3):
                            V.tensor_scalar(first(km[st][:, h]), first(k2[st][:, :]), cst[:, C_HM + h:C_HM + h + 1], None,
                                            ALU.mult).then_inc(s_kd.sem, 1)

                def attn2_max(w):
                    st, u = w % 2, w // 2
                    b, e = PS[:, 4 * st + u % 2], ex[st][:, u % 2]
                    dve.wait_ge(s_s2.sem, s_s2.at(r, w + 1))
                    if w >= 4:
                        dve.wait_ge(s_e2.sem, s_e2.at(r, w - 3))
                    if u % KINDS < 2:
                        V.tensor_reduce(e[:, 0, :], b.rearrange("q (h t) -> q h t", h=NH), AX.X, ALU.max, negate=True).then_inc(s_m2.sem, 1)
                    else:
                        V.tensor_reduce(e[:, 0, 0:1], b[:, 0:S], AX.X, ALU.max, negate=True).then_inc(s_m2.sem, 1)

                def attn2_weights(w):
                    st, u = w % 2, w // 2
                    p, e = pw[st][u % 2], ex[st][:, u % 2]
                    n = NH if u % KINDS < 2 else 1
                    dve.wait_ge(s_e2.sem, s_e2.at(r, w + 1))
                    V.reciprocal(e[:, 2, 0:n], e[:, 1, 0:n]).then_inc(s_i2.sem, 1)
                    dve.wait_ge(s_i2.sem, s_i2.at(r, w + 1))
                    if n > 1:
                        v = p.rearrange("q (h t) -> q h t", h=NH)
                        V.tensor_tensor(v, v, e[:, 2, :].unsqueeze(2).broadcast_to([128, NH, QA]), ALU.mult).then_inc(s_n2.sem, 1)
                    else:
                        V.tensor_scalar(p[:, 0:S], p[:, 0:S], e[:, 2, 0:1], None, ALU.mult).then_inc(s_n2.sem, 1)

                def attn2_values(w):
                    st, i = w % 2, w // 2 // KINDS
                    n = 2 * i + st
                    dve.wait_ge(s_o2.sem, s_o2.at(r, w + 1))
                    if i >= 1:
                        dve.wait_ge(s_at.sem, s_at.at(r, n - 1))
                    V.tensor_copy(on[st], PS[:, 4 * st + 3, 0:2 * S]).then_inc(s_on.sem, 1)

                def residual(w):
                    st, i = w % 2, w // 2 // KINDS
                    dve.wait_ge(s_at.sem, s_at.at(r, 2 * i + st + 1))
                    t = slice(i * S, (i + 1) * S)
                    V.tensor_tensor(h3[st][:, t], xl[st][:, t], PS[:, 4 * st + 3, 2 * S:3 * S], ALU.add).then_inc(s_h3.sem, 1)

                attn2_max(0)
                attn2_max(1)
                for w in range(2 * U2 + 3):
                    if w < 2 * U2:
                        attn2_weights(w)
                    if last_kind(w - 3):
                        residual(w - 3)
                    if w + 2 < 2 * U2:
                        attn2_max(w + 2)
                    if last_kind(w - 2):
                        attn2_values(w - 2)
                scale(3, flat)

                full = [TC, NT, NE]
                pri = cst[0:TC, C_PRI:C_PRI + NE].unsqueeze(1).broadcast_to(full)

                def route(st):
                    def wide(k):
                        return rm[st][:, k, :].unsqueeze(2).broadcast_to(full)

                    step = [0]

                    def then(ins, wait=True):
                        step[0] += 1
                        ins.then_inc(s_tk.sem, 1)
                        if wait:
                            dve.wait_ge(s_tk.sem, s_tk.at(r, step[0], st))

                    l, e, k, m = rl[st][:, :, :], re[st][:, :, :], rk[st][:, :, :], rm[st]
                    first, second, rest = rs1[st][:, :, :], rs2[st][:, :, :], rt[st][:, :, :]
                    dve.wait_ge(s_rt.sem, s_rt.at(r, 1, st))
                    logits = PS[0:TC, 4 * st, 0:NT * NE].rearrange("q (n e) -> q n e", e=NE)
                    then(V.tensor_reduce(m[:, 0, :], logits, AX.X, ALU.max))
                    then(V.tensor_tensor(l, logits, wide(0), ALU.subtract))
                    then(V.tensor_scalar(k, l, 0.0, None, ALU.is_ge))
                    then(V.tensor_tensor(k, k, pri, ALU.mult))
                    then(V.tensor_reduce(m[:, 1, :], k, AX.X, ALU.max))
                    then(V.tensor_tensor(first, k, wide(1), ALU.is_equal))
                    then(V.scalar_tensor_tensor(out=rest, in0=first, scalar=-1e30, in1=l, op0=ALU.mult, op1=ALU.add))
                    then(V.tensor_reduce(m[:, 2, :], rest, AX.X, ALU.max))
                    then(V.tensor_tensor(k, rest, wide(2), ALU.is_equal))
                    then(V.tensor_tensor(k, k, pri, ALU.mult))
                    then(V.tensor_reduce(m[:, 3, :], k, AX.X, ALU.max))
                    then(V.tensor_tensor(second, k, wide(3), ALU.is_equal))
                    then(V.tensor_tensor(first, first, second, ALU.add))
                    dve.wait_ge(s_re.sem, s_re.at(r, 1, st))
                    then(V.tensor_tensor(rest, e, first, ALU.mult), wait=False)
                    then(V.tensor_reduce(m[:, 4, :], e, AX.X, ALU.add))
                    then(V.tensor_reduce(m[:, 5, :], rest, AX.X, ALU.add))
                    then(V.scalar_tensor_tensor(out=m[:, 5, :], in0=m[:, 4, :], scalar=1e-9, in1=m[:, 5, :], op0=ALU.mult, op1=ALU.add))
                    then(V.reciprocal(m[:, 5, :], m[:, 5, :]))
                    assert step[0] == TOPK
                    for j in range(2):
                        V.tensor_tensor(wtok[st][:, :, 32 * j:32 * j + NE], rest, wide(5), ALU.mult).then_inc(s_wk.sem, 1)

                for st in range(2):
                    route(st)
                    dve.wait_ge(s_xh.sem, s_xh.at(r, 1, st))
                    low = xs[st][64:128, :].rearrange("q (c w) -> q c w", c=CHUNKS)
                    V.tensor_tensor(low, PS[64:128, 4 * st + 1:4 * st + 4, 0:CW], low.bitcast(fp32), ALU.subtract).then_inc(s_xl.sem, 1)
                for st in range(2):
                    dve.wait_ge(s_wh.sem, s_wh.at(r, 1, st))
                    low = wrow[st][32:40, :].rearrange("q (c w) -> q c w", c=CHUNKS)
                    V.tensor_tensor(low, PS[32:40, 4 * st + 1:4 * st + 4, 0:CW], low.bitcast(fp32), ALU.subtract).then_inc(s_wl.sem, 1)

                def finish(c):
                    st, q = c // CHUNKS, c % CHUNKS
                    t = slice(q * QW, (q + 1) * QW)
                    dve.wait_ge(s_yo.sem, s_yo.at(r, TILES * (c + 1)))
                    if c == 0:
                        dve.wait_ge(s_h23.sem, s_h23.at(r, 2))
                    V.tensor_tensor(h2[st][:, t], h2[st][:, t], PS[:, 6 + c % 2, 0:QW], ALU.add).then_inc(s_h4.sem, 1)

                for n in range(N):
                    m = rows(n % TILES)
                    dve.wait_ge(s_sg.sem, s_sg.at(r, n + 1))
                    dve.wait_ge(s_u.sem, s_u.at(r, n + 1))
                    if n >= 2:
                        dve.wait_ge(s_hh.sem, s_hh.at(r, n - 1))
                    V.tensor_tensor(tg[0:m, n % 2], sg[0:m, n % 2], PS[0:m, 2 + n % 2, 0:CW], ALU.mult).then_inc(s_tg.sem, 1)
                    dve.wait_ge(s_tg.sem, s_tg.at(r, n + 1))
                    dve.wait_ge(s_wb.sem, s_wb.at(r, n + 1))
                    if n >= 3:
                        dve.wait_ge(s_yo.sem, s_yo.at(r, n - 2))
                    V.tensor_tensor(hh[0:m, n % 3], tg[0:m, n % 2], PS[0:m, 4 + n % 2, 0:CW], ALU.mult).then_inc(s_hh.sem, 1)
                    if n % TILES == 3 and n > TILES:
                        finish(n // TILES - 1)
                    if n % 2 and 5 <= n < 5 + 12 * CH:
                        tap(r + 1, (n - 5) // 2)
                finish(2 * CHUNKS - 1)

        @block.tensor
        def _(pe):
            mm = nc.tensor.matmul
            pe.wait_ge(s_cst, 32)
            pe.wait_ge(s_raw, 36 * 16)
            pe.wait_ge(s_gam, 3)
            for k in range(12):
                last = nc.tensor.transpose(PS[:, k // 4, (k % 4) * 128:(k % 4 + 1) * 128], raw[:, k, :], ident)
                if k % 4 == 3:
                    last.then_inc(s_tr, 1)
            pe.wait_ge(s_rex, 9 * 16)
            for j, src in enumerate((raw1, raw3)):
                for k in range(TILES):
                    n = 3 * j + k // 4
                    if k % 4 == 0 and 3 + n >= 8:
                        pe.wait_ge(s_ev, 1)
                    m = rows(k)
                    last = nc.tensor.transpose(PS[:, (3 + n) % 8, (k % 4) * 128:(k % 4) * 128 + m],
                                               src[0:m, k].rearrange("q r c -> q (r c)"), ident[0:m, 0:m])
                    if k % 4 == 3 or k == TILES - 1:
                        last.then_inc(s_tr, 1)
            pe.wait_ge(s_ev, 3)
            for k in range(TILES):
                m = rows(k)
                last = nc.tensor.transpose(PS[0:m, 1 + k // 8, (k % 8) * D:(k % 8 + 1) * D], raw2[:, 128 * k:128 * k + m],
                                           ident[0:D, 0:D])
                if k in (7, TILES - 1):
                    last.then_inc(s_tr, 1)
            pe.wait_ge(s_ev, 4)
            nc.tensor.transpose(PS[:, 3, 256:384], raw[:, R_WO3, :], ident)
            mm(PS[:, 3, 0:128], raw[:, R_WV, :], wt[:, R_WO, :], start=True, stop=True)
            mm(PS[:, 3, 128:129], wt[:, R_WO, :], col[:, V_BV:V_BV + 1], start=True, stop=True).then_inc(s_tr, 1)
            pe.wait_ge(s_dset, 11)
            pe.wait_ge(s_aset, 3)
            pe.wait_ge(s_pset, 9)
            pe.wait_ge(s_ev, 9)

            def product(st, k, w, src, sem):
                for a in range(2):
                    last = mm(PS[:, 4 * st + k + a, 0:HW], w, part(src, a), start=True, stop=True)
                if sem is not None:
                    last.then_inc(sem.sem, 1)

            with pe.Fori(0, ROUNDS) as r:
                for st in range(2):
                    pe.wait_ge(s_cv.sem, s_cv.at(r, 12, st))
                    for c in range(CH):
                        for k in range(3):
                            for p in range(2):
                                o = (c % 2) * 144 + k * 48
                                last = mm(PS[64 * p:64 * p + 64, 4 * st + c // 2, o:o + 48], y[st][:, c, 64 * k:64 * k + 64],
                                          ident[0:TC, 48 * p:48 * p + 48], start=True, stop=True)
                        if c % 2:
                            last.then_inc(s_ft.sem, 1)
                for st in range(2):
                    pe.wait_ge(s_xe.sem, s_xe.at(r, 4, st))
                    product(st, 2, wt[:, R_WQ, :], xf[st], s_q)
                    product(st, 0, wt[:, R_WK, :], xf[st], s_k)
                for st in range(2):
                    pe.wait_ge(s_qe.sem, s_qe.at(r, 1, st))
                    for n in range(2 * PAIRS):
                        last = mm(PS[0:HS, 4 * st + 2 + n // 4, (n % 4) * 128:(n % 4 + 1) * 128], xf[st][:, n * HS:(n + 1) * HS],
                                  wvo[:, :], start=True, stop=True)
                    last.then_inc(s_v.sem, 1)

                def score1(w):
                    st, u = w % 2, w // 2
                    if u == 0:
                        pe.wait_ge(s_ke.sem, s_ke.at(r, 2, st))
                    if u >= 2:
                        pe.wait_ge(s_e1.sem, s_e1.at(r, w - 3))
                    mm(PS[0:HS, 4 * st + u % 2, 0:2 * S], qf[st][:, u * HS:(u + 1) * HS],
                       kbd[st][:, u // 2].rearrange("q p t -> q (p t)"), start=True, stop=True).then_inc(s_s1.sem, 1)

                def turn1(w):
                    st, u = w % 2, w // 2
                    if u == 0:
                        pe.wait_ge(s_ve.sem, s_ve.at(r, 1, st))
                    pe.wait_ge(s_n1.sem, s_n1.at(r, w + 1))
                    if w >= 2:
                        pe.wait_ge(s_pt1.sem, s_pt1.at(r, w - 1))
                    for k in range(4):
                        last = nc.tensor.transpose(PS[0:HS, 4 * st + 2, k * HS:(k + 1) * HS],
                                                   pw[st][u % 2][0:HS, k * HS:(k + 1) * HS], ident[0:HS, 0:HS])
                    last.then_inc(s_t1.sem, 1)

                def value1(w):
                    st, u = w % 2, w // 2
                    i, j = u // 2, u % 2
                    pe.wait_ge(s_pt1.sem, s_pt1.at(r, w + 1))
                    if j == 0 and i >= 1:
                        pe.wait_ge(s_h1.sem, s_h1.at(r, 2 * (i - 1) + st + 1))
                    for th in range(2):
                        for p in range(2):
                            k = 2 * p + th
                            last = mm(PS[64 * p:64 * p + 64, 4 * st + 3, j * HS:(j + 1) * HS], vt[st][0:HS, 2 * i + th, 64 * p:64 * p + 64],
                                      pt[st][0:HS, k * HS:(k + 1) * HS], start=(th == 0), stop=(th == 1))
                    last.then_inc(s_o1.sem, 1)

                for w in range(4):
                    score1(w)
                for w in range(2 * U1 + 1):
                    if w < 2 * U1:
                        turn1(w)
                    if w + 4 < 2 * U1:
                        score1(w + 4)
                    if w >= 1:
                        value1(w - 1)

                def centred(n, src, ready):
                    for st in range(2):
                        pe.wait_ge(ready.sem, ready.at(r, 2 * PAIRS - 1 + st) if n == 0 else ready.at(r, 1, st))
                        product(st, 0, centre, src[st][:, :], norms[n]["cen"])

                def var(n):
                    s = norms[n]
                    for st in range(2):
                        pe.wait_ge(s["sq"].sem, s["sq"].at(r, 1, st))
                        product(st, 2, avg, sq[st], s["var"])

                centred(0, h1, s_h1)
                var(0)
                for st in range(2):
                    pe.wait_ge(norms[0]["nx"].sem, norms[0]["nx"].at(r, 1, st))
                    product(st, 0, wt[:, R_BRE, :], xn[st], s_b)
                    product(st, 2, wt[:, R_BIM, :], xn[st], s_b)
                for st in range(2):
                    pe.wait_ge(s_rc.sem, s_rc.at(r, 2, st))
                    for a in range(2):
                        mm(PS[:, 4 * st + a, 0:HW], wt[:, R_CRE, :], part(ab[st][:, 0], a), start=True, stop=False)
                        last = mm(PS[:, 4 * st + a, 0:HW], wt[:, R_CIM, :], part(ab[st][:, 1], a), start=False, stop=True)
                    last.then_inc(s_y.sem, 1)
                centred(1, h2, s_h2)
                var(1)
                var(2)
                for st in range(2):
                    pe.wait_ge(norms[2]["nx"].sem, norms[2]["nx"].at(r, 1, st))
                    product(st, 0, wt[:, R_WQ2, :], xr[st], None)
                    product(st, 2, q_rot[:, :], xr[st], s_q2)
                for st in range(2):
                    pe.wait_ge(s_rp.sem, r * 8 + 2 * st + 2)
                    product(st, 0, wt[:, R_WK2, :], xr[st], None)
                    product(st, 2, k_rot[:, :], xr[st], s_k2)
                for st in range(2):
                    pe.wait_ge(s_rp.sem, r * 8 + 4 + 2 * st + 2)
                    for n, (t0, t1) in enumerate(((0, QA), (QA, S))):
                        for i in range(PAIRS):
                            last = mm(PS[0:t1 - t0, 4 * st + n, i * 128:(i + 1) * 128], xr[st][:, i * S + t0:i * S + t1],
                                      wt[:, R_WV2, :], start=True, stop=True)
                    last.then_inc(s_v2.sem, 1)

                def score2(w):
                    st, u = w % 2, w // 2
                    i, kind = u // KINDS, u % KINDS
                    b = PS[:, 4 * st + u % 2]
                    if u == 0:
                        pe.wait_ge(s_v2e.sem, s_v2e.at(r, 1, st))
                    if u < 2:
                        pe.wait_ge(s_km.sem, s_km.at(r, 2 * (2 * u + st) + 2))
                        pe.wait_ge(s_kd.sem, s_kd.at(r, 2 * (2 * u + st) + 2))
                    if u >= 2:
                        pe.wait_ge(s_e2.sem, s_e2.at(r, w - 3))
                    if u == 2:
                        pe.wait_ge(s_qt.sem, s_qt.at(r, 1, st))
                    if kind < 2:
                        mm(b, q2[st][:, i * S:i * S + QA], km[st][:, NH * kind:NH * (kind + 1), i * S:i * S + QA], start=True, stop=False)
                        mm(b, ident_b[:, :], neg_b[:, 0:QA].unsqueeze(1).broadcast_to([128, NH, QA]), start=False,
                           stop=True).then_inc(s_s2.sem, 1)
                    else:
                        mm(b[:, 0:S], qt[st][:, i * QA:(i + 1) * QA], k2[st][:, i * S:(i + 1) * S], start=True, stop=False)
                        mm(b[:, QA:S], ident_b[:, :], neg_b[:, QA:S], start=False, stop=True).then_inc(s_s2.sem, 1)

                def turn2(w):
                    st, u = w % 2, w // 2
                    b, p = PS[:, 4 * st + 2], pw[st][u % 2]
                    pe.wait_ge(s_n2.sem, s_n2.at(r, w + 1))
                    if w >= 2:
                        pe.wait_ge(s_pt2.sem, s_pt2.at(r, w - 1))
                    if u % KINDS < 2:
                        for h in range(NH):
                            last = nc.tensor.transpose(b[:, h * QA:(h + 1) * QA], p[:, h * QA:(h + 1) * QA], ident)
                    else:
                        nc.tensor.transpose(b[:, 0:QA], p[:, 0:QA], ident)
                        last = nc.tensor.transpose(b[0:QB, QA:2 * QA], p[:, QA:S], ident)
                    last.then_inc(s_t2.sem, 1)

                def value2(w):
                    st, u = w % 2, w // 2
                    i, kind = u // KINDS, u % KINDS
                    b = PS[:, 4 * st + 3, 0:2 * S].rearrange("q (r s) -> q r s", r=2)
                    pe.wait_ge(s_pt2.sem, s_pt2.at(r, w + 1))
                    if kind == 0 and i >= 1:
                        pe.wait_ge(s_h3.sem, s_h3.at(r, 2 * (i - 1) + st + 1))
                    for p in range(2):
                        for kv in range(NKV):
                            e = slice(64 * p + HP * kv, 64 * p + HP * kv + HP)
                            if kind == p:
                                last = mm(b[e, :, 0:QA], vt[st][:, i, e], pt[st][:, 2 * QA * kv:2 * QA * (kv + 1)], start=True, stop=True)
                            elif kind == 2:
                                o = 2 * QB * (2 * p + kv)
                                mm(b[e, :, QA:S], vt[st][:, i, e], pt[st][:, o:o + 2 * QB], start=True, stop=False)
                                last = mm(b[e, :, QA:S], vt[st][0:QB, PAIRS + i, e], pt[st][0:QB, QA + o:QA + o + 2 * QB],
                                          start=False, stop=True)
                    last.then_inc(s_o2.sem, 1)

                def project2(w):
                    st, i = w % 2, w // 2 // KINDS
                    pe.wait_ge(s_on.sem, s_on.at(r, 2 * i + st + 1))
                    for j, k in enumerate((R_WO2, R_WO3)):
                        last = mm(PS[:, 4 * st + 3, 2 * S:3 * S], wt[:, k, :], on[st][:, j * S:(j + 1) * S], start=(j == 0),
                                  stop=(j == 1))
                    last.then_inc(s_at.sem, 1)

                for w in range(4):
                    score2(w)
                for w in range(2 * U2 + 2):
                    if w < 2 * U2:
                        turn2(w)
                    if w + 4 < 2 * U2:
                        score2(w + 4)
                    if 1 <= w <= 2 * U2:
                        value2(w - 1)
                    if last_kind(w - 2):
                        project2(w - 2)
                var(3)
                for st in range(2):
                    pe.wait_ge(norms[3]["nx"].sem, norms[3]["nx"].at(r, 1, st))
                    for c in range(NTC):
                        last = mm(PS[0:TC, 4 * st, c * 2 * NE:(c + 1) * 2 * NE], flat[st][:, c * TC:(c + 1) * TC],
                                  wt[:, R_RT, 0:2 * NE], start=True, stop=True)
                    last.then_inc(s_rt.sem, 1)
                    for q in range(CHUNKS):
                        for p in range(2):
                            last = mm(PS[:, 4 * st + 1 + q, p * QW:(p + 1) * QW], cst[:, C_DUP + 128 * p:C_DUP + 128 * p + 128],
                                      flat[st][:, q * QW:(q + 1) * QW], start=True, stop=True)
                    last.then_inc(s_dup.sem, 1)
                for st in range(2):
                    pe.wait_ge(s_xl.sem, s_xl.at(r, 1, st))
                    for q in range(CHUNKS):
                        for p in range(2):
                            for c in range(2):
                                o = p * QW + c * TC
                                last = mm(PS[0:40, 4 * st + 1 + q, o:o + TC], wtok[st][:, (2 * q + c) * 2 + p, :],
                                          ident[0:TC, 0:TC], start=True, stop=True)
                    last.then_inc(s_wt.sem, 1)
                pe.wait_ge(s_wl.sem, s_wl.at(r, 2))

                def second(n):
                    c, k = n // TILES, n % TILES
                    m = rows(k)
                    pe.wait_ge(s_hh.sem, s_hh.at(r, n + 1))
                    if k == 0 and c >= 2:
                        pe.wait_ge(s_h4.sem, s_h4.at(r, c - 1))
                    for p in range(2):
                        last = mm(PS[64 * p:64 * p + 64, 6 + c % 2, 0:QW], w2t[0:m, k, :], hh[0:m, n % 3, p * QW:(p + 1) * QW],
                                  start=(k == 0), stop=(k == TILES - 1))
                    last.then_inc(s_yo.sem, 1)

                for n in range(N):
                    c, k = n // TILES, n % TILES
                    st, q = c // CHUNKS, c % CHUNKS
                    m = rows(k)
                    e, t = slice(128 * k, 128 * k + m), slice(q * CW, (q + 1) * CW)
                    g, u, b = PS[0:m, n % 2, 0:CW], PS[0:m, 2 + n % 2, 0:CW], PS[0:m, 4 + n % 2, 0:CW]
                    if n >= 2:
                        pe.wait_ge(s_sg.sem, s_sg.at(r, n - 1))
                    mm(g, w1h[:, e], xs[st][:, t], start=True, stop=False)
                    mm(g, w1l[:, e], xs[st][:, t], start=False, stop=True).then_inc(s_g.sem, 1)
                    if n >= 2:
                        pe.wait_ge(s_tg.sem, s_tg.at(r, n - 1))
                    mm(u, w3h[:, e], xs[st][:, t], start=True, stop=False)
                    mm(u, w3l[:, e], xs[st][:, t], start=False, stop=True).then_inc(s_u.sem, 1)
                    if n >= 2:
                        pe.wait_ge(s_hh.sem, s_hh.at(r, n - 1))
                    mm(b, sel[:, e], wrow[st][:, t], start=True, stop=True).then_inc(s_wb.sem, 1)
                    if n >= 2:
                        second(n - 2)
                second(N - 2)
                second(N - 1)
                for st in range(2):
                    for c in range(NTC):
                        pe.wait_ge(s_h4.sem, s_h4.at(r, CHUNKS * st + c // 2 + 1))
                        last = nc.tensor.transpose(PS[0:TC, 2 * st + c // 3, (c % 3) * 128:(c % 3 + 1) * 128],
                                                   h2[st][:, c * TC:(c + 1) * TC], ident)
                    last.then_inc(s_ot.sem, 1)
                pe.wait_ge(s_oe.sem, s_oe.at(r, 2))


_INS = ["x", "L0_tok_conv_w", "L0_tok_conv_b", "L0_tok_wq", "L0_tok_bq", "L0_tok_wk", "L0_tok_bk", "L0_tok_wv", "L0_tok_bv",
        "L0_tok_wo", "L0_tok_bo", "L0_attn_nu_log", "L0_attn_theta_log", "L0_attn_gamma_log", "L0_attn_B_re", "L0_attn_B_im",
        "L0_attn_C_re", "L0_attn_C_im", "L0_ffn_ln1_w", "L0_ffn_ln2_w", "L0_ffn_wq", "L0_ffn_wk", "L0_ffn_wv", "L0_ffn_wo",
        "L0_ffn_router_w", "L0_ffn_w1", "L0_ffn_w2", "L0_ffn_w3"]


def kernel(**inputs):
    import numpy as _np
    import concourse.bacc as _bacc
    from concourse import mybir as _mybir
    from concourse.bass_utils import run_bass_kernel_spmd as _run

    nc = _bacc.Bacc("TRN2", target_bir_lowering=False, num_devices=1)
    arrays, args = {}, []
    c, s = constants()
    for name, a in [(n, inputs[n]) for n in _INS] + [("consts", c), ("experts", s)]:
        a = _np.ascontiguousarray(a)
        arrays[f"in_{name}_dram"] = a
        args.append(nc.dram_tensor(f"in_{name}_dram", a.shape, _mybir.dt.from_np(a.dtype), kind="ExternalInput").ap())
    args.append(nc.dram_tensor("out_0_dram", (IMAGES, S, D), _mybir.dt.float32, kind="ExternalOutput").ap())
    vit_tower(nc, *args)
    r = _run(nc, [arrays], core_ids=[0])
    return r.results[0]["out_0_dram"]
```

```python
import numpy as np
from contextlib import ExitStack
import concourse.bass as bass
from concourse import mybir

D = 64
S = 144
IMAGES = 64
SIDE = 96
PAIRS = 4
GROUPS = IMAGES // (2 * PAIRS)
ROUNDS = GROUPS // 2
W = PAIRS * S
HW = W // 2
HS = S // 2
QA = 128
QB = S - QA
BANDS = SIDE // 8
CH = 4
NH, NKV, HD = 4, 2, 16
HP = 32
NE, HID = 8, 170
EPS_LN, EPS_RMS = 1e-5, 1e-6
UT = 128 // NE
TILES = -(-HID // UT)
EH = TILES * 128
CHUNKS = 3
CW = 2 * W // CHUNKS
QW = CW // 2
TC = 96
NTC = W // TC

C_ID, C_AVG, C_CEN, C_HM, C_ROPE, C_PRI, C_NEG = 0, 128, 256, 384, 392, 680, 688
C_DUP = C_NEG + S
C_END = C_DUP + 256


def constants():
    f = np.float32
    c = np.zeros((128, C_END), f)
    c[:, C_ID:C_ID + 128] = np.eye(128, dtype=f)
    for p in range(2):
        c[64 * p:64 * p + 64, C_AVG + 64 * p:C_AVG + 64 * p + 64] = 1.0 / D
    c[:, C_CEN:C_CEN + 128] = c[:, C_ID:C_ID + 128] - c[:, C_AVG:C_AVG + 128]
    for h in range(8):
        c[16 * h:16 * h + 16, C_HM + h] = HD ** -0.5
    inv = 1.0 / 10000.0 ** (np.arange(0, HD, 2, dtype=f) / HD)
    fr = np.outer(np.arange(S, dtype=f), inv)
    emb = np.concatenate([fr, fr], -1)
    c[:, C_ROPE:C_ROPE + S] = np.tile(np.cos(emb).T, (8, 1))
    c[:, C_ROPE + S:C_ROPE + 2 * S] = np.tile(np.sin(emb).T, (8, 1))
    c[:, C_PRI:C_PRI + NE] = np.arange(NE, 0, -1)
    t = np.arange(QA)
    c[:, C_NEG:C_NEG + QA] = np.where(t[None, :] > t[:, None], -1e30, 0.0)
    c[:, C_NEG + QA:C_NEG + S] = np.where(t[None, :QB] > t[:, None] % QB, -1e30, 0.0)
    for p in range(2):
        for r in range(2):
            c[64 * p:64 * p + 64, C_DUP + 128 * p + 64 * r:C_DUP + 128 * p + 64 * r + 64] = np.eye(D, dtype=f)
    s = np.zeros((128, 128), f)
    for e in range(NE):
        s[e, UT * e:UT * e + UT] = 1.0
        s[32 + e, UT * e:UT * e + UT] = 1.0
    return c, s


NR = 14
(R_WQ, R_WK, R_WO, R_CRE, R_CIM, R_WQ2, R_WK2, R_WV2, R_WO2, R_WO3, R_RT, R_BRE, R_BIM, R_WV) = range(NR)
NV = 9
V_BQ, V_BK, V_BV, V_BO, V_NU, V_TH, V_GA, V_L1, V_L2 = range(NV)
V_CW, V_CB = NV, NV + 4 * CH
V_END = V_CB + CH


def lay_out(a):
    f = np.float32
    w = np.zeros((128, NR, 128), f)
    for p in range(2):
        h = slice(64 * p, 64 * p + 64)
        for k, n in ((R_WQ, "L0_tok_wq"), (R_WK, "L0_tok_wk"), (R_WO, "L0_tok_wo"), (R_CRE, "L0_attn_C_re"),
                     (R_CIM, "L0_attn_C_im"), (R_WQ2, "L0_ffn_wq")):
            w[h, k, h] = a[n].T
        for k, n in ((R_BRE, "L0_attn_B_re"), (R_BIM, "L0_attn_B_im"), (R_WV, "L0_tok_wv")):
            w[h, k, h] = a[n]
        for j in range(NH):
            kv, r = j // 2, 64 * p + HD * j
            w[h, R_WK2, r:r + HD] = a["L0_ffn_wk"][HD * kv:HD * kv + HD].T
            r = 64 * p + HP * kv
            w[r:r + HD, (R_WO2, R_WO3)[j % 2], h] = a["L0_ffn_wo"][:, HD * j:HD * j + HD].T
        for kv in range(NKV):
            r = 64 * p + HP * kv
            w[h, R_WV2, r:r + HD] = a["L0_ffn_wv"][HD * kv:HD * kv + HD].T
        w[h, R_RT, NE * p:NE * p + NE] = a["L0_ffn_router_w"].T
    v = np.zeros((128, V_END), f)
    for k, n in enumerate(("tok_bq", "tok_bk", "tok_bv", "tok_bo", "attn_nu_log", "attn_theta_log", "attn_gamma_log",
                           "ffn_ln1_w", "ffn_ln2_w")):
        v[:, k] = np.tile(a["L0_" + n], 2)
    v[:, V_CW:V_CB] = a["L0_tok_conv_w"].reshape(1, -1)
    v[:, V_CB:] = a["L0_tok_conv_b"]
    up = np.zeros((2, NE, TILES * UT, D), f)
    up[:, :, :HID] = a["L0_ffn_w1"], a["L0_ffn_w3"]
    up = up.reshape(2, NE, TILES, UT, D).transpose(0, 4, 2, 1, 3).reshape(2, D, EH)
    down = np.zeros((NE, TILES * UT, D), f)
    down[:, :HID] = a["L0_ffn_w2"].transpose(0, 2, 1)
    down = down.reshape(NE, TILES, UT, D).transpose(0, 2, 1, 3).reshape(128, TILES, D)
    return w, v, np.concatenate([up[0], up[0]]), np.concatenate([up[1], up[1]]), down


def vit_tower(nc, x, small, vectors, up1, up3, down, consts, experts, out):
    fp32, bf16, f32r = mybir.dt.float32, mybir.dt.bfloat16, mybir.dt.float32r
    ALU, ACT, AX = mybir.AluOpType, mybir.ActivationFunctionType, mybir.AxisListType
    PI = float(np.pi)

    ctx = ExitStack()
    with ctx:
        def sb(name, shape, dt=fp32):
            return ctx.enter_context(nc.sbuf_tensor(name, shape, dt))

        class Count:
            def __init__(self, name, per):
                self.sem, self.per = ctx.enter_context(nc.semaphore(name)), per

            def at(self, r, n, st=0):
                return r * (2 * self.per) + st * self.per + n

            def half(self, r, n, h):
                return r * (2 * self.per) + h * (self.per // 2) + n

        def one(name):
            return ctx.enter_context(nc.semaphore(name))

        cst = sb("cst", [128, C_END])
        ident = cst[:, C_ID:C_ID + 128]
        avg = cst[:, C_AVG:C_AVG + 128]
        centre = cst[:, C_CEN:C_CEN + 128]
        rope = cst[:, C_ROPE:C_ROPE + 2 * S].rearrange("q (k s) -> q k s", k=2)
        ident_b = sb("ident_b", [128, 128], bf16)
        neg_b = sb("neg_b", [128, S], bf16)
        wt = sb("wt", [128, NR - 1, 128])
        wvo = sb("wvo", [128, 128])
        q_rot = sb("q_rot", [128, 128])
        k_rot = sb("k_rot", [128, 128])
        w1h, w1l = sb("w1h", [128, EH], f32r), sb("w1l", [128, EH], f32r)
        w3h, w3l = sb("w3h", [128, EH], f32r), sb("w3l", [128, EH], f32r)
        sel = sb("sel", [128, 128], f32r)
        w2t = sb("w2t", [128, TILES, D])
        col = sb("col", [128, V_END])
        cw, cb = col[0:TC, V_CW:V_CB], col[0:TC, V_CB:V_END]
        bq8 = sb("bq8", [128, 1])
        bvo = sb("bvo", [128, 1])
        eps = sb("eps", [128, 3])
        tmp = sb("tmp", [128, 8])
        ang = sb("ang", [128, 8])
        lam = sb("lam", [128, 1])
        gam = sb("gam", [128, 1])
        rot = sb("rot", [128, 3, S])
        rot_cos, rot_sin = rot[:, 0, :], rot[:, 1, :]
        decay = sb("decay", [128, W])

        def both(name, shape, dt=fp32):
            return [sb(f"{name}{st}", shape, dt) for st in range(2)]

        NT = 2 * NTC
        HH = 5
        img = both("img", [TC, 768])
        y = both("y", [TC, CH, 192])
        t4 = both("t4", [128, 4, W])
        km = both("km", [128, 8, W])
        kbd = both("kbd", [128, PAIRS, 2, S])
        h1 = both("h1", [128, W])
        h2 = both("h2", [128, W])
        xl = both("xl", [128, W])
        h3 = both("h3", [128, W])
        q2 = both("q2", [128, W])
        k2 = both("k2", [128, W])
        vt = both("vt", [128, 2 * PAIRS, 128])
        pt = both("pt", [128, 4 * QA])
        ex = both("ex", [128, 2, 3, 4])
        rl, re, rk, rs1, rs2, rt = (both(n, [TC, NT, NE]) for n in ("rl", "re", "rk", "rs1", "rs2", "rt"))
        rm = both("rm", [TC, 6, NT])
        wtok = both("wtok", [TC, NT, 72])
        ot = both("ot", [TC, NTC, 128])
        wrow = both("wrow", [128, 2 * W], f32r)
        xs = both("xs", [128, 2 * W], f32r)
        sg = sb("sg", [128, 2, CW])
        tg = sb("tg", [128, 3, CW])
        hh = sb("hh", [128, HH, CW])
        zin = [t[:, 0:2] for t in km]
        z = [t[:, 2:4] for t in km]
        ab = [t[:, 4:6] for t in km]
        xn = [t[:, 6] for t in km]
        xf = [t[:, 7] for t in km]
        qf = [t[:, 2] for t in km]
        xr = [t[:, :] for t in h1]
        sq = [t[:, 0] for t in t4]
        rstd = [t[:, 1] for t in t4]
        flat = [t[:, 2] for t in t4]
        rms = [t[:, 2] for t in t4]
        pw = [(t[:, 0, 0:4 * QA], t[:, 3, 0:4 * QA]) for t in t4]
        qt = [t[:, 1, 0:4 * QA] for t in t4]
        on = [t[:, 2, 0:2 * S] for t in t4]
        wbs = km[0][:, 0:2, 0:CW]
        kmf = [t[:, :, :].rearrange("q h w -> q (h w)") for t in km]
        up = [t[:, 3 * W:3 * W + EH] for t in kmf]
        raw = kmf[1][:, 0:3 * 128].rearrange("q (a b) -> q a b", a=3)
        rot_t = kmf[1][:, 3 * 128:3 * 128 + 4 * S].rearrange("q (k s) -> q k s", k=4)
        sel_raw = kmf[1][:, 4 * 128 + 4 * S:5 * 128 + 4 * S]

        PS = ctx.enter_context(nc.psum_tensor("PS", [128, 8, 512], fp32))

        s_col, s_cst, s_raw, s_up, s_down = one("s_col"), one("s_cst"), one("s_raw"), one("s_up"), one("s_down")
        s_tr, s_dch, s_ach, s_pch, s_rot = one("s_tr"), one("s_dch"), one("s_ach"), one("s_pch"), one("s_rot")
        s_gam, s_lin, s_ang, s_sin = one("s_gam"), one("s_lin"), one("s_ang"), one("s_sin")
        s_high, s_dset, s_aset, s_pset, s_pk = one("s_high"), one("s_dset"), one("s_aset"), one("s_pset"), one("s_pk")
        s_img = [one(f"s_img{st}") for st in range(2)]
        s_out = [one(f"s_out{st}") for st in range(2)]
        s_cv0, s_cv, s_ft, s_xe = Count("s_cv0", 4), Count("s_cv", 12), Count("s_ft", 2), Count("s_xe", 2)
        s_xd = Count("s_xd", 2)
        s_q, s_k, s_v, s_qe, s_ke, s_ve = (Count(n, c) for n, c in (
            ("s_q", 1), ("s_k", 1), ("s_v", 1), ("s_qe", 1), ("s_ke", 2), ("s_ve", 1)))
        U1 = 2 * PAIRS
        (s_s1, s_m1, s_e1, s_i1, s_n1, s_t1, s_pt1, s_o1) = (
            Count(n, U1) for n in ("s_s1", "s_m1", "s_e1", "s_i1", "s_n1", "s_t1", "s_pt1", "s_o1"))
        s_h1 = Count("s_h1", PAIRS)
        norms = [{k: Count(f"s_{k}{n}", 2) for k in ("cen", "sq", "var", "ln", "rs", "nx")} for n in range(4)]
        s_b, s_rm, s_ra, s_sc = Count("s_b", 2), Count("s_rm", 4), Count("s_ra", 4), Count("s_sc", 4)
        s_rb, s_rc, s_y, s_h2 = Count("s_rb", 4), Count("s_rc", 4), Count("s_y", 2), Count("s_h2", 2)
        s_q2, s_k2, s_km = Count("s_q2", 2), Count("s_k2", 2), Count("s_km", 2)
        s_rp, s_rq = ([Count(f"{n}_{i}", 2) for i in "qk"] for n in ("s_rp", "s_rq"))
        TURNS = ((0, 0), (0, 1), (1, 0), (0, 2), (1, 1), (0, 3), (1, 2), (1, 3))
        s_kd = Count("s_kd", 6)
        s_v2, s_v2e = Count("s_v2", 1), Count("s_v2e", 1)
        KINDS = 3
        U2 = PAIRS * KINDS
        s_qt = Count("s_qt", 1)
        (s_s2, s_m2, s_e2, s_i2, s_n2, s_t2, s_pt2, s_o2) = (
            Count(n, U2) for n in ("s_s2", "s_m2", "s_e2", "s_i2", "s_n2", "s_t2", "s_pt2", "s_o2"))
        s_on, s_at = Count("s_on", PAIRS), Count("s_at", PAIRS)
        s_h3, s_h23 = Count("s_h3", PAIRS), Count("s_h23", 1)
        TOPK = 17
        s_rt, s_tk, s_re, s_wk = Count("s_rt", 1), Count("s_tk", TOPK), Count("s_re", 1), Count("s_wk", 2)
        s_dup, s_xh, s_xl = Count("s_dup", CHUNKS), Count("s_xh", CHUNKS), Count("s_xl", CHUNKS)
        s_wt, s_wh, s_wl = Count("s_wt", CHUNKS), Count("s_wh", CHUNKS), Count("s_wl", CHUNKS)
        N = 2 * CHUNKS * TILES
        s_wb, s_wbe = Count("s_wb", CHUNKS), Count("s_wbe", CHUNKS)
        s_g, s_u, s_sg, s_tg, s_yo = (Count(n, N // 2) for n in ("s_g", "s_u", "s_sg", "s_tg", "s_yo"))
        s_hd, s_hp = Count("s_hd", N // 3), Count("s_hp", N // 6)
        s_h4, s_ot, s_oe = Count("s_h4", CHUNKS), Count("s_ot", 2), Count("s_oe", 2)
        OUT = ((0, 0, 40), (0, 1, 43), (1, 0, 61), (1, 1, N))

        def halves(st, k):
            return PS[:, 4 * st + k:4 * st + k + 2, 0:HW]

        def psum_quads(st, k):
            return halves(st, k).rearrange("q a (i s) -> q a i s", s=S)

        def conv_rows(st, c):
            o = (c % 2) * S
            return PS[:, 4 * st + c // 2, o:o + S].rearrange("q (k i b) -> q k i b", k=3, i=PAIRS)

        def tokens(st, c):
            return xf[st].rearrange("q (i c b k) -> q c k i b", i=PAIRS, c=CH, k=3)[:, c]

        def first(ap):
            return ap.rearrange("q (i s) -> q i s", s=S)[:, :, 0:QA]

        def pair_up(ap):
            return ap.rearrange("q (a w) -> q a w", a=2)

        def bank(h, k):
            return PS[:, 2 * h + k, 0:HW]

        def piece(t, h):
            return part(t[h // 2], h % 2)

        def pairs(ap):
            return ap.rearrange("q (i s) -> q i s", s=S)

        def two_pairs(ap):
            return ap.rearrange("q k (i s) -> q k i s", s=S)

        def two_banks(h):
            return PS[:, 2 * h:2 * h + 2, 0:HW]

        def two_tables(t):
            return t.unsqueeze(2).broadcast_to([128, 2, 2, S])

        def two_parts(t, k, a):
            return t[:, k:k + 2, a * HW:(a + 1) * HW]

        def pair_ready(r, h):
            return r * (2 * PAIRS) + 2 * (2 * (h % 2) + 1) + h // 2 + 1

        def part(t, a):
            return t[:, a * HW:(a + 1) * HW]

        def last_kind(w):
            return 0 <= w < 2 * U2 and w // 2 % KINDS == KINDS - 1

        W0 = 4
        XROW = 10
        WROW = 20
        LAG = 3
        WB = 8

        def rows_bank(st, q):
            return 5 if st or q else 4

        def on_pool(n):
            return n % 3 == 2

        def hidden(r, n):
            if on_pool(n):
                return s_hp.sem, s_hp.at(r, (n + 1) // 3)
            return s_hd.sem, s_hd.at(r, n + 1 - (n + 1) // 3)

        block = ctx.enter_context(nc.Block())

        @block.sync
        def _(sp):
            xv = x.rearrange("b a h w -> (b a h w)").rearrange("(n r) -> n r", r=768)
            half_rows = IMAGES // 2 * BANDS
            ov = out.rearrange("b s d -> (b s) d")
            half_tok = IMAGES // 2 * S

            def load(r, st):
                for p in range(2):
                    sp.dma_start(img[st][48 * p:48 * p + 48, :],
                                 xv[bass.ds(r * (2 * PAIRS * BANDS) + st * PAIRS * BANDS + p * half_rows, PAIRS * BANDS), :]
                                 ).then_inc(s_img[st], 16)

            def store(r, st):
                for p in range(2):
                    sp.dma_start(ov[bass.ds(r * (2 * W) + st * W + p * half_tok, W), :].rearrange("(c r) d -> r c d", r=TC),
                                 ot[st][:, :, 64 * p:64 * p + 64]).then_inc(s_out[st], 16)

            sp.dma_start(col[:, :], vectors).then_inc(s_col, 16)
            for st in range(2):
                load(0, st)
            sp.dma_start(cst[:, :], consts).then_inc(s_cst, 16)
            sp.dma_start(raw, small[:, R_BRE:NR, :]).then_inc(s_raw, 16)
            sp.dma_start(wt[:, 0:R_BRE, :], small[:, 0:R_BRE, :]).then_inc(s_raw, 16)
            sp.dma_start(sel_raw, experts).then_inc(s_cst, 16)
            for k, m in enumerate((up1, up3)):
                sp.dma_start(up[k], m).then_inc(s_up, 16)
            sp.dma_start(w2t[:, :, :], down).then_inc(s_down, 16)
            with sp.Fori(1, ROUNDS) as r:
                for st in range(2):
                    sp.wait_ge(s_cv.sem, s_cv.at(r - 1, 12, st))
                    load(r, st)
                for st in range(2):
                    sp.wait_ge(s_oe.sem, s_oe.at(r - 1, 2, st))
                    store(r - 1, st)
            for st in range(2):
                sp.wait_ge(s_cv.sem, s_cv.at(ROUNDS - 1, 12, st))
                load(ROUNDS - 1, st)
            for st in range(2):
                sp.wait_ge(s_oe.sem, s_oe.at(ROUNDS - 1, 2, st))
                store(ROUNDS - 1, st)
            for st in range(2):
                sp.wait_ge(s_out[st], 32 * ROUNDS + 1)

        @block.gpsimd
        def _(pool):
            for k, v in enumerate((EPS_LN, EPS_RMS, EPS_LN * EPS_RMS)):
                nc.gpsimd.memset(eps[:, k:k + 1], v).then_inc(s_pset, 1)
            for st in range(2):
                nc.gpsimd.memset(kbd[st][:, :, :, :], 0.0).then_inc(s_pk, 1)
            for st in range(2):
                nc.gpsimd.memset(ot[st][:, :, :], 0.0).then_inc(s_out[st], 1)
                nc.gpsimd.memset(wtok[st][:, :, :], 0.0).then_inc(s_pset, 1)
                nc.gpsimd.memset(wrow[st][:, :].bitcast(fp32), 0.0).then_inc(s_pset, 1)
            chain = [0]

            def link(ins):
                chain[0] += 1
                ins.then_inc(s_pch, 1)
                pool.wait_ge(s_pch, chain[0])

            G = nc.gpsimd
            G.memset(rot_cos[:, 0:1], 1.0)
            G.memset(rot_sin[:, 0:1], 0.0)
            pool.wait_ge(s_sin, 2)
            G.tensor_copy(rot_sin[:, 1:2], ang[:, 6:7])
            link(G.tensor_copy(rot_cos[:, 1:2], ang[:, 7:8]))
            m = 1
            while m < S - 1:
                n = min(m, S - 1 - m)
                a, b = slice(1, 1 + n), slice(m + 1, m + 1 + n)
                turn = rot[:, 0:2, m:m + 1].broadcast_to([128, 2, n])
                flip = rot[:, 1::-1, m:m + 1].broadcast_to([128, 2, n])
                G.tensor_tensor(rot_t[:, 0:2, 0:n], rot[:, 0:2, a], turn, ALU.mult)
                link(G.tensor_tensor(rot_t[:, 2:4, 0:n], rot[:, 0:2, a], flip, ALU.mult))
                G.tensor_tensor(rot_cos[:, b], rot_t[:, 0, 0:n], rot_t[:, 1, 0:n], ALU.subtract)
                link(G.tensor_tensor(rot_sin[:, b], rot_t[:, 2, 0:n], rot_t[:, 3, 0:n], ALU.add))
                m *= 2
            G.tensor_copy(rot[:, 2, :], rot_cos)
            link(G.memset(decay[:, :], 1.0))
            pool.wait_ge(s_lin, 2)
            link(G.tensor_scalar(decay[:, :], decay[:, :], lam[:, 0:1], None, ALU.mult))
            G.memset(decay[:, :].rearrange("q (i s) -> q i s", s=S)[:, :, 0:1], 0.0).then_inc(s_rot, 1)

            with pool.Fori(0, ROUNDS) as r:
                for h in range(4):
                    st, a = h // 2, h % 2
                    t = t4[st]
                    for k, (i, j, op) in enumerate(((0, 1, ALU.add), (3, 2, ALU.subtract))):
                        pool.wait_ge(s_rm.sem, s_rm.half(r, k + 1, h))
                        nc.gpsimd.tensor_tensor(part(zin[st][:, k], a), part(t[:, i], a), part(t[:, j], a), op).then_inc(s_ra.sem, 1)
                for h in range(4):
                    st, a = h // 2, h % 2
                    t = t4[st]
                    for k, op in enumerate((ALU.subtract, ALU.add)):
                        pool.wait_ge(s_rb.sem, s_rb.half(r, k + 1, h))
                        nc.gpsimd.tensor_tensor(part(ab[st][:, k], a), part(t[:, 2 * k], a), part(t[:, 2 * k + 1], a), op).then_inc(s_rc.sem, 1)
                for n, h in TURNS:
                    st, a = h // 2, h % 2
                    pool.wait_ge(s_rp[n].sem, s_rp[n].half(r, 1, h))
                    nc.gpsimd.tensor_tensor(piece((q2, k2)[n], h), part(t4[st][:, 2 * n], a), part(t4[st][:, 2 * n + 1], a),
                                            ALU.add).then_inc(s_rq[n].sem, 1)
                hm = cst[:, C_HM:C_HM + 8].unsqueeze(1).unsqueeze(3).broadcast_to([128, PAIRS, 8, QB])
                for st in range(2):
                    pool.wait_ge(s_rq[0].sem, s_rq[0].at(r, 2, st))
                    q = q2[st][:, :].rearrange("q (i s) -> q i s", s=S)[:, :, QA:].unsqueeze(2).broadcast_to([128, PAIRS, 8, QB])
                    nc.gpsimd.tensor_tensor(qt[st].rearrange("q (i h s) -> q i h s", i=PAIRS, h=8), q, hm, ALU.mult).then_inc(s_qt.sem, 1)
                for st in range(2):
                    pool.wait_ge(s_h3.sem, s_h3.at(r, 2 * PAIRS))
                    nc.gpsimd.tensor_tensor(h2[st][:, :], h2[st][:, :], h3[st][:, :], ALU.add).then_inc(s_h23.sem, 1)
                for n in range(2, N, 3):
                    c = n // TILES
                    pool.wait_ge(s_wbe.sem, s_wbe.at(r, c + 1))
                    pool.wait_ge(s_tg.sem, s_tg.at(r, n + 1))
                    if n >= HH:
                        pool.wait_ge(s_yo.sem, s_yo.at(r, n - HH + 1))
                    nc.gpsimd.tensor_tensor(hh[:, n % HH], tg[:, n % 3], wbs[:, c % 2], ALU.mult).then_inc(s_hp.sem, 1)

        @block.scalar
        def _(act):
            A = nc.scalar.activation
            chain = [0]

            def link(ins):
                chain[0] += 1
                ins.then_inc(s_ach, 1)
                act.wait_ge(s_ach, chain[0])

            def tap0(r, k):
                st, c = k // CH, k % CH
                if c == 0:
                    act.wait_ge(s_img[st], r * 32 + 32)
                A(y[st][:, c, :].rearrange("q (i j) -> q i j", i=4),
                  img[st][:, :].rearrange("q (i a j b) -> q i a j b", i=4, a=2, b=2)[:, :, 0, :, 0], ACT.Identity,
                  bias=cb[:, c:c + 1], scale=cw[:, 4 * c:4 * c + 1]).then_inc(s_cv0.sem, 1)

            act.wait_ge(s_col, 16)
            link(A(tmp[:, 0:1], col[:, V_NU:V_NU + 1], ACT.Exp))
            A(lam[:, :], tmp[:, 0:1], ACT.Exp, scale=-1.0).then_inc(s_lin, 1)
            A(tmp[:, 1:2], col[:, V_TH:V_TH + 1], ACT.Exp).then_inc(s_lin, 1)
            A(gam[:, :], col[:, V_GA:V_GA + 1], ACT.Exp).then_inc(s_gam, 1)
            for k in range(2 * CH):
                tap0(0, k)
            act.wait_ge(s_ang, 1)
            A(ang[:, 6:7], ang[:, 4:5], ACT.Sin).then_inc(s_sin, 1)
            A(ang[:, 7:8], ang[:, 5:6], ACT.Sin).then_inc(s_sin, 1)
            act.wait_ge(s_cst, 32)
            A(ident_b[:, :], ident, ACT.Copy).then_inc(s_aset, 1)
            A(neg_b[:, :], cst[:, C_NEG:C_NEG + S], ACT.Copy).then_inc(s_aset, 1)
            A(sel[:, :], sel_raw, ACT.Copy).then_inc(s_aset, 1)
            act.wait_ge(s_up, 32)
            for k, high in enumerate((w1h, w3h)):
                A(high[:, :], up[k], ACT.Copy, scale=col[:, V_L2:V_L2 + 1]).then_inc(s_high, 1)
            act.wait_ge(s_pset, 7)

            nc.scalar.preload_act_table_set("natural_log_exp_and_others")
            with act.Fori(0, ROUNDS) as r:
                for c in range(CH):
                    act.wait_ge(s_ft.sem, s_ft.at(r, 1 + c // 2))
                    A(tokens(0, c), conv_rows(0, c), ACT.Copy).then_inc(s_xe.sem, 1)
                for st in range(2):
                    act.wait_ge(s_q.sem, s_q.at(r, 1, st))
                    A(pair_up(qf[st]), halves(st, 2), ACT.Identity, bias=bq8[:, 0:1], scale=D ** -0.5).then_inc(s_qe.sem, 1)
                for st in range(2):
                    act.wait_ge(s_v.sem, s_v.at(r, 1, st))
                    A(vt[st][0:HS, :, :].rearrange("q (a i) e -> q a (i e)", a=2), PS[0:HS, 4 * st + 2:4 * st + 4, :],
                      ACT.Copy).then_inc(s_ve.sem, 1)

                def attn1_exp(w):
                    st, u = w % 2, w // 2
                    b, p, e = PS[0:HS, 4 * st + u % 2], pw[st][u % 2], ex[st][0:HS, u % 2]
                    act.wait_ge(s_m1.sem, s_m1.at(r, w + 1))
                    if w >= 4:
                        act.wait_ge(s_t1.sem, s_t1.at(r, w - 3))
                        act.wait_ge(s_i1.sem, s_i1.at(r, w - 3))
                    for p_ in range(2):
                        t = slice(p_ * S, (p_ + 1) * S)
                        last = A(p[0:HS, t], b[:, t], ACT.Exp, bias=e[:, 0, p_:p_ + 1], accum_out=e[:, 1, p_:p_ + 1])
                    last.then_inc(s_e1.sem, 1)

                def attn1_out(w):
                    st = w % 2
                    act.wait_ge(s_t1.sem, s_t1.at(r, w + 1))
                    if w >= 2:
                        act.wait_ge(s_o1.sem, s_o1.at(r, w - 1))
                    A(pt[st][0:HS, 0:2 * S], PS[0:HS, 4 * st + 2, 0:2 * S], ACT.Copy).then_inc(s_pt1.sem, 1)

                for w in range(2 * U1):
                    attn1_exp(w)
                    if w >= 2:
                        attn1_out(w - 2)
                attn1_out(2 * U1 - 2)
                attn1_out(2 * U1 - 1)

                def norm(n, e):
                    s = norms[n]
                    for h in range(4):
                        if n == 3:
                            act.wait_ge(s_h3.sem, pair_ready(r, h))
                            A(piece(sq, h), piece(h3, h), ACT.Square).then_inc(s["sq"].sem, 1)
                        else:
                            act.wait_ge(s["cen"].sem, s["cen"].half(r, 1, h))
                            A(piece(sq, h), bank(h, 0), ACT.Square).then_inc(s["sq"].sem, 1)
                    def log(m, h, dst, e, scale):
                        act.wait_ge(s["var"].sem, s["var"].half(r, 1, h))
                        A(piece(dst, h), bank(h, 1), ACT.Ln, bias=eps[:, e:e + 1], scale=scale).then_inc(norms[m]["ln"].sem, 1)

                    def root(m, h, dst):
                        act.wait_ge(norms[m]["ln"].sem, norms[m]["ln"].half(r, 1, h))
                        A(piece(dst, h), piece(dst, h), ACT.Exp, scale=-0.5).then_inc(norms[m]["rs"].sem, 1)

                    if n == 1:
                        for h in range(4):
                            log(2, h, rms, 2, 1 + EPS_RMS)
                            log(1, h, rstd, 0, 1.0)
                            root(2, h, rms)
                            root(1, h, rstd)
                    else:
                        for h in range(5):
                            if h < 4:
                                log(n, h, rstd, e, 1.0)
                            if h >= 1:
                                root(n, h - 1, rstd)

                norm(0, 0)
                norm(1, 0)
                def values_out(st):
                    act.wait_ge(s_v2.sem, s_v2.at(r, 1, st))
                    A(vt[st][:, 0:PAIRS, :].rearrange("q i e -> q (i e)"), PS[:, 4 * st, :], ACT.Copy)
                    A(vt[st][0:QB, PAIRS:, :].rearrange("q i e -> q (i e)"), PS[0:QB, 4 * st + 1, :],
                      ACT.Copy).then_inc(s_v2e.sem, 1)

                def mask_k(hf, st):
                    act.wait_ge(s_rq[1].sem, s_rq[1].at(r, 2, st))
                    h = NH * hf
                    A(first(km[st][:, h]), first(k2[st][:, :]), ACT.Copy, scale=cst[:, C_HM + h:C_HM + h + 1]).then_inc(s_km.sem, 1)

                values_out(0)
                mask_k(0, 0)
                values_out(1)
                mask_k(0, 1)
                mask_k(1, 0)
                mask_k(1, 1)

                def attn2_exp(w):
                    st, u = w % 2, w // 2
                    b, p, e = PS[:, 4 * st + u % 2], pw[st][u % 2], ex[st][:, u % 2]
                    act.wait_ge(s_m2.sem, s_m2.at(r, w + 1))
                    if w >= 4:
                        act.wait_ge(s_t2.sem, s_t2.at(r, w - 3))
                        act.wait_ge(s_i2.sem, s_i2.at(r, w - 3))
                    if u % KINDS < 2:
                        for h in range(NH):
                            t = slice(h * QA, (h + 1) * QA)
                            last = A(p[:, t], b[:, t], ACT.Exp, bias=e[:, 0, h:h + 1], accum_out=e[:, 1, h:h + 1])
                    else:
                        last = A(p[:, 0:S], b[:, 0:S], ACT.Exp, bias=e[:, 0, 0:1], accum_out=e[:, 1, 0:1])
                    last.then_inc(s_e2.sem, 1)

                def attn2_out(w):
                    st, u = w % 2, w // 2
                    act.wait_ge(s_t2.sem, s_t2.at(r, w + 1))
                    if w >= 2:
                        act.wait_ge(s_o2.sem, s_o2.at(r, w - 1))
                    b = PS[:, 4 * st + 2]
                    if u % KINDS < 2:
                        A(pt[st][:, :], b, ACT.Copy).then_inc(s_pt2.sem, 1)
                    else:
                        A(pt[st][:, 0:QA], b[:, 0:QA], ACT.Copy)
                        A(pt[st][0:QB, QA:2 * QA], b[0:QB, QA:2 * QA], ACT.Copy).then_inc(s_pt2.sem, 1)

                for w in range(2 * U2):
                    attn2_exp(w)
                    if w >= 2:
                        attn2_out(w - 2)
                attn2_out(2 * U2 - 2)
                attn2_out(2 * U2 - 1)
                norm(3, 1)
                def inputs_high(st, q):
                    act.wait_ge(s_dup.sem, s_dup.at(r, q + 1, st))
                    A(xs[st][:, q * CW:(q + 1) * CW], PS[:, 5 if st else 5 + q, 0:CW], ACT.Copy).then_inc(s_xh.sem, 1)

                for st in range(2):
                    act.wait_ge(s_tk.sem, s_tk.at(r, 2, st) if st == 0 else r * 2 * TOPK + 4)
                    A(re[st][:, :, :], rl[st][:, :, :], ACT.Exp).then_inc(s_re.sem, 1)
                for q in range(CHUNKS):
                    inputs_high(0, q)

                def tokens_out(st, a):
                    act.wait_ge(s_ot.sem, s_ot.at(r, a + 1, st))
                    act.wait_ge(s_out[st], r * 32 + 1)
                    A(ot[st][:, 3 * a:3 * a + 3, :].rearrange("q c e -> q (c e)"), PS[0:TC, 5, 0:CW], ACT.Copy).then_inc(s_oe.sem, 1)

                def weights_high(st, q):
                    act.wait_ge(s_wt.sem, s_wt.at(r, q + 1, st))
                    A(wrow[st][0:40, q * CW:(q + 1) * CW], PS[0:40, rows_bank(st, q), 0:CW], ACT.Copy).then_inc(s_wh.sem, 1)

                def weights_out(c):
                    act.wait_ge(s_wb.sem, s_wb.at(r, c + 1))
                    if c >= 2:
                        for n in (TILES * (c - 1) - 1, TILES * (c - 1) - 2, TILES * (c - 1) - 3):
                            act.wait_ge(*hidden(r, n))
                    A(wbs[:, c % 2], PS[:, 4, 0:CW], ACT.Copy).then_inc(s_wbe.sem, 1)

                def silu(n):
                    act.wait_ge(s_g.sem, s_g.at(r, n + 1))
                    if n >= 2:
                        act.wait_ge(s_tg.sem, s_tg.at(r, n - 1))
                    A(sg[:, n % 2], PS[:, n % 2, 0:CW], ACT.Silu).then_inc(s_sg.sem, 1)

                silu(0)
                silu(1)
                weights_high(0, 0)
                weights_out(0)
                for n in range(2, N):
                    silu(n)
                    if n < 2 + 2 * CH:
                        tap0(r + 1, n - 2)
                    for q in range(CHUNKS):
                        if q and n == W0 + 3 * q - 2:
                            weights_high(0, q)
                        if n == XROW + 3 * q + 1:
                            inputs_high(1, q)
                        if n == WROW + 3 * q + 1:
                            weights_high(1, q)
                    if n % TILES == WB + 1 and n < N - TILES:
                        weights_out(n // TILES + 1)
                    for st, a, after in OUT:
                        if n == after + 1:
                            tokens_out(st, a)
                nc.scalar.preload_act_table_set("natural_log_exp_and_others")
                tokens_out(1, 1)

        @block.vector
        def _(dve):
            V = nc.vector
            chain = [0]

            def link(ins):
                chain[0] += 1
                ins.then_inc(s_dch, 1)
                dve.wait_ge(s_dch, chain[0])

            def tap(r, k):
                st, t, c = k // (3 * CH), 1 + k % (3 * CH) // CH, k % CH
                if t == 1:
                    dve.wait_ge(s_cv0.sem, s_cv0.at(r, c + 1, st))
                else:
                    dve.wait_ge(s_cv.sem, s_cv.at(r, CH * (t - 2) + c + 1, st))
                iv = img[st][:, :].rearrange("q (i a j b) -> q i a j b", i=4, a=2, b=2)
                yc = y[st][:, c, :].rearrange("q (i j) -> q i j", i=4)
                V.scalar_tensor_tensor(out=yc, in0=iv[:, :, t // 2, :, t % 2], scalar=cw[:, 4 * c + t:4 * c + t + 1],
                                       in1=yc, op0=ALU.mult, op1=ALU.add).then_inc(s_cv.sem, 1)

            dve.wait_ge(s_lin, 2)
            link(V.tensor_copy(ang[:, 0:1], tmp[:, 1:2]))
            link(V.tensor_scalar_add(ang[:, 1:2], ang[:, 0:1], PI / 2))
            link(V.tensor_scalar(ang[:, 2:4], ang[:, 0:2], 1 / (2 * PI), 12582912.0, ALU.mult, ALU.add))
            link(V.tensor_scalar_add(ang[:, 2:4], ang[:, 2:4], -12582912.0))
            hi = 6.28125
            link(V.scalar_tensor_tensor(out=ang[:, 4:6], in0=ang[:, 2:4], scalar=-hi, in1=ang[:, 0:2], op0=ALU.mult, op1=ALU.add))
            link(V.scalar_tensor_tensor(out=ang[:, 4:6], in0=ang[:, 2:4], scalar=-(2 * PI - hi), in1=ang[:, 4:6], op0=ALU.mult, op1=ALU.add))
            pi32 = 3.1415925
            V.tensor_scalar(ang[:, 4:6], ang[:, 4:6], pi32, -pi32, ALU.min, ALU.max).then_inc(s_ang, 1)
            for k in range(6 * CH):
                tap(0, k)
            dve.wait_ge(s_raw, 32)
            V.tensor_scalar(bq8[:, :], col[:, V_BQ:V_BQ + 1], D ** -0.5, None, ALU.mult).then_inc(s_dset, 1)
            dve.wait_ge(s_gam, 1)
            for k in range(2):
                V.tensor_scalar(raw[:, k, :], raw[:, k, :], gam[:, 0:1], None, ALU.mult).then_inc(s_gam, 1)
            for k in (R_WQ2, R_WK2, R_WV2):
                link(V.tensor_scalar(wt[:, k, :], wt[:, k, :], col[:, V_L1:V_L1 + 1], None, ALU.mult))
            link(V.tensor_scalar(wt[:, R_RT, :], wt[:, R_RT, :], col[:, V_L2:V_L2 + 1], None, ALU.mult))
            link(V.tensor_scalar(wt[:, R_CIM, :], wt[:, R_CIM, :], -1.0, None, ALU.mult))
            for k, dst in ((R_WQ2, q_rot), (R_WK2, k_rot)):
                a = wt[:, k, :].rearrange("q (h r j) -> q h r j", r=2, j=HD // 2)
                b = dst[:, :].rearrange("q (h r j) -> q h r j", r=2, j=HD // 2)
                V.tensor_scalar(b[:, :, 0], a[:, :, 1], -1.0, None, ALU.mult).then_inc(s_dset, 1)
                V.tensor_copy(b[:, :, 1], a[:, :, 0]).then_inc(s_dset, 1)
            dve.wait_ge(s_tr, 2)
            V.tensor_copy(wt[:, R_BRE:R_BIM + 1, :].rearrange("q a b -> q (a b)"), PS[:, 7, 0:256]).then_inc(s_dset, 1)
            V.tensor_copy(wvo[:, :], PS[:, 6, 0:128]).then_inc(s_dset, 1)
            V.tensor_scalar(bvo[:, :], PS[:, 6, 128:129], col[:, V_BO:V_BO + 1], None, ALU.add).then_inc(s_dset, 1)
            for k, (high, low) in enumerate(((w1h, w1l), (w3h, w3l))):
                dve.wait_ge(s_high, k + 1)
                V.scalar_tensor_tensor(out=low[:, :], in0=up[k], scalar=col[:, V_L2:V_L2 + 1], in1=high[:, :].bitcast(fp32),
                                       op0=ALU.mult, op1=ALU.subtract).then_inc(s_dset, 1)
            dve.wait_ge(s_pk, 2)

            with dve.Fori(0, ROUNDS) as r:
                for c in range(CH):
                    dve.wait_ge(s_ft.sem, s_ft.at(r, 1 + c // 2, 1))
                    V.tensor_copy(tokens(1, c), conv_rows(1, c)).then_inc(s_xd.sem, 1)
                for st in range(2):
                    dve.wait_ge(s_k.sem, s_k.at(r, 1, st))
                    for p in range(2):
                        q = slice(64 * p, 64 * p + 64)
                        V.tensor_scalar(kbd[st][q, :, p, :].rearrange("q (a i) s -> q a i s", a=2), psum_quads(st, 0)[q],
                                        col[q, V_BK:V_BK + 1], None, ALU.add).then_inc(s_ke.sem, 1)

                def attn1_max(w):
                    st, u = w % 2, w // 2
                    dve.wait_ge(s_s1.sem, s_s1.at(r, w + 1))
                    if w >= 4:
                        dve.wait_ge(s_e1.sem, s_e1.at(r, w - 3))
                    V.tensor_reduce(ex[st][0:HS, u % 2, 0, 0:2], PS[0:HS, 4 * st + u % 2, 0:2 * S].rearrange("q (p t) -> q p t", p=2),
                                    AX.X, ALU.max, negate=True).then_inc(s_m1.sem, 1)

                def attn1_weights(w):
                    st, u = w % 2, w // 2
                    e = ex[st][0:HS, u % 2]
                    v = pw[st][u % 2][0:HS, 0:2 * S].rearrange("q (p t) -> q p t", p=2)
                    dve.wait_ge(s_e1.sem, s_e1.at(r, w + 1))
                    V.reciprocal(e[:, 2, 0:2], e[:, 1, 0:2]).then_inc(s_i1.sem, 1)
                    dve.wait_ge(s_i1.sem, s_i1.at(r, w + 1))
                    V.tensor_tensor(v, v, e[:, 2, 0:2].unsqueeze(2).broadcast_to([HS, 2, S]), ALU.mult).then_inc(s_n1.sem, 1)

                def attn1_close(w):
                    st, i = w % 2, w // 4
                    dve.wait_ge(s_o1.sem, s_o1.at(r, w + 1))
                    V.tensor_scalar(h1[st][:, i * S:(i + 1) * S], PS[:, 4 * st + 3, 0:S], bvo[:, 0:1], None, ALU.add).then_inc(s_h1.sem, 1)

                attn1_max(0)
                attn1_max(1)
                for w in range(2 * U1 + 2):
                    if w < 2 * U1:
                        attn1_weights(w)
                    if w + 2 < 2 * U1:
                        attn1_max(w + 2)
                    if w >= 2 and (w - 2) // 2 % 2:
                        attn1_close(w - 2)

                def scale(n, dst):
                    s = norms[n]
                    for h in range(4):
                        dve.wait_ge(s["rs"].sem, s["rs"].half(r, 1, h))
                        V.tensor_tensor(piece(dst, h), bank(h, 0) if n < 2 else piece(h3, h), piece(rstd, h), ALU.mult).then_inc(s["nx"].sem, 1)

                scale(0, xn)
                dve.wait_ge(s_rot, 1)
                for h in range(4):
                    st, a = h // 2, h % 2
                    dve.wait_ge(s_b.sem, s_b.half(r, 1, h))
                    for k in range(2):
                        V.tensor_tensor(two_pairs(two_parts(t4[st], 2 * k, a)), two_pairs(two_banks(h)), two_tables(rot[:, k:k + 2, :]),
                                        ALU.mult).then_inc(s_rm.sem, 1)
                for h in range(4):
                    st, a = h // 2, h % 2
                    for k in range(2):
                        dve.wait_ge(s_ra.sem, s_ra.half(r, k + 1, h))
                        V.tensor_tensor_scan(part(z[st][:, k], a), part(decay, 0), part(zin[st][:, k], a), 0.0, ALU.mult,
                                             ALU.add).then_inc(s_sc.sem, 1)
                    dve.wait_ge(s_sc.sem, s_sc.half(r, 2, h))
                    for k in range(2):
                        V.tensor_tensor(two_pairs(two_parts(t4[st], 2 * k, a)), two_pairs(two_parts(z[st], 0, a)),
                                        two_tables(rot[:, k:k + 2, :]), ALU.mult).then_inc(s_rb.sem, 1)
                for h in range(4):
                    dve.wait_ge(s_y.sem, s_y.half(r, 1, h))
                    V.tensor_tensor(piece(h2, h), piece(h1, h), bank(h, 0), ALU.add).then_inc(s_h2.sem, 1)
                def normed(h):
                    for m, src, dst in ((2, rms, xr), (1, rstd, xl)):
                        dve.wait_ge(norms[m]["rs"].sem, norms[m]["rs"].half(r, 1, h))
                        V.tensor_tensor(piece(dst, h), bank(h, 0), piece(src, h), ALU.mult).then_inc(norms[m]["nx"].sem, 1)

                def rotate(n, h):
                    s = (s_q2, s_k2)[n]
                    dve.wait_ge(s.sem, s.half(r, 1, h))
                    V.tensor_tensor(two_pairs(two_parts(t4[h // 2], 2 * n, h % 2)), two_pairs(two_banks(h)), two_tables(rope),
                                    ALU.mult).then_inc(s_rp[n].sem, 1)

                normed(0)
                for n, h in TURNS:
                    if n == 0 and h < 3:
                        normed(h + 1)
                    rotate(n, h)

                for hf in range(2):
                    for st in range(2):
                        dve.wait_ge(s_rq[1].sem, s_rq[1].at(r, 2, st))
                        for h in range(NH * hf + 1, NH * hf + NH):
                            V.tensor_scalar(first(km[st][:, h]), first(k2[st][:, :]), cst[:, C_HM + h:C_HM + h + 1], None,
                                            ALU.mult).then_inc(s_kd.sem, 1)

                def attn2_max(w):
                    st, u = w % 2, w // 2
                    b, e = PS[:, 4 * st + u % 2], ex[st][:, u % 2]
                    dve.wait_ge(s_s2.sem, s_s2.at(r, w + 1))
                    if w >= 4:
                        dve.wait_ge(s_e2.sem, s_e2.at(r, w - 3))
                    if u % KINDS < 2:
                        V.tensor_reduce(e[:, 0, :], b.rearrange("q (h t) -> q h t", h=NH), AX.X, ALU.max, negate=True).then_inc(s_m2.sem, 1)
                    else:
                        V.tensor_reduce(e[:, 0, 0:1], b[:, 0:S], AX.X, ALU.max, negate=True).then_inc(s_m2.sem, 1)

                def attn2_weights(w):
                    st, u = w % 2, w // 2
                    p, e = pw[st][u % 2], ex[st][:, u % 2]
                    n = NH if u % KINDS < 2 else 1
                    dve.wait_ge(s_e2.sem, s_e2.at(r, w + 1))
                    V.reciprocal(e[:, 2, 0:n], e[:, 1, 0:n]).then_inc(s_i2.sem, 1)
                    dve.wait_ge(s_i2.sem, s_i2.at(r, w + 1))
                    if n > 1:
                        v = p.rearrange("q (h t) -> q h t", h=NH)
                        V.tensor_tensor(v, v, e[:, 2, :].unsqueeze(2).broadcast_to([128, NH, QA]), ALU.mult).then_inc(s_n2.sem, 1)
                    else:
                        V.tensor_scalar(p[:, 0:S], p[:, 0:S], e[:, 2, 0:1], None, ALU.mult).then_inc(s_n2.sem, 1)

                def attn2_values(w):
                    st, i = w % 2, w // 2 // KINDS
                    n = 2 * i + st
                    dve.wait_ge(s_o2.sem, s_o2.at(r, w + 1))
                    if i >= 1:
                        dve.wait_ge(s_at.sem, s_at.at(r, n - 1))
                    V.tensor_copy(on[st], PS[:, 4 * st + 3, 0:2 * S]).then_inc(s_on.sem, 1)

                def residual(w):
                    st, i = w % 2, w // 2 // KINDS
                    dve.wait_ge(s_at.sem, s_at.at(r, 2 * i + st + 1))
                    t = slice(i * S, (i + 1) * S)
                    V.tensor_tensor(h3[st][:, t], xl[st][:, t], PS[:, 4 * st + 3, 2 * S:3 * S], ALU.add).then_inc(s_h3.sem, 1)

                attn2_max(0)
                attn2_max(1)
                for w in range(2 * U2 + 3):
                    if w < 2 * U2:
                        attn2_weights(w)
                    if w + 2 < 2 * U2:
                        attn2_max(w + 2)
                    if last_kind(w - 3):
                        residual(w - 3)
                    if last_kind(w - 2):
                        attn2_values(w - 2)
                scale(3, flat)

                full = [TC, NT, NE]
                pri = cst[0:TC, C_PRI:C_PRI + NE].unsqueeze(1).broadcast_to(full)

                def route(st, j):
                    def wide(k):
                        return rm[st][:, k, :].unsqueeze(2).broadcast_to(full)

                    def before(st, j):
                        if j <= 2:
                            return r * 2 * TOPK + 2 * st + j
                        return r * 2 * TOPK + st * (TOPK - 2) + j + 2

                    l, e, k, m = rl[st][:, :, :], re[st][:, :, :], rk[st][:, :, :], rm[st]
                    first_, second, rest = rs1[st][:, :, :], rs2[st][:, :, :], rt[st][:, :, :]
                    logits = PS[0:TC, 4 * st, 0:NT * NE].rearrange("q (n e) -> q n e", e=NE)
                    if j == 0:
                        dve.wait_ge(s_rt.sem, s_rt.at(r, 1, st))
                    else:
                        dve.wait_ge(s_tk.sem, before(st, j))
                    if j == 0:
                        ins = V.tensor_reduce(m[:, 0, :], logits, AX.X, ALU.max)
                    elif j == 1:
                        ins = V.tensor_tensor(l, logits, wide(0), ALU.subtract)
                    elif j == 2:
                        ins = V.scalar_tensor_tensor(out=k, in0=l, scalar=0.0, in1=pri, op0=ALU.is_ge, op1=ALU.mult)
                    elif j == 3:
                        ins = V.tensor_reduce(m[:, 1, :], k, AX.X, ALU.max)
                    elif j == 4:
                        ins = V.tensor_tensor(first_, k, wide(1), ALU.is_equal)
                    elif j == 5:
                        ins = V.scalar_tensor_tensor(out=rest, in0=first_, scalar=-1e30, in1=l, op0=ALU.mult, op1=ALU.add)
                    elif j == 6:
                        ins = V.tensor_reduce(m[:, 2, :], rest, AX.X, ALU.max)
                    elif j == 7:
                        ins = V.tensor_tensor(k, rest, wide(2), ALU.is_equal)
                    elif j == 8:
                        ins = V.tensor_tensor(k, k, pri, ALU.mult)
                    elif j == 9:
                        ins = V.tensor_reduce(m[:, 3, :], k, AX.X, ALU.max)
                    elif j == 10:
                        ins = V.tensor_tensor(second, k, wide(3), ALU.is_equal)
                    elif j == 11:
                        ins = V.tensor_tensor(first_, first_, second, ALU.add)
                    elif j == 12:
                        dve.wait_ge(s_re.sem, s_re.at(r, 1, st))
                        ins = V.tensor_tensor(rest, e, first_, ALU.mult)
                    elif j == 13:
                        ins = V.tensor_reduce(m[:, 4, :], e, AX.X, ALU.add)
                    elif j == 14:
                        ins = V.tensor_reduce(m[:, 5, :], rest, AX.X, ALU.add)
                    elif j == 15:
                        ins = V.scalar_tensor_tensor(out=m[:, 5, :], in0=m[:, 4, :], scalar=1e-9, in1=m[:, 5, :], op0=ALU.mult, op1=ALU.add)
                    elif j == 16:
                        ins = V.reciprocal(m[:, 5, :], m[:, 5, :])
                    if j < TOPK:
                        ins.then_inc(s_tk.sem, 1)
                    else:
                        for o in (0, 32):
                            V.tensor_tensor(wtok[st][:, :, o:o + NE], rest, wide(5), ALU.mult).then_inc(s_wk.sem, 1)

                for st in range(2):
                    route(st, 0)
                    route(st, 1)

                def inputs_low(st, q):
                    dve.wait_ge(s_xh.sem, s_xh.at(r, q + 1, st))
                    low = xs[st][64:128, q * CW:(q + 1) * CW]
                    V.tensor_tensor(low, PS[64:128, 5 if st else 5 + q, 0:CW], low.bitcast(fp32), ALU.subtract).then_inc(s_xl.sem, 1)

                def weights_low(st, q):
                    dve.wait_ge(s_wh.sem, s_wh.at(r, q + 1, st))
                    low = wrow[st][32:40, q * CW:(q + 1) * CW]
                    V.tensor_tensor(low, PS[32:40, rows_bank(st, q), 0:CW], low.bitcast(fp32), ALU.subtract).then_inc(s_wl.sem, 1)

                def finish(c):
                    st, q = c // CHUNKS, c % CHUNKS
                    t = slice(q * QW, (q + 1) * QW)
                    dve.wait_ge(s_yo.sem, s_yo.at(r, TILES * (c + 1)))
                    if c == 0:
                        dve.wait_ge(s_h23.sem, s_h23.at(r, 2))
                    V.tensor_tensor(h2[st][:, t], h2[st][:, t], PS[:, 6 + c % 2, 0:QW], ALU.add).then_inc(s_h4.sem, 1)

                def gate(n):
                    dve.wait_ge(s_sg.sem, s_sg.at(r, n + 1))
                    dve.wait_ge(s_u.sem, s_u.at(r, n + 1))
                    if n >= 3:
                        dve.wait_ge(*hidden(r, n - 3))
                    V.tensor_tensor(tg[:, n % 3], sg[:, n % 2], PS[:, 2 + n % 2, 0:CW], ALU.mult).then_inc(s_tg.sem, 1)

                def weigh(n):
                    c = n // TILES
                    dve.wait_ge(s_tg.sem, s_tg.at(r, n + 1))
                    dve.wait_ge(s_wbe.sem, s_wbe.at(r, c + 1))
                    if n >= HH:
                        dve.wait_ge(s_yo.sem, s_yo.at(r, n - HH + 1))
                    V.tensor_tensor(hh[:, n % HH], tg[:, n % 3], wbs[:, c % 2], ALU.mult).then_inc(s_hd.sem, 1)

                for j in range(2, TOPK + 1):
                    route(0, j)
                    for q in range(CHUNKS):
                        if j == 7 + 3 * q:
                            inputs_low(0, q)
                gate(0)
                gate(1)
                weights_low(0, 0)
                for n in range(N):
                    if n >= 2:
                        gate(n)
                    if not on_pool(n):
                        weigh(n)
                    if n % TILES == 4 and n > TILES:
                        finish(n // TILES - 1)
                    if n < TOPK - 1:
                        route(1, 2 + n)
                    for q in range(CHUNKS):
                        if q and n == W0 + 3 * q - 2:
                            weights_low(0, q)
                        if n == XROW + 3 * q + 1:
                            inputs_low(1, q)
                        if n == WROW + 3 * q + 1:
                            weights_low(1, q)
                    if n >= N - 9 * CH and n % 3 != 0:
                        tap(r + 1, (n - N + 9 * CH) // 3 * 2 + n % 3 - 1)
                finish(2 * CHUNKS - 1)

        @block.tensor
        def _(pe):
            mm = nc.tensor.matmul
            pe.wait_ge(s_cst, 32)
            pe.wait_ge(s_raw, 32)
            mm(PS[:, 6, 0:128], raw[:, 2, :], wt[:, R_WO, :], start=True, stop=True)
            mm(PS[:, 6, 128:129], wt[:, R_WO, :], col[:, V_BV:V_BV + 1], start=True, stop=True).then_inc(s_tr, 1)
            pe.wait_ge(s_gam, 3)
            for k in range(2):
                last = nc.tensor.transpose(PS[:, 7, k * 128:(k + 1) * 128], raw[:, k, :], ident)
            last.then_inc(s_tr, 1)
            pe.wait_ge(s_dset, 8)
            pe.wait_ge(s_aset, 3)
            pe.wait_ge(s_pset, 7)
            pe.wait_ge(s_pk, 2)
            pe.wait_ge(s_down, 16)

            def product(st, k, w, src, sem):
                for a in range(2):
                    last = mm(PS[:, 4 * st + k + a, 0:HW], w, part(src, a), start=True, stop=True)
                if sem is not None:
                    last.then_inc(sem.sem, 1)

            with pe.Fori(0, ROUNDS) as r:
                for st in range(2):
                    pe.wait_ge(s_cv.sem, s_cv.at(r, 12, st))
                    for c in range(CH):
                        for k in range(3):
                            for p in range(2):
                                o = (c % 2) * 144 + k * 48
                                last = mm(PS[64 * p:64 * p + 64, 4 * st + c // 2, o:o + 48], y[st][:, c, 64 * k:64 * k + 64],
                                          ident[0:TC, 48 * p:48 * p + 48], start=True, stop=True)
                        if c % 2:
                            last.then_inc(s_ft.sem, 1)
                for st in range(2):
                    x_ = s_xd if st else s_xe
                    pe.wait_ge(x_.sem, x_.at(r, CH))
                    product(st, 2, wt[:, R_WQ, :], xf[st], s_q)
                    product(st, 0, wt[:, R_WK, :], xf[st], s_k)
                for st in range(2):
                    pe.wait_ge(s_qe.sem, s_qe.at(r, 1, st))
                    for n in range(2 * PAIRS):
                        last = mm(PS[0:HS, 4 * st + 2 + n // 4, (n % 4) * 128:(n % 4 + 1) * 128], xf[st][:, n * HS:(n + 1) * HS],
                                  wvo[:, :], start=True, stop=True)
                    last.then_inc(s_v.sem, 1)

                def score1(w):
                    st, u = w % 2, w // 2
                    if u == 0:
                        pe.wait_ge(s_ke.sem, s_ke.at(r, 2, st))
                    if u >= 2:
                        pe.wait_ge(s_e1.sem, s_e1.at(r, w - 3))
                    mm(PS[0:HS, 4 * st + u % 2, 0:2 * S], qf[st][:, u * HS:(u + 1) * HS],
                       kbd[st][:, u // 2].rearrange("q p t -> q (p t)"), start=True, stop=True).then_inc(s_s1.sem, 1)

                def turn1(w):
                    st, u = w % 2, w // 2
                    if u == 0:
                        pe.wait_ge(s_ve.sem, s_ve.at(r, 1, st))
                    pe.wait_ge(s_n1.sem, s_n1.at(r, w + 1))
                    if w >= 2:
                        pe.wait_ge(s_pt1.sem, s_pt1.at(r, w - 1))
                    for k in range(4):
                        last = nc.tensor.transpose(PS[0:HS, 4 * st + 2, k * HS:(k + 1) * HS],
                                                   pw[st][u % 2][0:HS, k * HS:(k + 1) * HS], ident[0:HS, 0:HS])
                    last.then_inc(s_t1.sem, 1)

                def value1(w):
                    st, u = w % 2, w // 2
                    i, j = u // 2, u % 2
                    pe.wait_ge(s_pt1.sem, s_pt1.at(r, w + 1))
                    if j == 0 and i >= 1:
                        pe.wait_ge(s_h1.sem, s_h1.at(r, 2 * (i - 1) + st + 1))
                    for th in range(2):
                        for p in range(2):
                            k = 2 * p + th
                            last = mm(PS[64 * p:64 * p + 64, 4 * st + 3, j * HS:(j + 1) * HS], vt[st][0:HS, 2 * i + th, 64 * p:64 * p + 64],
                                      pt[st][0:HS, k * HS:(k + 1) * HS], start=(th == 0), stop=(th == 1))
                    last.then_inc(s_o1.sem, 1)

                for w in range(4):
                    score1(w)
                for w in range(2 * U1 + 1):
                    if w < 2 * U1:
                        turn1(w)
                    if w + 4 < 2 * U1:
                        score1(w + 4)
                    if w >= 1:
                        value1(w - 1)

                def centred(n, src):
                    for h in range(4):
                        if n == 0:
                            pe.wait_ge(s_h1.sem, pair_ready(r, h))
                        else:
                            pe.wait_ge(s_h2.sem, s_h2.half(r, 1, h))
                        mm(bank(h, 0), centre, piece(src, h), start=True, stop=True).then_inc(norms[n]["cen"].sem, 1)

                def var(n):
                    s = norms[n]
                    for h in range(4):
                        pe.wait_ge(s["sq"].sem, s["sq"].half(r, 1, h))
                        mm(bank(h, 1), avg, piece(sq, h), start=True, stop=True).then_inc(s["var"].sem, 1)

                centred(0, h1)
                var(0)
                for h in range(4):
                    pe.wait_ge(norms[0]["nx"].sem, norms[0]["nx"].half(r, 1, h))
                    mm(bank(h, 0), wt[:, R_BRE, :], piece(xn, h), start=True, stop=True)
                    mm(bank(h, 1), wt[:, R_BIM, :], piece(xn, h), start=True, stop=True).then_inc(s_b.sem, 1)
                for h in range(4):
                    st, a = h // 2, h % 2
                    pe.wait_ge(s_rc.sem, s_rc.half(r, 2, h))
                    mm(bank(h, 0), wt[:, R_CRE, :], part(ab[st][:, 0], a), start=True, stop=False)
                    mm(bank(h, 0), wt[:, R_CIM, :], part(ab[st][:, 1], a), start=False, stop=True).then_inc(s_y.sem, 1)
                centred(1, h2)
                var(1)
                def values_in2(st):
                    pe.wait_ge(s_rp[1].sem, s_rp[1].half(r, 1, 2 * st))
                    pe.wait_ge(norms[2]["nx"].sem, norms[2]["nx"].at(r, 2, st))
                    for n, (t0, t1) in enumerate(((0, QA), (QA, S))):
                        for i in range(PAIRS):
                            last = mm(PS[0:t1 - t0, 4 * st + n, i * 128:(i + 1) * 128], xr[st][:, i * S + t0:i * S + t1],
                                      wt[:, R_WV2, :], start=True, stop=True)
                    last.then_inc(s_v2.sem, 1)

                for n, h in TURNS:
                    if n == 0:
                        pe.wait_ge(norms[2]["nx"].sem, norms[2]["nx"].half(r, 1, h))
                        pe.wait_ge(norms[1]["nx"].sem, norms[1]["nx"].half(r, 1, h))
                        mm(bank(h, 0), wt[:, R_WQ2, :], piece(xr, h), start=True, stop=True)
                        mm(bank(h, 1), q_rot[:, :], piece(xr, h), start=True, stop=True).then_inc(s_q2.sem, 1)
                    else:
                        pe.wait_ge(s_rp[0].sem, s_rp[0].half(r, 1, h))
                        mm(bank(h, 0), wt[:, R_WK2, :], piece(xr, h), start=True, stop=True)
                        mm(bank(h, 1), k_rot[:, :], piece(xr, h), start=True, stop=True).then_inc(s_k2.sem, 1)
                    if (n, h) == (1, 2):
                        values_in2(0)
                values_in2(1)

                def score2(w):
                    st, u = w % 2, w // 2
                    i, kind = u // KINDS, u % KINDS
                    b = PS[:, 4 * st + u % 2]
                    if u == 0:
                        pe.wait_ge(s_v2e.sem, s_v2e.at(r, 1, st))
                    if u < 2:
                        pe.wait_ge(s_km.sem, s_km.at(r, 2 * u + st + 1))
                        pe.wait_ge(s_kd.sem, s_kd.at(r, 3 * (2 * u + st + 1)))
                    if u >= 2:
                        pe.wait_ge(s_e2.sem, s_e2.at(r, w - 3))
                    if u == 2:
                        pe.wait_ge(s_qt.sem, s_qt.at(r, 1, st))
                    if kind < 2:
                        mm(b, q2[st][:, i * S:i * S + QA], km[st][:, NH * kind:NH * (kind + 1), i * S:i * S + QA], start=True, stop=False)
                        mm(b, ident_b[:, :], neg_b[:, 0:QA].unsqueeze(1).broadcast_to([128, NH, QA]), start=False,
                           stop=True).then_inc(s_s2.sem, 1)
                    else:
                        mm(b[:, 0:S], qt[st][:, i * QA:(i + 1) * QA], k2[st][:, i * S:(i + 1) * S], start=True, stop=False)
                        mm(b[:, QA:S], ident_b[:, :], neg_b[:, QA:S], start=False, stop=True).then_inc(s_s2.sem, 1)

                def turn2(w):
                    st, u = w % 2, w // 2
                    b, p = PS[:, 4 * st + 2], pw[st][u % 2]
                    pe.wait_ge(s_n2.sem, s_n2.at(r, w + 1))
                    if w >= 2:
                        pe.wait_ge(s_pt2.sem, s_pt2.at(r, w - 1))
                    if u % KINDS < 2:
                        for h in range(NH):
                            last = nc.tensor.transpose(b[:, h * QA:(h + 1) * QA], p[:, h * QA:(h + 1) * QA], ident)
                    else:
                        nc.tensor.transpose(b[:, 0:QA], p[:, 0:QA], ident)
                        last = nc.tensor.transpose(b[0:QB, QA:2 * QA], p[:, QA:S], ident)
                    last.then_inc(s_t2.sem, 1)

                def value2(w):
                    st, u = w % 2, w // 2
                    i, kind = u // KINDS, u % KINDS
                    b = PS[:, 4 * st + 3, 0:2 * S].rearrange("q (r s) -> q r s", r=2)
                    pe.wait_ge(s_pt2.sem, s_pt2.at(r, w + 1))
                    if kind == 0 and i >= 1:
                        pe.wait_ge(s_h3.sem, s_h3.at(r, 2 * (i - 1) + st + 1))
                    for p in range(2):
                        for kv in range(NKV):
                            e = slice(64 * p + HP * kv, 64 * p + HP * kv + HP)
                            if kind == p:
                                last = mm(b[e, :, 0:QA], vt[st][:, i, e], pt[st][:, 2 * QA * kv:2 * QA * (kv + 1)], start=True, stop=True)
                            elif kind == 2:
                                o = 2 * QB * (2 * p + kv)
                                mm(b[e, :, QA:S], vt[st][:, i, e], pt[st][:, o:o + 2 * QB], start=True, stop=False)
                                last = mm(b[e, :, QA:S], vt[st][0:QB, PAIRS + i, e], pt[st][0:QB, QA + o:QA + o + 2 * QB],
                                          start=False, stop=True)
                    last.then_inc(s_o2.sem, 1)

                def project2(w):
                    st, i = w % 2, w // 2 // KINDS
                    pe.wait_ge(s_on.sem, s_on.at(r, 2 * i + st + 1))
                    for j, k in enumerate((R_WO2, R_WO3)):
                        last = mm(PS[:, 4 * st + 3, 2 * S:3 * S], wt[:, k, :], on[st][:, j * S:(j + 1) * S], start=(j == 0),
                                  stop=(j == 1))
                    last.then_inc(s_at.sem, 1)

                for w in range(4):
                    score2(w)
                for w in range(2 * U2 + 2):
                    if w < 2 * U2:
                        turn2(w)
                    if w + 4 < 2 * U2:
                        score2(w + 4)
                    if 1 <= w <= 2 * U2:
                        value2(w - 1)
                    if last_kind(w - 2):
                        project2(w - 2)
                var(3)
                for st in range(2):
                    pe.wait_ge(norms[3]["nx"].sem, norms[3]["nx"].at(r, 2, st))
                    for c in range(NTC):
                        last = mm(PS[0:TC, 4 * st, c * 2 * NE:(c + 1) * 2 * NE], flat[st][:, c * TC:(c + 1) * TC],
                                  wt[:, R_RT, 0:2 * NE], start=True, stop=True)
                    last.then_inc(s_rt.sem, 1)

                def doubled(st, q):
                    if st:
                        if q == 0:
                            pe.wait_ge(s_wl.sem, s_wl.at(r, CHUNKS))
                        else:
                            pe.wait_ge(s_xl.sem, s_xl.at(r, q, st))
                    for p in range(2):
                        last = mm(PS[:, 5 if st else 5 + q, p * QW:(p + 1) * QW], cst[:, C_DUP + 128 * p:C_DUP + 128 * p + 128],
                                  flat[st][:, q * QW:(q + 1) * QW], start=True, stop=True)
                    last.then_inc(s_dup.sem, 1)

                def weights_rows(st, q):
                    pe.wait_ge(s_wk.sem, s_wk.at(r, 2, st))
                    if q > 1 or (st and q):
                        pe.wait_ge(s_wl.sem, s_wl.at(r, q, st))
                    elif st:
                        pe.wait_ge(s_xl.sem, s_xl.at(r, CHUNKS, st))
                    else:
                        pe.wait_ge(s_xl.sem, s_xl.at(r, 1))
                    for p in range(2):
                        for c in range(2):
                            o = p * QW + c * TC
                            last = nc.tensor.transpose(PS[0:72, rows_bank(st, q), o:o + TC], wtok[st][:, (2 * q + c) * 2 + p, :],
                                                       ident[0:TC, 0:TC])
                    last.then_inc(s_wt.sem, 1)

                def broadcast(c):
                    st, q = c // CHUNKS, c % CHUNKS
                    pe.wait_ge(s_wl.sem, s_wl.at(r, q + 1, st))
                    if c:
                        pe.wait_ge(s_wbe.sem, s_wbe.at(r, c))
                    mm(PS[:, 4, 0:CW], sel[:, :], wrow[st][:, q * CW:(q + 1) * CW], start=True, stop=True).then_inc(s_wb.sem, 1)

                def turn_out(st, a):
                    if st + a:
                        pe.wait_ge(s_oe.sem, s_oe.at(r, a, st))
                    else:
                        pe.wait_ge(s_wl.sem, s_wl.at(r, CHUNKS, 1))
                    for c in range(3 * a, 3 * a + 3):
                        pe.wait_ge(s_h4.sem, s_h4.at(r, CHUNKS * st + c // 2 + 1))
                        last = nc.tensor.transpose(PS[0:TC, 5, (c % 3) * 128:(c % 3 + 1) * 128], h2[st][:, c * TC:(c + 1) * TC], ident)
                    last.then_inc(s_ot.sem, 1)

                def first_products(n):
                    c, k = n // TILES, n % TILES
                    st, q = c // CHUNKS, c % CHUNKS
                    e, t = slice(128 * k, 128 * k + 128), slice(q * CW, (q + 1) * CW)
                    g, u = PS[:, n % 2, 0:CW], PS[:, 2 + n % 2, 0:CW]
                    if k == 0:
                        pe.wait_ge(s_xl.sem, s_xl.at(r, q + 1, st))
                    if n >= 2:
                        pe.wait_ge(s_sg.sem, s_sg.at(r, n - 1))
                    mm(g, w1h[:, e], xs[st][:, t], start=True, stop=False)
                    mm(g, w1l[:, e], xs[st][:, t], start=False, stop=True).then_inc(s_g.sem, 1)
                    if n >= 2:
                        pe.wait_ge(s_tg.sem, s_tg.at(r, n - 1))
                    mm(u, w3h[:, e], xs[st][:, t], start=True, stop=False)
                    mm(u, w3l[:, e], xs[st][:, t], start=False, stop=True).then_inc(s_u.sem, 1)

                def second_products(n):
                    c, k = n // TILES, n % TILES
                    pe.wait_ge(*hidden(r, n))
                    if k == 0 and c >= 2:
                        pe.wait_ge(s_h4.sem, s_h4.at(r, c - 1))
                    for p in range(2):
                        last = mm(PS[64 * p:64 * p + 64, 6 + c % 2, 0:QW], w2t[:, k, :], hh[:, n % HH, p * QW:(p + 1) * QW],
                                  start=(k == 0), stop=(k == TILES - 1))
                    last.then_inc(s_yo.sem, 1)

                for q in range(CHUNKS):
                    doubled(0, q)
                pe.wait_ge(s_tk.sem, r * 2 * TOPK + 4)
                pe.wait_ge(s_dset, 10)
                first_products(0)
                first_products(1)
                weights_rows(0, 0)
                broadcast(0)
                for n in range(2, N + LAG):
                    if n < N:
                        first_products(n)
                    if n >= LAG:
                        second_products(n - LAG)
                    for q in range(CHUNKS):
                        if q and n == W0 + 3 * q - 3:
                            weights_rows(0, q)
                        if n == XROW + 3 * q:
                            doubled(1, q)
                        if n == WROW + 3 * q:
                            weights_rows(1, q)
                    if n % TILES == WB and n < N - TILES:
                        broadcast(n // TILES + 1)
                    for st, a, after in OUT[:3]:
                        if n == after:
                            turn_out(st, a)
                turn_out(1, 1)
                pe.wait_ge(s_oe.sem, s_oe.at(r, 4))


_INS = ["x", "L0_tok_conv_w", "L0_tok_conv_b", "L0_tok_wq", "L0_tok_bq", "L0_tok_wk", "L0_tok_bk", "L0_tok_wv", "L0_tok_bv",
        "L0_tok_wo", "L0_tok_bo", "L0_attn_nu_log", "L0_attn_theta_log", "L0_attn_gamma_log", "L0_attn_B_re", "L0_attn_B_im",
        "L0_attn_C_re", "L0_attn_C_im", "L0_ffn_ln1_w", "L0_ffn_ln2_w", "L0_ffn_wq", "L0_ffn_wk", "L0_ffn_wv", "L0_ffn_wo",
        "L0_ffn_router_w", "L0_ffn_w1", "L0_ffn_w2", "L0_ffn_w3"]


def kernel(**inputs):
    import numpy as _np
    import concourse.bacc as _bacc
    from concourse import mybir as _mybir
    from concourse.bass_utils import run_bass_kernel_spmd as _run

    nc = _bacc.Bacc("TRN2", target_bir_lowering=False, num_devices=1)
    arrays, args = {}, []
    c, s = constants()
    names = ("small", "vectors", "up1", "up3", "down")
    packed = zip(names, lay_out({n: _np.asarray(inputs[n]) for n in _INS}))
    for name, a in [("x", inputs["x"]), *packed, ("consts", c), ("experts", s)]:
        a = _np.ascontiguousarray(a)
        arrays[f"in_{name}_dram"] = a
        args.append(nc.dram_tensor(f"in_{name}_dram", a.shape, _mybir.dt.from_np(a.dtype), kind="ExternalInput").ap())
    args.append(nc.dram_tensor("out_0_dram", (IMAGES, S, D), _mybir.dt.float32, kind="ExternalOutput").ap())
    vit_tower(nc, *args)
    r = _run(nc, [arrays], core_ids=[0])
    return r.results[0]["out_0_dram"]
```
